# Optimizing a Trainium2 kernel written in Bass

```python
import numpy as np
import jax
import jax.numpy as jnp

def _softmax(x, axis=-1):
    return jax.nn.softmax(x, axis=axis)

def _gelu(x):
    return jax.nn.gelu(x, approximate=True)

def _silu(x):
    return jax.nn.silu(x)

def _sigmoid(x):
    return jax.nn.sigmoid(x)

def _layernorm(x, axis=-1, eps=1e-05):
    m = jnp.mean(x, axis=axis, keepdims=True)
    v = jnp.var(x, axis=axis, keepdims=True)
    return (x - m) / jnp.sqrt(v + eps)

def _scatter_add(tgt, idx, src, axis=0):
    return tgt.at[idx].add(src)

def _segment_sum(src, seg, n):
    return jax.ops.segment_sum(src, seg, n)
kernel_name = 'mk_xattn_seq_d4_seqx_r4_d1283c'

def setup_inputs(seed: int=0):
    np.random.seed(seed)
    _w = jnp.asarray

    def _rec_inputs():
        import jax
        import jax.numpy as jnp
        _rk = jax.random.key(seed)
        x = -0.0001661 + 0.9999 * jax.random.normal(jax.random.fold_in(_rk, 1), (4, 512, 256), jnp.float32)
        _lenS = 512 - jax.random.randint(jax.random.fold_in(_rk, 7), (4,), 0, max(1, 512 // 4) + 1, jnp.int32)
        _lenS2 = 64 - jax.random.randint(jax.random.fold_in(_rk, 8), (4,), 0, max(1, 64 // 4) + 1, jnp.int32)
        _ctx_768P = jax.random.normal(jax.random.fold_in(_rk, 11), (4, 16, 192), jnp.float32)
        _ctx_768c = jax.random.dirichlet(jax.random.fold_in(_rk, 511), 0.3 * jnp.ones((16,), jnp.float32), (4, 64))
        _ctx_768t = jnp.einsum('bsk,bkd->bsd', _ctx_768c, _ctx_768P)
        _ctx_768t = _ctx_768t * jax.lax.rsqrt(jnp.mean(jnp.square(_ctx_768t)) + 1e-12) * 0.953939
        ctx_768 = 8.47981e-05 + 1.00068 * (_ctx_768t + 0.3 * jax.random.normal(jax.random.fold_in(_rk, 611), (4, 64, 192), jnp.float32))
        return (x, ctx_768)
    x, ctx_768 = _rec_inputs()

    def _L0_xattn_setup():
        import jax, jax.numpy as jnp
        import numpy as np
        LATENT = 256
        TEXT = 192
        HEADS = 16
        HEAD_DIM = LATENT // HEADS
        SCALE = HEAD_DIM ** (-0.5)
        LN_EPS = 1e-05
        key = jax.random.key(seed)
        ks = jax.random.split(key, 16)
        B, Tx, Txf = (4, 1024, 64)

        def lin(k, fan_in, fan_out):
            bound = 1.0 / np.sqrt(fan_in)
            kw, kb = jax.random.split(k)
            W = jax.random.uniform(kw, (fan_in, fan_out), jnp.float32, -bound, bound)
            b = jax.random.uniform(kb, (fan_out,), jnp.float32, -bound, bound)
            return (W, b)
        Wq, bq = lin(ks[0], LATENT, LATENT)
        Wk, bk = lin(ks[1], TEXT, LATENT)
        Wv, bv = lin(ks[2], TEXT, LATENT)
        Wo, bo = lin(ks[3], LATENT, LATENT)
        W1, b1 = lin(ks[4], LATENT, 4 * LATENT)
        W2, b2 = lin(ks[5], 4 * LATENT, LATENT)
        return {'x': jax.random.normal(ks[6], (B, Tx, LATENT), jnp.float32), 'xf': jax.random.normal(ks[7], (B, Txf, TEXT), jnp.float32), 'Wq': Wq, 'bq': bq, 'Wk': Wk, 'bk': bk, 'Wv': Wv, 'bv': bv, 'Wo': Wo, 'bo': bo, 'ln_g': jnp.ones((LATENT,), jnp.float32), 'ln_b': jnp.zeros((LATENT,), jnp.float32), 'W1': W1, 'b1': b1, 'W2': W2, 'b2': b2}
    _L0_xattn_all = _L0_xattn_setup()
    _L0_xattn_in = {k: v for k, v in _L0_xattn_all.items() if k in ('Wq', 'bq', 'Wk', 'bk', 'Wv', 'bv', 'Wo', 'bo', 'ln_g', 'ln_b', 'W1', 'b1', 'W2', 'b2')}
    del _L0_xattn_all

    def _L1_xattn_setup():
        import jax, jax.numpy as jnp
        import numpy as np
        HEADS = 16
        D_HEAD = 64
        EPS = 1e-05

        def _ln(x, g, b):
            m = jnp.mean(x, axis=-1, keepdims=True)
            v = jnp.var(x, axis=-1, keepdims=True)
            return (x - m) * jax.lax.rsqrt(v + EPS) * g + b

        def _attn(xq, xc, Wq, Wk, Wv, Wo, bo):
            B, N, _ = xq.shape
            S = xc.shape[1]
            q = (xq @ Wq).reshape(B, N, HEADS, D_HEAD)
            k = (xc @ Wk).reshape(B, S, HEADS, D_HEAD)
            v = (xc @ Wv).reshape(B, S, HEADS, D_HEAD)
            scale = D_HEAD ** (-0.5)
            scores = jnp.einsum('bnhd,bshd->bhns', q, k) * scale
            attn = jax.nn.softmax(scores, axis=-1)
            out = jnp.einsum('bhns,bshd->bnhd', attn, v).reshape(B, N, HEADS * D_HEAD)
            return out @ Wo + bo

        def _geglu_ff(x, Wp, bp, Wf, bf):
            h = x @ Wp + bp
            a, gate = jnp.split(h, 2, axis=-1)
            return a * jax.nn.gelu(gate, approximate=False) @ Wf + bf
        key = jax.random.key(seed)
        ks = jax.random.split(key, 16)
        dim, ctx, inner, ffin = (256, 192, HEADS * D_HEAD, 4 * 256)

        def w(k, i, o):
            return jax.random.normal(k, (i, o), jnp.float32) * i ** (-0.5)
        inp = {'x': jax.random.normal(ks[0], (4, 512, dim), jnp.float32), 'context': jax.random.normal(ks[1], (4, 77, ctx), jnp.float32), 'Wq1': w(ks[2], dim, inner), 'Wk1': w(ks[3], dim, inner), 'Wv1': w(ks[4], dim, inner), 'Wo1': w(ks[5], inner, dim), 'bo1': jnp.zeros((dim,), jnp.float32), 'Wq2': w(ks[6], dim, inner), 'Wk2': w(ks[7], ctx, inner), 'Wv2': w(ks[8], ctx, inner), 'Wo2': w(ks[9], inner, dim), 'bo2': jnp.zeros((dim,), jnp.float32), 'Wp': w(ks[10], dim, 2 * ffin), 'bp': jnp.zeros((2 * ffin,), jnp.float32), 'Wf': w(ks[11], ffin, dim), 'bf': jnp.zeros((dim,), jnp.float32), 'g1': jnp.ones((dim,), jnp.float32), 'b1': jnp.zeros((dim,), jnp.float32), 'g2': jnp.ones((dim,), jnp.float32), 'b2': jnp.zeros((dim,), jnp.float32), 'g3': jnp.ones((dim,), jnp.float32), 'b3': jnp.zeros((dim,), jnp.float32)}
        return inp
    _L1_xattn_all = _L1_xattn_setup()
    _L1_xattn_in = {k: v for k, v in _L1_xattn_all.items() if k in ('Wq1', 'Wk1', 'Wv1', 'Wo1', 'bo1', 'Wq2', 'Wk2', 'Wv2', 'Wo2', 'bo2', 'Wp', 'bp', 'Wf', 'bf', 'g1', 'b1', 'g2', 'b2', 'g3', 'b3')}
    del _L1_xattn_all

    def _L2_xattn_setup():
        import jax, jax.numpy as jnp
        import numpy as np
        B_, S_, P_, D_ = (2, 128, 64, 256)
        L_ = 4
        DI_ = 2 * D_
        DS_ = 16
        DC_ = 4
        DR_ = D_ // 16
        PCD_ = 192

        def rmsnorm(x, w, eps=1e-05):
            return x * jax.lax.rsqrt(jnp.mean(x * x, axis=-1, keepdims=True) + eps) * w

        def mamba_block(x, ip_w, cw, cb, xp_w, dtp_w, dtp_b, A_log, Dp, op_w):
            B, S, _ = x.shape
            xz = jnp.einsum('bsd,ed->bse', x, ip_w)
            xi, z = jnp.split(xz, 2, axis=-1)
            xt = xi.transpose(0, 2, 1)
            conv = jax.lax.conv_general_dilated(xt, cw[:, None, :], (1,), [(DC_ - 1, 0)], feature_group_count=DI_) + cb[:, None]
            xi = jax.nn.silu(conv.transpose(0, 2, 1))
            xdbl = jnp.einsum('bse,fe->bsf', xi, xp_w)
            dt, Bm, Cm = jnp.split(xdbl, [DR_, DR_ + DS_], axis=-1)
            dt = jax.nn.softplus(jnp.einsum('bsr,er->bse', dt, dtp_w) + dtp_b)
            A = -jnp.exp(A_log)
            dA = jnp.exp(dt[..., None] * A)
            dBu = dt[..., None] * Bm[:, :, None, :] * xi[..., None]

            def step(h, t):
                da, dbu, c = t
                h = da * h + dbu
                return (h, jnp.einsum('bes,bs->be', h, c))
            h0 = jnp.zeros((B, DI_, DS_), x.dtype)
            _, ys = jax.lax.scan(step, h0, (dA.transpose(1, 0, 2, 3), dBu.transpose(1, 0, 2, 3), Cm.transpose(1, 0, 2)))
            y = ys.transpose(1, 0, 2) + xi * Dp
            y = y * jax.nn.silu(z)
            return jnp.einsum('bse,de->bsd', y, op_w)
        key = jax.random.key(seed)
        ks = jax.random.split(key, 12)
        n = lambda k, s, sc=0.02: jax.random.normal(k, s, dtype=jnp.float32) * sc
        A_log = jnp.log(jnp.broadcast_to(jnp.arange(1, DS_ + 1, dtype=jnp.float32), (L_, DI_, DS_)))
        return {'x': jax.random.normal(ks[0], (B_, S_, D_), dtype=jnp.float32), 'prepend_cond': jax.random.normal(ks[1], (B_, P_, PCD_), dtype=jnp.float32), 'pre_w1': n(ks[2], (PCD_, D_)), 'pre_w2': n(ks[3], (D_, D_)), 'norm_w': jnp.ones((L_, D_), jnp.float32), 'in_proj_w': n(ks[4], (L_, 2 * DI_, D_)), 'conv_w': n(ks[5], (L_, DI_, DC_), 0.1), 'conv_b': jnp.zeros((L_, DI_), jnp.float32), 'x_proj_w': n(ks[6], (L_, DR_ + 2 * DS_, DI_)), 'dt_proj_w': n(ks[7], (L_, DI_, DR_), 0.1), 'dt_proj_b': jax.random.uniform(ks[8], (L_, DI_), jnp.float32, -4.0, -2.0), 'A_log': A_log, 'D_param': jnp.ones((L_, DI_), jnp.float32), 'out_proj_w': n(ks[9], (L_, D_, DI_)), 'final_norm_w': jnp.ones((D_,), jnp.float32)}
    _L2_xattn_all = _L2_xattn_setup()
    _L2_xattn_in = {k: v for k, v in _L2_xattn_all.items() if k in ('pre_w1', 'pre_w2', 'norm_w', 'in_proj_w', 'conv_w', 'conv_b', 'x_proj_w', 'dt_proj_w', 'dt_proj_b', 'A_log', 'D_param', 'out_proj_w', 'final_norm_w')}
    del _L2_xattn_all

    def _L3_xattn_setup():
        import jax, jax.numpy as jnp
        import numpy as np
        B, S, L = (2, 512, 128)
        WIDTH, HEADS, CTX = (256, 16, 192)
        HD = WIDTH // HEADS
        EPS = 1e-05

        def _layernorm(x, g, b):
            m = jnp.mean(x, axis=-1, keepdims=True)
            v = jnp.mean(jnp.square(x - m), axis=-1, keepdims=True)
            return (x - m) * jax.lax.rsqrt(v + EPS) * g + b

        def _mha(q_in, kv_in, wq, bq, wk, bk, wv, bv, wo, bo):
            b = q_in.shape[0]
            q = (q_in @ wq.T + bq).reshape(b, -1, HEADS, HD).transpose(0, 2, 1, 3)
            k = (kv_in @ wk.T + bk).reshape(b, -1, HEADS, HD).transpose(0, 2, 1, 3)
            v = (kv_in @ wv.T + bv).reshape(b, -1, HEADS, HD).transpose(0, 2, 1, 3)
            scores = jnp.einsum('bhqd,bhkd->bhqk', q, k) * HD ** (-0.5)
            p = jax.nn.softmax(scores, axis=-1)
            o = jnp.einsum('bhqk,bhkd->bhqd', p, v)
            o = o.transpose(0, 2, 1, 3).reshape(b, -1, WIDTH)
            return o @ wo.T + bo
        key = jax.random.key(seed)
        ks = jax.random.split(key, 32)

        def xav(k, shape, gain=1.0):
            fan_out, fan_in = shape
            a = gain * np.sqrt(6.0 / (fan_in + fan_out))
            return jax.random.uniform(k, shape, jnp.float32, -a, a)
        g2 = 1.0 / np.sqrt(2.0)
        inp = {'x': jax.random.normal(ks[0], (B, S, WIDTH), jnp.float32), 'context': jax.random.normal(ks[1], (B, L, CTX), jnp.float32), 'ln1_g': jnp.ones((WIDTH,), jnp.float32), 'ln1_b': jnp.zeros((WIDTH,), jnp.float32), 'ln2_g': jnp.ones((WIDTH,), jnp.float32), 'ln2_b': jnp.zeros((WIDTH,), jnp.float32), 'ln3_g': jnp.ones((WIDTH,), jnp.float32), 'ln3_b': jnp.zeros((WIDTH,), jnp.float32), 'sa_wq': xav(ks[2], (WIDTH, WIDTH), g2), 'sa_bq': jnp.zeros((WIDTH,), jnp.float32), 'sa_wk': xav(ks[3], (WIDTH, WIDTH), g2), 'sa_bk': jnp.zeros((WIDTH,), jnp.float32), 'sa_wv': xav(ks[4], (WIDTH, WIDTH), g2), 'sa_bv': jnp.zeros((WIDTH,), jnp.float32), 'sa_wo': xav(ks[5], (WIDTH, WIDTH), 1.0), 'sa_bo': jnp.zeros((WIDTH,), jnp.float32), 'ca_wq': xav(ks[6], (WIDTH, WIDTH), g2), 'ca_bq': jnp.zeros((WIDTH,), jnp.float32), 'ca_wk': xav(ks[7], (WIDTH, CTX), g2), 'ca_bk': jnp.zeros((WIDTH,), jnp.float32), 'ca_wv': xav(ks[8], (WIDTH, CTX), g2), 'ca_bv': jnp.zeros((WIDTH,), jnp.float32), 'ca_wo': xav(ks[9], (WIDTH, WIDTH), 1.0), 'ca_bo': jnp.zeros((WIDTH,), jnp.float32), 'mlp_w1': 0.02 * jax.random.normal(ks[10], (4 * WIDTH, WIDTH), jnp.float32), 'mlp_b1': jnp.zeros((4 * WIDTH,), jnp.float32), 'mlp_w2': 0.02 * jax.random.normal(ks[11], (WIDTH, 4 * WIDTH), jnp.float32), 'mlp_b2': jnp.zeros((WIDTH,), jnp.float32)}
        return inp
    _L3_xattn_all = _L3_xattn_setup()
    _L3_xattn_in = {k: v for k, v in _L3_xattn_all.items() if k in ('ln1_g', 'ln1_b', 'ln2_g', 'ln2_b', 'ln3_g', 'ln3_b', 'sa_wq', 'sa_bq', 'sa_wk', 'sa_bk', 'sa_wv', 'sa_bv', 'sa_wo', 'sa_bo', 'ca_wq', 'ca_bq', 'ca_wk', 'ca_bk', 'ca_wv', 'ca_bv', 'ca_wo', 'ca_bo', 'mlp_w1', 'mlp_b1', 'mlp_w2', 'mlp_b2')}
    del _L3_xattn_all
    return {'x': x, 'ctx_768': ctx_768, 'L0_xattn_Wq': _L0_xattn_in['Wq'], 'L0_xattn_bq': _L0_xattn_in['bq'], 'L0_xattn_Wk': _L0_xattn_in['Wk'], 'L0_xattn_bk': _L0_xattn_in['bk'], 'L0_xattn_Wv': _L0_xattn_in['Wv'], 'L0_xattn_bv': _L0_xattn_in['bv'], 'L0_xattn_Wo': _L0_xattn_in['Wo'], 'L0_xattn_bo': _L0_xattn_in['bo'], 'L0_xattn_ln_g': _L0_xattn_in['ln_g'], 'L0_xattn_ln_b': _L0_xattn_in['ln_b'], 'L0_xattn_W1': _L0_xattn_in['W1'], 'L0_xattn_b1': _L0_xattn_in['b1'], 'L0_xattn_W2': _L0_xattn_in['W2'], 'L0_xattn_b2': _L0_xattn_in['b2'], 'L1_xattn_Wq1': _L1_xattn_in['Wq1'], 'L1_xattn_Wk1': _L1_xattn_in['Wk1'], 'L1_xattn_Wv1': _L1_xattn_in['Wv1'], 'L1_xattn_Wo1': _L1_xattn_in['Wo1'], 'L1_xattn_bo1': _L1_xattn_in['bo1'], 'L1_xattn_Wq2': _L1_xattn_in['Wq2'], 'L1_xattn_Wk2': _L1_xattn_in['Wk2'], 'L1_xattn_Wv2': _L1_xattn_in['Wv2'], 'L1_xattn_Wo2': _L1_xattn_in['Wo2'], 'L1_xattn_bo2': _L1_xattn_in['bo2'], 'L1_xattn_Wp': _L1_xattn_in['Wp'], 'L1_xattn_bp': _L1_xattn_in['bp'], 'L1_xattn_Wf': _L1_xattn_in['Wf'], 'L1_xattn_bf': _L1_xattn_in['bf'], 'L1_xattn_g1': _L1_xattn_in['g1'], 'L1_xattn_b1': _L1_xattn_in['b1'], 'L1_xattn_g2': _L1_xattn_in['g2'], 'L1_xattn_b2': _L1_xattn_in['b2'], 'L1_xattn_g3': _L1_xattn_in['g3'], 'L1_xattn_b3': _L1_xattn_in['b3'], 'L2_xattn_pre_w1': _L2_xattn_in['pre_w1'], 'L2_xattn_pre_w2': _L2_xattn_in['pre_w2'], 'L2_xattn_norm_w': _L2_xattn_in['norm_w'], 'L2_xattn_in_proj_w': _L2_xattn_in['in_proj_w'], 'L2_xattn_conv_w': _L2_xattn_in['conv_w'], 'L2_xattn_conv_b': _L2_xattn_in['conv_b'], 'L2_xattn_x_proj_w': _L2_xattn_in['x_proj_w'], 'L2_xattn_dt_proj_w': _L2_xattn_in['dt_proj_w'], 'L2_xattn_dt_proj_b': _L2_xattn_in['dt_proj_b'], 'L2_xattn_A_log': _L2_xattn_in['A_log'], 'L2_xattn_D_param': _L2_xattn_in['D_param'], 'L2_xattn_out_proj_w': _L2_xattn_in['out_proj_w'], 'L2_xattn_final_norm_w': _L2_xattn_in['final_norm_w'], 'L3_xattn_ln1_g': _L3_xattn_in['ln1_g'], 'L3_xattn_ln1_b': _L3_xattn_in['ln1_b'], 'L3_xattn_ln2_g': _L3_xattn_in['ln2_g'], 'L3_xattn_ln2_b': _L3_xattn_in['ln2_b'], 'L3_xattn_ln3_g': _L3_xattn_in['ln3_g'], 'L3_xattn_ln3_b': _L3_xattn_in['ln3_b'], 'L3_xattn_sa_wq': _L3_xattn_in['sa_wq'], 'L3_xattn_sa_bq': _L3_xattn_in['sa_bq'], 'L3_xattn_sa_wk': _L3_xattn_in['sa_wk'], 'L3_xattn_sa_bk': _L3_xattn_in['sa_bk'], 'L3_xattn_sa_wv': _L3_xattn_in['sa_wv'], 'L3_xattn_sa_bv': _L3_xattn_in['sa_bv'], 'L3_xattn_sa_wo': _L3_xattn_in['sa_wo'], 'L3_xattn_sa_bo': _L3_xattn_in['sa_bo'], 'L3_xattn_ca_wq': _L3_xattn_in['ca_wq'], 'L3_xattn_ca_bq': _L3_xattn_in['ca_bq'], 'L3_xattn_ca_wk': _L3_xattn_in['ca_wk'], 'L3_xattn_ca_bk': _L3_xattn_in['ca_bk'], 'L3_xattn_ca_wv': _L3_xattn_in['ca_wv'], 'L3_xattn_ca_bv': _L3_xattn_in['ca_bv'], 'L3_xattn_ca_wo': _L3_xattn_in['ca_wo'], 'L3_xattn_ca_bo': _L3_xattn_in['ca_bo'], 'L3_xattn_mlp_w1': _L3_xattn_in['mlp_w1'], 'L3_xattn_mlp_b1': _L3_xattn_in['mlp_b1'], 'L3_xattn_mlp_w2': _L3_xattn_in['mlp_w2'], 'L3_xattn_mlp_b2': _L3_xattn_in['mlp_b2']}

def reference(x, ctx_768, L0_xattn_Wq, L0_xattn_bq, L0_xattn_Wk, L0_xattn_bk, L0_xattn_Wv, L0_xattn_bv, L0_xattn_Wo, L0_xattn_bo, L0_xattn_ln_g, L0_xattn_ln_b, L0_xattn_W1, L0_xattn_b1, L0_xattn_W2, L0_xattn_b2, L1_xattn_Wq1, L1_xattn_Wk1, L1_xattn_Wv1, L1_xattn_Wo1, L1_xattn_bo1, L1_xattn_Wq2, L1_xattn_Wk2, L1_xattn_Wv2, L1_xattn_Wo2, L1_xattn_bo2, L1_xattn_Wp, L1_xattn_bp, L1_xattn_Wf, L1_xattn_bf, L1_xattn_g1, L1_xattn_b1, L1_xattn_g2, L1_xattn_b2, L1_xattn_g3, L1_xattn_b3, L2_xattn_pre_w1, L2_xattn_pre_w2, L2_xattn_norm_w, L2_xattn_in_proj_w, L2_xattn_conv_w, L2_xattn_conv_b, L2_xattn_x_proj_w, L2_xattn_dt_proj_w, L2_xattn_dt_proj_b, L2_xattn_A_log, L2_xattn_D_param, L2_xattn_out_proj_w, L2_xattn_final_norm_w, L3_xattn_ln1_g, L3_xattn_ln1_b, L3_xattn_ln2_g, L3_xattn_ln2_b, L3_xattn_ln3_g, L3_xattn_ln3_b, L3_xattn_sa_wq, L3_xattn_sa_bq, L3_xattn_sa_wk, L3_xattn_sa_bk, L3_xattn_sa_wv, L3_xattn_sa_bv, L3_xattn_sa_wo, L3_xattn_sa_bo, L3_xattn_ca_wq, L3_xattn_ca_bq, L3_xattn_ca_wk, L3_xattn_ca_bk, L3_xattn_ca_wv, L3_xattn_ca_bv, L3_xattn_ca_wo, L3_xattn_ca_bo, L3_xattn_mlp_w1, L3_xattn_mlp_b1, L3_xattn_mlp_w2, L3_xattn_mlp_b2):
    import jax
    import jax.numpy as jnp

    def _L0_xattn_ref(x, xf, Wq, bq, Wk, bk, Wv, bv, Wo, bo, ln_g, ln_b, W1, b1, W2, b2):
        import jax, jax.numpy as jnp
        import numpy as np
        LATENT = 256
        TEXT = 192
        HEADS = 16
        HEAD_DIM = LATENT // HEADS
        SCALE = HEAD_DIM ** (-0.5)
        LN_EPS = 1e-05
        B, Tx, D = x.shape
        Txf = xf.shape[1]
        q = (x @ Wq + bq).reshape(B, Tx, HEADS, HEAD_DIM).transpose(0, 2, 1, 3)
        k = (xf @ Wk + bk).reshape(B, Txf, HEADS, HEAD_DIM).transpose(0, 2, 1, 3)
        v = (xf @ Wv + bv).reshape(B, Txf, HEADS, HEAD_DIM).transpose(0, 2, 1, 3)
        scores = jnp.einsum('bhqd,bhkd->bhqk', q * SCALE, k)
        probs = jax.nn.softmax(scores, axis=-1)
        attn = jnp.einsum('bhqk,bhkd->bhqd', probs, v)
        out = attn.transpose(0, 2, 1, 3).reshape(B, Tx, D)
        out = out @ Wo + bo
        mu = jnp.mean(out, axis=-1, keepdims=True)
        var = jnp.var(out, axis=-1, keepdims=True)
        h = (out - mu) * jax.lax.rsqrt(var + LN_EPS) * ln_g + ln_b
        h = jax.nn.gelu(h @ W1 + b1, approximate=False)
        ffn = h @ W2 + b2
        out = out + ffn
        return x + out

    def _L1_xattn_ref(x, context, Wq1, Wk1, Wv1, Wo1, bo1, Wq2, Wk2, Wv2, Wo2, bo2, Wp, bp, Wf, bf, g1, b1, g2, b2, g3, b3):
        import jax, jax.numpy as jnp
        import numpy as np
        HEADS = 16
        D_HEAD = 64
        EPS = 1e-05

        def _ln(x, g, b):
            m = jnp.mean(x, axis=-1, keepdims=True)
            v = jnp.var(x, axis=-1, keepdims=True)
            return (x - m) * jax.lax.rsqrt(v + EPS) * g + b

        def _attn(xq, xc, Wq, Wk, Wv, Wo, bo):
            B, N, _ = xq.shape
            S = xc.shape[1]
            q = (xq @ Wq).reshape(B, N, HEADS, D_HEAD)
            k = (xc @ Wk).reshape(B, S, HEADS, D_HEAD)
            v = (xc @ Wv).reshape(B, S, HEADS, D_HEAD)
            scale = D_HEAD ** (-0.5)
            scores = jnp.einsum('bnhd,bshd->bhns', q, k) * scale
            attn = jax.nn.softmax(scores, axis=-1)
            out = jnp.einsum('bhns,bshd->bnhd', attn, v).reshape(B, N, HEADS * D_HEAD)
            return out @ Wo + bo

        def _geglu_ff(x, Wp, bp, Wf, bf):
            h = x @ Wp + bp
            a, gate = jnp.split(h, 2, axis=-1)
            return a * jax.nn.gelu(gate, approximate=False) @ Wf + bf
        x = _attn(_ln(x, g1, b1), _ln(x, g1, b1), Wq1, Wk1, Wv1, Wo1, bo1) + x
        x = _attn(_ln(x, g2, b2), context, Wq2, Wk2, Wv2, Wo2, bo2) + x
        x = _geglu_ff(_ln(x, g3, b3), Wp, bp, Wf, bf) + x
        return x

    def _L2_xattn_ref(x, prepend_cond, pre_w1, pre_w2, norm_w, in_proj_w, conv_w, conv_b, x_proj_w, dt_proj_w, dt_proj_b, A_log, D_param, out_proj_w, final_norm_w):
        import jax, jax.numpy as jnp
        import numpy as np
        B_, S_, P_, D_ = (2, 128, 64, 256)
        L_ = 4
        DI_ = 2 * D_
        DS_ = 16
        DC_ = 4
        DR_ = D_ // 16
        PCD_ = 192

        def rmsnorm(x, w, eps=1e-05):
            return x * jax.lax.rsqrt(jnp.mean(x * x, axis=-1, keepdims=True) + eps) * w

        def mamba_block(x, ip_w, cw, cb, xp_w, dtp_w, dtp_b, A_log, Dp, op_w):
            B, S, _ = x.shape
            xz = jnp.einsum('bsd,ed->bse', x, ip_w)
            xi, z = jnp.split(xz, 2, axis=-1)
            xt = xi.transpose(0, 2, 1)
            conv = jax.lax.conv_general_dilated(xt, cw[:, None, :], (1,), [(DC_ - 1, 0)], feature_group_count=DI_) + cb[:, None]
            xi = jax.nn.silu(conv.transpose(0, 2, 1))
            xdbl = jnp.einsum('bse,fe->bsf', xi, xp_w)
            dt, Bm, Cm = jnp.split(xdbl, [DR_, DR_ + DS_], axis=-1)
            dt = jax.nn.softplus(jnp.einsum('bsr,er->bse', dt, dtp_w) + dtp_b)
            A = -jnp.exp(A_log)
            dA = jnp.exp(dt[..., None] * A)
            dBu = dt[..., None] * Bm[:, :, None, :] * xi[..., None]

            def step(h, t):
                da, dbu, c = t
                h = da * h + dbu
                return (h, jnp.einsum('bes,bs->be', h, c))
            h0 = jnp.zeros((B, DI_, DS_), x.dtype)
            _, ys = jax.lax.scan(step, h0, (dA.transpose(1, 0, 2, 3), dBu.transpose(1, 0, 2, 3), Cm.transpose(1, 0, 2)))
            y = ys.transpose(1, 0, 2) + xi * Dp
            y = y * jax.nn.silu(z)
            return jnp.einsum('bse,de->bsd', y, op_w)
        p = jax.nn.silu(prepend_cond @ pre_w1) @ pre_w2
        h = jnp.concatenate([p, x], axis=1)
        for l in range(L_):
            h = h + mamba_block(rmsnorm(h, norm_w[l]), in_proj_w[l], conv_w[l], conv_b[l], x_proj_w[l], dt_proj_w[l], dt_proj_b[l], A_log[l], D_param[l], out_proj_w[l])
        h = rmsnorm(h, final_norm_w)
        return h[:, P_:, :]

    def _L3_xattn_ref(x, context, ln1_g, ln1_b, ln2_g, ln2_b, ln3_g, ln3_b, sa_wq, sa_bq, sa_wk, sa_bk, sa_wv, sa_bv, sa_wo, sa_bo, ca_wq, ca_bq, ca_wk, ca_bk, ca_wv, ca_bv, ca_wo, ca_bo, mlp_w1, mlp_b1, mlp_w2, mlp_b2):
        import jax, jax.numpy as jnp
        import numpy as np
        B, S, L = (2, 512, 128)
        WIDTH, HEADS, CTX = (256, 16, 192)
        HD = WIDTH // HEADS
        EPS = 1e-05

        def _layernorm(x, g, b):
            m = jnp.mean(x, axis=-1, keepdims=True)
            v = jnp.mean(jnp.square(x - m), axis=-1, keepdims=True)
            return (x - m) * jax.lax.rsqrt(v + EPS) * g + b

        def _mha(q_in, kv_in, wq, bq, wk, bk, wv, bv, wo, bo):
            b = q_in.shape[0]
            q = (q_in @ wq.T + bq).reshape(b, -1, HEADS, HD).transpose(0, 2, 1, 3)
            k = (kv_in @ wk.T + bk).reshape(b, -1, HEADS, HD).transpose(0, 2, 1, 3)
            v = (kv_in @ wv.T + bv).reshape(b, -1, HEADS, HD).transpose(0, 2, 1, 3)
            scores = jnp.einsum('bhqd,bhkd->bhqk', q, k) * HD ** (-0.5)
            p = jax.nn.softmax(scores, axis=-1)
            o = jnp.einsum('bhqk,bhkd->bhqd', p, v)
            o = o.transpose(0, 2, 1, 3).reshape(b, -1, WIDTH)
            return o @ wo.T + bo
        h = _layernorm(x, ln1_g, ln1_b)
        x = x + _mha(h, h, sa_wq, sa_bq, sa_wk, sa_bk, sa_wv, sa_bv, sa_wo, sa_bo)
        h = _layernorm(x, ln2_g, ln2_b)
        x = x + _mha(h, context, ca_wq, ca_bq, ca_wk, ca_bk, ca_wv, ca_bv, ca_wo, ca_bo)
        h = _layernorm(x, ln3_g, ln3_b)
        h = jax.nn.gelu(h @ mlp_w1.T + mlp_b1, approximate=False) @ mlp_w2.T + mlp_b2
        return x + h
    x = _L0_xattn_ref(x, ctx_768, L0_xattn_Wq, L0_xattn_bq, L0_xattn_Wk, L0_xattn_bk, L0_xattn_Wv, L0_xattn_bv, L0_xattn_Wo, L0_xattn_bo, L0_xattn_ln_g, L0_xattn_ln_b, L0_xattn_W1, L0_xattn_b1, L0_xattn_W2, L0_xattn_b2)
    x = _L1_xattn_ref(x, ctx_768, L1_xattn_Wq1, L1_xattn_Wk1, L1_xattn_Wv1, L1_xattn_Wo1, L1_xattn_bo1, L1_xattn_Wq2, L1_xattn_Wk2, L1_xattn_Wv2, L1_xattn_Wo2, L1_xattn_bo2, L1_xattn_Wp, L1_xattn_bp, L1_xattn_Wf, L1_xattn_bf, L1_xattn_g1, L1_xattn_b1, L1_xattn_g2, L1_xattn_b2, L1_xattn_g3, L1_xattn_b3)
    x = _L2_xattn_ref(x, ctx_768, L2_xattn_pre_w1, L2_xattn_pre_w2, L2_xattn_norm_w, L2_xattn_in_proj_w, L2_xattn_conv_w, L2_xattn_conv_b, L2_xattn_x_proj_w, L2_xattn_dt_proj_w, L2_xattn_dt_proj_b, L2_xattn_A_log, L2_xattn_D_param, L2_xattn_out_proj_w, L2_xattn_final_norm_w)
    x = _L3_xattn_ref(x, ctx_768, L3_xattn_ln1_g, L3_xattn_ln1_b, L3_xattn_ln2_g, L3_xattn_ln2_b, L3_xattn_ln3_g, L3_xattn_ln3_b, L3_xattn_sa_wq, L3_xattn_sa_bq, L3_xattn_sa_wk, L3_xattn_sa_bk, L3_xattn_sa_wv, L3_xattn_sa_bv, L3_xattn_sa_wo, L3_xattn_sa_bo, L3_xattn_ca_wq, L3_xattn_ca_bq, L3_xattn_ca_wk, L3_xattn_ca_bk, L3_xattn_ca_wv, L3_xattn_ca_bv, L3_xattn_ca_wo, L3_xattn_ca_bo, L3_xattn_mlp_w1, L3_xattn_mlp_b1, L3_xattn_mlp_w2, L3_xattn_mlp_b2)
    return x

_drawn_inputs = setup_inputs


def setup_inputs(seed=0):
    import zlib

    import numpy as np

    out = dict(_drawn_inputs(seed))
    spreads = {'L0_xattn_ln_g': (1.0, 0.2),
     'L0_xattn_ln_b': (0.0, 0.275),
     'L1_xattn_bo1': (0.0, 0.1),
     'L1_xattn_bo2': (0.0, 0.1),
     'L1_xattn_bp': (0.0, 0.1),
     'L1_xattn_bf': (0.0, 0.1),
     'L1_xattn_g1': (1.0, 0.2),
     'L1_xattn_b1': (0.0, 0.1),
     'L1_xattn_g2': (1.0, 0.2),
     'L1_xattn_b2': (0.0, 0.33),
     'L1_xattn_g3': (1.0, 0.2),
     'L1_xattn_b3': (0.0, 0.1),
     'L2_xattn_norm_w': (1.0, 0.6),
     'L2_xattn_conv_b': (0.0, 0.8),
     'L2_xattn_D_param': (1.0, 0.6),
     'L2_xattn_final_norm_w': (1.0, 0.2),
     'L3_xattn_ln1_g': (1.0, 0.6),
     'L3_xattn_ln1_b': (0.0, 0.1),
     'L3_xattn_ln2_g': (1.0, 0.6),
     'L3_xattn_ln2_b': (0.0, 0.8),
     'L3_xattn_ln3_g': (1.0, 0.6),
     'L3_xattn_ln3_b': (0.0, 0.8),
     'L3_xattn_sa_bq': (0.0, 0.8),
     'L3_xattn_sa_bk': (0.0, 2.0),
     'L3_xattn_sa_bv': (0.0, 0.1),
     'L3_xattn_sa_bo': (0.0, 0.1),
     'L3_xattn_ca_bq': (0.0, 0.8),
     'L3_xattn_ca_bk': (0.0, 2.0),
     'L3_xattn_ca_bv': (0.0, 0.1),
     'L3_xattn_ca_bo': (0.0, 0.1),
     'L3_xattn_mlp_b1': (0.0, 0.268),
     'L3_xattn_mlp_b2': (0.0, 0.1)}
    factors = {'L0_xattn_bq': 8.0,
     'L0_xattn_bk': 64.0,
     'L0_xattn_b1': 3.025,
     'L2_xattn_pre_w1': 8.0,
     'L2_xattn_pre_w2': 8.0,
     'L2_xattn_in_proj_w': 8.0,
     'L2_xattn_conv_w': 8.0,
     'L2_xattn_x_proj_w': 8.0,
     'L2_xattn_dt_proj_w': 8.0,
     'L2_xattn_dt_proj_b': 8.0,
     'L2_xattn_A_log': 8.0,
     'L2_xattn_out_proj_w': 8.0}
    for name, (base, spread) in spreads.items():
        noise = np.random.default_rng([zlib.crc32(name.encode()), seed]).standard_normal(out[name].shape)
        drawn = base * np.exp(spread * noise) if base else spread * noise
        out[name] = jnp.asarray(drawn.astype(out[name].dtype))
    for name, factor in factors.items():
        out[name] = (out[name] * factor).astype(out[name].dtype)
    return out
```

```python
import numpy as np
from contextlib import ExitStack
import concourse.bass as bass
from concourse import mybir

F32 = mybir.dt.float32
ALU = mybir.AluOpType
ACT = mybir.ActivationFunctionType
AX = mybir.AxisListType

P = 128
B = 4
T = 512
D = 256
H = 16
KEYS = 64
CTX = 192
INNER = 1024
FF = 1024
NT = T // P
ND = D // P
EPS = 1e-5
L = 4
DI = 512
NE = DI // P
DS = 16
DR = 16
S2 = KEYS + T
NX = DR + 2 * DS
BANK = 512
TT = [(s, min(P, S2 - s)) for s in range(0, S2, P)]
SOFTPLUS_LINEAR = 20.0

C_IDENT, C_MEAN = 0, P
C_MK = 2 * P
C_MV = C_MK + 8
C_M64 = C_MV + 32
C_PAR = C_M64 + 2
C_END = C_PAR + 2


def columns(*parts):
    at, out = 0, {}
    for name, n in parts:
        out[name] = at
        at += n
    return out, at


W0, W0N = columns(("q", 2 * D), ("k", 2 * D), ("v", 2 * D), ("p1", 2 * D), ("p2", 2 * D),
                  ("o", 2 * D), ("w1", 2 * FF), ("w2", 8 * D))
W1A, W1AN = columns(("q", 2 * INNER), ("k", 2 * INNER), ("v", 2 * INNER), ("o", 8 * D))
W1B, W1BN = columns(("q", 2 * INNER), ("k", 2 * INNER), ("v", 2 * INNER), ("o", 8 * D),
                    ("p", 4 * FF), ("f", 8 * D))
W2, W2N = columns(("in", 2 * 2 * DI), ("x", NE * NX), ("out", NE * D), ("dt", DI))
W3, W3N = columns(("sq", 2 * D), ("sk", 2 * D), ("sv", 2 * D), ("so", 2 * D),
                  ("cq", 2 * D), ("ck", 2 * D), ("cv", 2 * D), ("co", 2 * D),
                  ("w1", 2 * FF), ("w2", 8 * D))
V0, V0N = columns(("q", 2), ("k", 2), ("v", 2), ("o", 2), ("g", 2), ("b", 2), ("b1", 8), ("b2", 2),
                  ("g1", 2), ("n1", 2), ("o1", 2), ("g2", 2), ("n2", 2), ("o2", 2), ("g3", 2), ("n3", 2),
                  ("p", 16), ("f", 2))
V2, V2N = columns(("norm", 2), ("cw", NE * 4), ("cb", NE), ("dtb", NE), ("D", NE), ("A", NE * DS))
V3, V3N = columns(("fin", 2), ("g1", 2), ("n1", 2), ("g2", 2), ("n2", 2), ("g3", 2), ("n3", 2),
                  ("sq", 2), ("sk", 2), ("sv", 2), ("so", 2), ("cq", 2), ("ck", 2), ("cv", 2), ("co", 2),
                  ("b1", 8), ("b2", 2))


class Steps:

    def __init__(self, sem, known):
        self.sem, self.known, self.n, self.names = sem, known, 0, {}

    def step(self, name=None):
        self.n += 1
        if name is not None:
            assert name not in self.names, name
            self.names[name] = self.n
        return 1

    def at(self, name):
        return self.known.get(name, 1)


class Program:

    def __init__(self, sems, known):
        self.pe, self.act, self.dve, self.pool = (
            Steps(s, known.get(n, {})) for s, n in zip(sems, ("pe", "act", "dve", "pool")))
        self.where = {}
        self.known_where = known.get("where", {})

    def bank_of(self, job):
        return self.known_where.get(job, 0)

    def result(self):
        return {"pe": self.pe.names, "act": self.act.names, "dve": self.dve.names,
                "pool": self.pool.names, "where": self.where}


class Ring:

    def __init__(self, prog, view, slots):
        self.prog, self.view, self.slots, self.i, self.last = prog, view, slots, 0, [None] * len(slots)

    def take(self, job, steps, emptied):
        k = self.i % len(self.slots)
        self.i += 1
        freed, self.last[k] = self.last[k], (steps.sem, steps.at(emptied))
        self.prog.where[job] = self.slots[k]
        return self.view(self.slots[k]), freed


def build(nc, known, x_in, ctx_in, cst_in, w0_in, w1a_in, w1b_in, v0_in, w2_in, v2_in, w3_in, v3_in, out):
    found = {}
    stack = ExitStack()
    with stack:
        sem = lambda name: stack.enter_context(nc.semaphore(name))
        pe_done, act_done, dve_done, pool_done = (sem(n) for n in ("pe_done", "act_done", "dve_done", "pool_done"))
        engine_sems = (pe_done, act_done, dve_done, pool_done)
        const_loaded, w0_loaded, w1a_loaded, w1b_loaded, w3_loaded = (
            sem(n) for n in ("const_loaded", "w0_loaded", "w1a_loaded", "w1b_loaded", "w3_loaded"))
        x_loaded, x_stored, layer_loaded = sem("x_loaded"), sem("x_stored"), sem("layer_loaded")
        per_block = (*engine_sems, x_loaded, x_stored)

        hs = nc.dram_tensor("hs", (B, P, ND * S2), F32, kind="Internal").ap()
        psum = stack.enter_context(nc.psum_tensor("psum", [P, 8 * BANK], F32))
        cst = stack.enter_context(nc.sbuf_tensor("cst", [P, C_END], F32))
        ident = cst[:, C_IDENT:C_IDENT + P]
        mean_w = cst[:, C_MEAN:C_MEAN + P]

        def bank(i):
            return psum[:, i * BANK:(i + 1) * BANK]

        def wide(i):
            return psum[:, i * BANK:i * BANK + S2]

        def end_of_block():
            for s in per_block:
                nc.sync.sem_clear(s)
            nc.all_engine_barrier()

        class Dense:

            def __init__(self, name, sb):
                self.prog = prog = Program(engine_sems, known.get(name, {}))
                self.lin = Ring(prog, bank, [0, 1, 2])
                self.scr = Ring(prog, bank, [3, 4, 5])
                self.trn = Ring(prog, bank, [6, 7])
                self.dx = sb("dx", [P, ND, T])
                self.sq = sb("sq", [P, ND, T])
                self.rs = sb("rs", [P, T])
                self.ln = sb("ln", [P, ND, T])
                self.pr = sb("pr", [P, 3, T])
                self.ptr = sb("ptr", [P, 2 * NT, P])
                self.mx = sb("mx", [P, 4, H // 2])
                self.sm = sb("sm", [P, 4, H // 2])
                self.ri = sb("ri", [P, 4, H // 2])
                self.smh = sb("smh", [P, 2, H])
                self.rih = sb("rih", [P, 2, H])
                self.nm = sb("nm", [P, 4])

            def pe_linear(self, pe, name, w, x, nk, tiles, of, width=T):
                p = self.prog
                for j in tiles:
                    b, emptied = self.lin.take(f"{name} {j}", of, f"{name} {j} out")
                    if emptied:
                        pe.wait_ge(*emptied)
                    for k in range(nk):
                        mm = nc.tensor.matmul(b[:, 0:width], w[:, k, j * P:(j + 1) * P], x[:, k, 0:width],
                                              start=k == 0, stop=k == nk - 1)
                    mm.then_inc(pe_done, p.pe.step(f"{name} {j}"))

            def full(self, job):
                return bank(self.prog.bank_of(job))

            def pe_norm(self, pe, name, x, ready, rms=False):
                p = self.prog
                if not rms:
                    pe.wait_ge(*ready)
                    b, emptied = self.lin.take(f"{name} mean", p.dve, f"{name} centred")
                    if emptied:
                        pe.wait_ge(*emptied)
                    for k in range(ND):
                        mm = nc.tensor.matmul(b, mean_w, x[:, k, :], start=k == 0, stop=k == ND - 1)
                    mm.then_inc(pe_done, p.pe.step(f"{name} mean"))
                b, emptied = self.lin.take(f"{name} var", p.act, f"{name} log")
                if emptied:
                    pe.wait_ge(*emptied)
                pe.wait_ge(act_done, p.act.at(f"{name} squares"))
                for k in range(ND):
                    mm = nc.tensor.matmul(b, mean_w, self.sq[:, k, :], start=k == 0, stop=k == ND - 1)
                mm.then_inc(pe_done, p.pe.step(f"{name} var"))

            def act_norm(self, act, name, src=None):
                p = self.prog
                if src is None:
                    src = self.dx
                    act.wait_ge(dve_done, p.dve.at(f"{name} centred"))
                for k in range(ND):
                    a = nc.scalar.activation(self.sq[:, k, :], src[:, k, :], ACT.Square)
                    a.then_inc(act_done, p.act.step(f"{name} squares" if k == ND - 1 else None))
                act.wait_ge(pe_done, p.pe.at(f"{name} var"))
                nc.scalar.activation(self.rs[:, :], self.full(f"{name} var"), ACT.Ln, bias=self.eps[:, 0:1])\
                    .then_inc(act_done, p.act.step(f"{name} log"))
                act.wait_ge(act_done, p.act.n)
                nc.scalar.activation(self.rs[:, :], self.rs[:, :], ACT.Exp, scale=-0.5)\
                    .then_inc(act_done, p.act.step(f"{name} rstd"))

            def dve_norm(self, dve, name, x, g, b):
                p = self.prog
                dve.wait_ge(dve_done, p.dve.n)
                dve.wait_ge(pe_done, p.pe.at(f"{name} mean"))
                for k in range(ND):
                    nc.vector.tensor_tensor(self.dx[:, k, :], x[:, k, :], self.full(f"{name} mean"), ALU.subtract)\
                        .then_inc(dve_done, p.dve.step(f"{name} centred" if k == ND - 1 else None))
                dve.wait_ge(dve_done, p.dve.n)
                dve.wait_ge(act_done, p.act.at(f"{name} rstd"))
                for k in range(ND):
                    nc.vector.scalar_tensor_tensor(self.ln[:, k, :], self.dx[:, k, :], g[:, k:k + 1], self.rs[:, :],
                                                   ALU.mult, ALU.mult).then_inc(dve_done, p.dve.step())
                for k in range(ND):
                    dve.wait_ge(dve_done, p.dve.n - 1)
                    nc.vector.tensor_scalar(self.ln[:, k, :], self.ln[:, k, :], b[:, k:k + 1], None, ALU.add)\
                        .then_inc(dve_done, p.dve.step(f"{name} out" if k == ND - 1 else None))

            def dve_residual(self, dve, name, x, bias):
                p = self.prog
                for j in range(ND):
                    dve.wait_ge(dve_done, p.dve.n)
                    dve.wait_ge(pe_done, p.pe.at(f"{name} {j}"))
                    nc.vector.scalar_tensor_tensor(x[:, j, :], self.full(f"{name} {j}"), bias[:, j:j + 1], x[:, j, :],
                                                   ALU.add, ALU.add).then_inc(dve_done, p.dve.step(f"{name} {j} out"))

            def pe_mlp(self, pe, name, ready, w1, w2, hid):
                p = self.prog
                pe.wait_ge(*ready)
                self.pe_linear(pe, f"{name} up", w1, self.ln, ND, range(FF // P), p.act)
                pe.wait_ge(act_done, p.act.at(f"{name} up {FF // P - 1} out"))
                self.pe_linear(pe, f"{name} down", w2, hid, FF // P, range(ND), p.dve)

            def act_mlp(self, act, name, b1, hid):
                p = self.prog
                for j in range(FF // P):
                    act.wait_ge(pe_done, p.pe.at(f"{name} up {j}"))
                    nc.scalar.activation(hid[:, j, :], self.full(f"{name} up {j}"), ACT.Gelu, bias=b1[:, j:j + 1])\
                        .then_inc(act_done, p.act.step(f"{name} up {j} out"))

            def cross_units(self):
                return [(qt, g) for qt in range(NT) for g in range(2)]

            def pe_cross(self, pe, name, q, kbd, vbd, wide_heads):
                p = self.prog
                units = self.cross_units()

                def scores(u):
                    qt, g = units[u]
                    b, emptied = self.scr.take(f"{name} s {u}", p.dve, f"{name} shifted {u}")
                    if emptied:
                        pe.wait_ge(*emptied)
                    if wide_heads:
                        for f in range(4):
                            mm = nc.tensor.matmul(b[:, f * P:(f + 1) * P], q[:, 4 * g + f, qt * P:(qt + 1) * P],
                                                  kbd[:, 4 * g + f, :], start=True, stop=True)
                    else:
                        mm = nc.tensor.matmul(b, q[:, g, qt * P:(qt + 1) * P], kbd[:, g, :], start=True, stop=True)
                    mm.then_inc(pe_done, p.pe.step(f"{name} s {u}"))

                def flip(u):
                    b, emptied = self.trn.take(f"{name} t {u}", p.act, f"{name} flipped {u}")
                    if emptied:
                        pe.wait_ge(*emptied)
                    pe.wait_ge(pool_done, p.pool.at(f"{name} normed {u}"))
                    for hp in range(4):
                        mm = nc.tensor.transpose(b[:, hp * P:(hp + 1) * P], self.pr[:, u % 3, hp * P:(hp + 1) * P],
                                                 ident)
                    mm.then_inc(pe_done, p.pe.step(f"{name} t {u}"))

                for u in range(len(units) + 2):
                    if u < len(units):
                        scores(u)
                    if u >= 2:
                        flip(u - 2)
                pe.wait_ge(act_done, p.act.at(f"{name} flipped {len(units) - 1}"))
                if wide_heads:
                    for f in range(8):
                        b, emptied = self.lin.take(f"{name} o {f}", p.dve, f"{name} o {f} out")
                        if emptied:
                            pe.wait_ge(*emptied)
                        nc.tensor.matmul(b, vbd[:, f, :], self.pt[:, f // 4, f % 4, :], start=True, stop=True)\
                            .then_inc(pe_done, p.pe.step(f"{name} o {f}"))
                else:
                    for g in range(2):
                        b, emptied = self.lin.take(f"{name} o {g}", p.dve, f"{name} o {g} out")
                        if emptied:
                            pe.wait_ge(*emptied)
                        for hp in range(4):
                            mm = nc.tensor.matmul(b, vbd[:, g, hp, :], self.pt[:, g, hp, :],
                                                  start=hp == 0, stop=hp == 3)
                        mm.then_inc(pe_done, p.pe.step(f"{name} o {g}"))

            def dve_cross(self, dve, name):
                p = self.prog
                n = len(self.cross_units())

                def shift(u):
                    dve.wait_ge(pe_done, p.pe.at(f"{name} s {u}"))
                    s = self.full(f"{name} s {u}").rearrange("p (h k) -> p h k", k=KEYS)
                    dve.wait_ge(dve_done, p.dve.n)
                    nc.vector.tensor_reduce(self.mx[:, u % 4, :], s, AX.X, ALU.max)\
                        .then_inc(dve_done, p.dve.step())
                    dve.wait_ge(dve_done, p.dve.n)
                    if u >= 3:
                        dve.wait_ge(pe_done, p.pe.at(f"{name} t {u - 3}"))
                    nc.vector.tensor_tensor(self.pr[:, u % 3, :].rearrange("p (h k) -> p h k", k=KEYS), s,
                                            self.mx[:, u % 4, :].unsqueeze(2).to_broadcast([P, 8, KEYS]),
                                            ALU.subtract).then_inc(dve_done, p.dve.step(f"{name} shifted {u}"))

                def total(u):
                    dve.wait_ge(act_done, p.act.at(f"{name} exp {u}"))
                    dve.wait_ge(dve_done, p.dve.n)
                    nc.vector.tensor_reduce(self.sm[:, u % 4, :],
                                            self.pr[:, u % 3, :].rearrange("p (h k) -> p h k", k=KEYS),
                                            AX.X, ALU.add).then_inc(dve_done, p.dve.step())
                    dve.wait_ge(dve_done, p.dve.n)
                    nc.vector.reciprocal(self.ri[:, u % 4, :], self.sm[:, u % 4, :])\
                        .then_inc(dve_done, p.dve.step(f"{name} sums {u}"))

                for u in range(n + 1):
                    if u < n:
                        shift(u)
                    if u >= 1:
                        total(u - 1)

            def act_cross(self, act, name):
                p = self.prog
                n = len(self.cross_units())
                for u in range(n + 2):
                    if u < n:
                        act.wait_ge(dve_done, p.dve.at(f"{name} shifted {u}"))
                        nc.scalar.activation(self.pr[:, u % 3, :], self.pr[:, u % 3, :], ACT.Exp)\
                            .then_inc(act_done, p.act.step(f"{name} exp {u}"))
                    if u >= 2:
                        v = u - 2
                        qt, g = self.cross_units()[v]
                        act.wait_ge(pe_done, p.pe.at(f"{name} t {v}"))
                        nc.scalar.activation(self.pt[:, g, :, qt * P:(qt + 1) * P],
                                             self.full(f"{name} t {v}").rearrange("p (h t) -> p h t", h=4), ACT.Copy)\
                            .then_inc(act_done, p.act.step(f"{name} flipped {v}"))

            def pool_cross(self, pool, name):
                p = self.prog
                for u in range(len(self.cross_units())):
                    pool.wait_ge(dve_done, p.dve.at(f"{name} sums {u}"))
                    v = self.pr[:, u % 3, :].rearrange("p (h k) -> p h k", k=KEYS)
                    nc.gpsimd.tensor_tensor(v, v, self.ri[:, u % 4, :].unsqueeze(2).to_broadcast([P, 8, KEYS]),
                                            ALU.mult).then_inc(pool_done, p.pool.step(f"{name} normed {u}"))

            def pe_self(self, pe, name, q, k_of, v, hd):
                p = self.prog
                units = [(qt, h) for qt in range(NT) for h in range(H)]
                per_bank = min(H, BANK // hd)
                o_bank = {}

                def scores(u):
                    qt, h = units[u]
                    rows, lhs, rhs = k_of(h)
                    b, emptied = self.scr.take(f"{name} s {u}", p.act, f"{name} exp {u}")
                    if emptied:
                        pe.wait_ge(*emptied)
                    nc.tensor.matmul(b, q[rows, lhs, qt * P:(qt + 1) * P], rhs, start=True, stop=True)\
                        .then_inc(pe_done, p.pe.step(f"{name} s {u}"))

                def flip(u):
                    b, emptied = self.trn.take(f"{name} t {u}", p.dve, f"{name} flipped {u}")
                    if emptied:
                        pe.wait_ge(*emptied)
                    pe.wait_ge(act_done, p.act.at(f"{name} exp {u}"))
                    for kt in range(NT):
                        mm = nc.tensor.transpose(b[:, kt * P:(kt + 1) * P], self.pr[:, u % 3, kt * P:(kt + 1) * P],
                                                 ident)
                    mm.then_inc(pe_done, p.pe.step(f"{name} t {u}"))

                def weigh(u):
                    qt, h = units[u]
                    if h % per_bank == 0:
                        job = f"{name} h {qt} {h // per_bank}"
                        o_bank[0], emptied = self.lin.take(job, p.dve, f"{job} out")
                        if emptied:
                            pe.wait_ge(*emptied)
                    pe.wait_ge(dve_done, p.dve.at(f"{name} flipped {u}"))
                    at = (h % per_bank) * hd
                    for kt in range(NT):
                        mm = nc.tensor.matmul(o_bank[0][:, at:at + hd], self.ptr[:, NT * (u % 2) + kt, :],
                                              v[:, kt, h * hd:(h + 1) * hd], start=kt == 0, stop=kt == NT - 1)
                    mm.then_inc(pe_done, p.pe.step(f"{name} w {u}"))

                def turn(qt):
                    nf = H * hd // P
                    pe.wait_ge(dve_done, p.dve.at(f"{name} h {qt} {H // per_bank - 1} out"))
                    for f0 in range(0, nf, 4):
                        b, emptied = self.trn.take(f"{name} r {qt} {f0}", p.act, f"{name} turned {qt} {f0}")
                        if emptied:
                            pe.wait_ge(*emptied)
                        for f in range(f0, min(nf, f0 + 4)):
                            mm = nc.tensor.transpose(b[:, (f - f0) * P:(f - f0 + 1) * P],
                                                     self.osb[:, f * P:(f + 1) * P], ident)
                        mm.then_inc(pe_done, p.pe.step(f"{name} r {qt} {f0}"))

                n = len(units)
                for u in range(n + 3):
                    if u < n:
                        scores(u)
                    if 1 <= u <= n:
                        flip(u - 1)
                    if 2 <= u <= n + 1:
                        weigh(u - 2)
                    if u >= 3 and (u - 3) % H == H - 1:
                        turn((u - 3) // H)

            def dve_self(self, dve, name, hd):
                p = self.prog
                n = NT * H
                per_bank = min(H, BANK // hd)

                def maximum(u):
                    dve.wait_ge(pe_done, p.pe.at(f"{name} s {u}"))
                    if u >= 4:
                        dve.wait_ge(act_done, p.act.at(f"{name} exp {u - 4}"))
                    nc.vector.tensor_reduce(self.nm[:, u % 4:u % 4 + 1], self.full(f"{name} s {u}"), AX.X, ALU.max,
                                            negate=True).then_inc(dve_done, p.dve.step(f"{name} max {u}"))

                def flipped(u):
                    dve.wait_ge(pe_done, p.pe.at(f"{name} t {u}"))
                    if u >= 2:
                        dve.wait_ge(pe_done, p.pe.at(f"{name} w {u - 2}"))
                    nc.vector.tensor_copy(self.ptr[:, NT * (u % 2):NT * (u % 2) + NT, :],
                                          self.full(f"{name} t {u}").rearrange("p (k t) -> p k t", k=NT))\
                        .then_inc(dve_done, p.dve.step(f"{name} flipped {u}"))

                def finish(u):
                    qt, c = u // H, (u % H) // per_bank
                    job = f"{name} h {qt} {c}"
                    cols = slice(c * per_bank, (c + 1) * per_bank)
                    dve.wait_ge(act_done, p.act.at(f"{name} exp {u}"))
                    dve.wait_ge(dve_done, p.dve.n)
                    nc.vector.reciprocal(self.rih[:, qt % 2, cols], self.smh[:, qt % 2, cols])\
                        .then_inc(dve_done, p.dve.step())
                    dve.wait_ge(dve_done, p.dve.n)
                    dve.wait_ge(pe_done, p.pe.at(f"{name} w {u}"))
                    if qt:
                        dve.wait_ge(act_done, p.act.at(f"{name} turned {qt - 1} 0"))
                        if H * hd // P > 4:
                            dve.wait_ge(act_done, p.act.at(f"{name} turned {qt - 1} 4"))
                    nc.vector.tensor_tensor(
                        self.osb[:, c * per_bank * hd:(c + 1) * per_bank * hd].rearrange("p (h d) -> p h d", d=hd),
                        self.full(job)[:, 0:per_bank * hd].rearrange("p (h d) -> p h d", d=hd),
                        self.rih[:, qt % 2, cols].unsqueeze(2).to_broadcast([P, per_bank, hd]),
                        ALU.mult).then_inc(dve_done, p.dve.step(f"{job} out"))

                for u in range(n + 3):
                    if u < n:
                        maximum(u)
                    if 1 <= u <= n:
                        flipped(u - 1)
                    if u >= 2 and (u - 2) % per_bank == per_bank - 1:
                        finish(u - 2)

            def act_self(self, act, name, hd, dst, bias=None):
                p = self.prog
                n = NT * H
                nf = H * hd // P
                for u in range(n + 4):
                    if u < n:
                        qt, h = divmod(u, H)
                        act.wait_ge(dve_done, p.dve.at(f"{name} max {u}"))
                        if u >= 3:
                            act.wait_ge(pe_done, p.pe.at(f"{name} t {u - 3}"))
                        if h == 0 and qt >= 2:
                            act.wait_ge(dve_done, p.dve.at(f"{name} h {qt - 2} {H // min(H, BANK // hd) - 1} out"))
                        nc.scalar.activation(self.pr[:, u % 3, :], self.full(f"{name} s {u}"), ACT.Exp,
                                             bias=self.nm[:, u % 4:u % 4 + 1],
                                             accum_out=self.smh[:, qt % 2, h:h + 1])\
                            .then_inc(act_done, p.act.step(f"{name} exp {u}"))
                    if u >= 4 and (u - 4) % H == H - 1:
                        qt = (u - 4) // H
                        for f0 in range(0, nf, 4):
                            act.wait_ge(pe_done, p.pe.at(f"{name} r {qt} {f0}"))
                            w = min(4, nf - f0)
                            b = self.full(f"{name} r {qt} {f0}")
                            if bias is None:
                                nc.scalar.activation(dst[:, f0:f0 + w, qt * P:(qt + 1) * P],
                                                     b[:, 0:w * P].rearrange("p (f t) -> p f t", f=w), ACT.Copy)\
                                    .then_inc(act_done, p.act.step(f"{name} turned {qt} {f0}"))
                            else:
                                for f in range(w):
                                    nc.scalar.activation(dst[:, f0 + f, qt * P:(qt + 1) * P],
                                                         b[:, f * P:(f + 1) * P], ACT.Identity,
                                                         bias=bias[:, f0 + f:f0 + f + 1])\
                                        .then_inc(act_done, p.act.step(f"{name} turned {qt} {f0}" if f == w - 1 else None))

        with ExitStack() as mem:
            def sb(name, shape):
                return mem.enter_context(nc.sbuf_tensor(f"a_{name}", shape, F32))

            w0, w1a, w1b, v0 = sb("w0", [P, W0N]), sb("w1a", [P, W1AN]), sb("w1b", [P, W1BN]), sb("v0", [P, V0N])
            big = sb("big", [P, 3, 8, T])
            x = sb("x", [P, ND, T])
            cx = sb("ctx", [P, 2, P])
            ksb = sb("ksb", [P, 8, KEYS])
            p1 = sb("p1", [P, 2, KEYS])
            p2 = sb("p2", [P, 2, KEYS])
            st = Dense("a", sb)
            st.osb = sb("osb", [P, INNER])
            st.eps = sb("eps", [P, 1])
            st.pt = big[:, 1, :, :].rearrange("p (g h) t -> p g h t", g=2)
            pr = st.prog

            def mat(t, cols, name, k, n):
                return t[:, cols[name]:cols[name] + k * n].rearrange("p (k n) -> p k n", k=k)

            def vec(name, n=2):
                return v0[:, V0[name]:V0[name] + n]

            hid = big[:, 2, :, :]
            q1 = big[:, 0, :, :]
            k1 = big[:, 1, :, :]
            v1 = big[:, 2, :, :].rearrange("p (t a) c -> p t (a c)", t=NT)
            q0 = big[:, 0, 0:2, :]
            kbd0 = big[:, 0, 2:4, :]
            vbd0 = big[:, 0, 4:6, :].rearrange("p g (h m) -> p g h m", h=4)
            o0 = big[:, 0, 6:8, :]
            a0 = big[:, 1, 0:2, :]
            kbd1 = big[:, 2, 0:2, :].rearrange("p a (f m) -> p (a f) m", m=P)
            vbd1 = big[:, 2, 2:4, :].rearrange("p a (f m) -> p (a f) m", m=P)

            with nc.Block() as block:
                @block.sync
                def _(sp):
                    sp.dma_start(cst[:, :], cst_in).then_inc(const_loaded, 16)
                    sp.dma_start(v0[:, :], v0_in).then_inc(const_loaded, 16)
                    sp.dma_start(w0[:, :], w0_in).then_inc(w0_loaded, 16)
                    sp.dma_start(w1a[:, :], w1a_in).then_inc(w1a_loaded, 16)
                    sp.dma_start(w1b[:, :], w1b_in).then_inc(w1b_loaded, 16)

                @block.gpsimd
                def _(pool):
                    nc.gpsimd.memset(st.eps[:, :], EPS).then_inc(pool_done, 1)
                    pool.wait_ge(pool_done, 1)
            end_of_block()

            with nc.Fori(0, B) as b:
                with nc.Block() as block:
                    @block.sync
                    def _(sp):
                        sp.dma_start(x[:, :, :], x_in[b].rearrange("p (k t) -> p k t", k=ND)).then_inc(x_loaded, 16)
                        sp.dma_start(cx[:, :, :], ctx_in[b].rearrange("p (k t) -> p k t", k=2)).then_inc(x_loaded, 16)
                        h_out = hs[b].rearrange("p (k t) -> p k t", k=ND)
                        sp.wait_ge(act_done, pr.act.at("pre2 out"))
                        sp.dma_start(h_out[:, :, 0:KEYS], p2[:, :, :]).then_inc(x_stored, 16)
                        sp.wait_ge(dve_done, pr.dve.at("l1 down 1 out"))
                        sp.dma_start(h_out[:, :, KEYS:S2], x[:, :, :]).then_inc(x_stored, 16)
                        sp.wait_ge(x_stored, 32)

                    @block.tensor
                    def _(pe):
                        pe.wait_ge(const_loaded, 32)
                        pe.wait_ge(w0_loaded, 16)
                        pe.wait_ge(x_loaded, 32)
                        bk, emptied = st.lin.take("pre1", pr.act, "pre1 out")
                        if emptied:
                            pe.wait_ge(*emptied)
                        w = mat(w0, W0, "p1", 2, D)
                        for j in range(2):
                            for k in range(2):
                                mm = nc.tensor.matmul(bk[:, j * KEYS:(j + 1) * KEYS], w[:, k, j * P:(j + 1) * P],
                                                      cx[:, k, 0:KEYS], start=k == 0, stop=k == 1)
                        mm.then_inc(pe_done, pr.pe.step("pre1"))
                        bk, emptied = st.lin.take("k0", pr.act, "k0 out")
                        if emptied:
                            pe.wait_ge(*emptied)
                        w = mat(w0, W0, "k", 2, D)
                        for j in range(2):
                            for k in range(2):
                                mm = nc.tensor.matmul(bk[:, j * KEYS:(j + 1) * KEYS], w[:, k, j * P:(j + 1) * P],
                                                      cx[:, k, 0:KEYS], start=k == 0, stop=k == 1)
                        mm.then_inc(pe_done, pr.pe.step("k0"))
                        bk, emptied = st.lin.take("v0", pr.dve, "v0 out")
                        if emptied:
                            pe.wait_ge(*emptied)
                        w = mat(w0, W0, "v", 2, D)
                        for k in range(2):
                            mm = nc.tensor.matmul(bk[:, 0:D], cx[:, k, :], w[:, k, :], start=k == 0, stop=k == 1)
                        mm.then_inc(pe_done, pr.pe.step("v0"))
                        st.pe_linear(pe, "q0", mat(w0, W0, "q", 2, D), x, 2, range(2), pr.dve)
                        pe.wait_ge(act_done, pr.act.at("pre1 out"))
                        bk, emptied = st.lin.take("pre2", pr.act, "pre2 out")
                        if emptied:
                            pe.wait_ge(*emptied)
                        w = mat(w0, W0, "p2", 2, D)
                        for j in range(2):
                            for k in range(2):
                                mm = nc.tensor.matmul(bk[:, j * KEYS:(j + 1) * KEYS], w[:, k, j * P:(j + 1) * P],
                                                      p1[:, k, :], start=k == 0, stop=k == 1)
                        mm.then_inc(pe_done, pr.pe.step("pre2"))
                        pe.wait_ge(dve_done, pr.dve.at("q0 1 out"))
                        pe.wait_ge(dve_done, pr.dve.at("kbd0"))
                        st.pe_cross(pe, "x0", q0, kbd0, vbd0, False)
                        pe.wait_ge(dve_done, pr.dve.at("x0 o 1 out"))
                        st.pe_linear(pe, "o0", mat(w0, W0, "o", 2, D), o0, 2, range(2), pr.act)
                        st.pe_norm(pe, "n0", a0, (act_done, pr.act.at("o0 1 out")))
                        st.pe_mlp(pe, "l0", (dve_done, pr.dve.at("n0 out")), mat(w0, W0, "w1", 2, FF), mat(w0, W0, "w2", 8, D), hid)
                        st.pe_norm(pe, "n1", x, (dve_done, pr.dve.at("x0 sum")))
                        pe.wait_ge(w1a_loaded, 16)
                        pe.wait_ge(dve_done, pr.dve.at("n1 out"))
                        st.pe_linear(pe, "q1", mat(w1a, W1A, "q", 2, INNER), st.ln, 2, range(8), pr.act)
                        st.pe_linear(pe, "k1", mat(w1a, W1A, "k", 2, INNER), st.ln, 2, range(8), pr.act)
                        w = mat(w1a, W1A, "v", 2, INNER)
                        for t in range(NT):
                            for c in range(2):
                                bk, emptied = st.lin.take(f"v1 {t} {c}", pr.dve, f"v1 {t} {c} out")
                                if emptied:
                                    pe.wait_ge(*emptied)
                                for k in range(ND):
                                    mm = nc.tensor.matmul(bk, st.ln[:, k, t * P:(t + 1) * P], w[:, k, c * T:(c + 1) * T],
                                                          start=k == 0, stop=k == ND - 1)
                                mm.then_inc(pe_done, pr.pe.step(f"v1 {t} {c}"))
                        pe.wait_ge(act_done, pr.act.at("k1 7 out"))
                        pe.wait_ge(dve_done, pr.dve.at(f"v1 {NT - 1} 1 out"))

                        def keys_of(h):
                            rows = slice(64 * (h % 2), 64 * (h % 2) + 64)
                            return rows, h // 2, k1[rows, h // 2, :]
                        st.pe_self(pe, "s1", q1, keys_of, v1, 64)
                        pe.wait_ge(act_done, pr.act.at(f"s1 turned {NT - 1} 4"))
                        st.pe_linear(pe, "o1", mat(w1a, W1A, "o", 8, D), q1, 8, range(2), pr.dve)
                        pe.wait_ge(w1b_loaded, 16)
                        bk, emptied = st.lin.take("k2", pr.act, "k2 out")
                        if emptied:
                            pe.wait_ge(*emptied)
                        w = mat(w1b, W1B, "k", 2, INNER)
                        for j in range(8):
                            for k in range(2):
                                mm = nc.tensor.matmul(bk[:, j * KEYS:(j + 1) * KEYS], w[:, k, j * P:(j + 1) * P],
                                                      cx[:, k, 0:KEYS], start=k == 0, stop=k == 1)
                        mm.then_inc(pe_done, pr.pe.step("k2"))
                        st.pe_norm(pe, "n2", x, (dve_done, pr.dve.at("o1 1 out")))
                        w = mat(w1b, W1B, "v", 2, INNER)
                        for c in range(2):
                            bk, emptied = st.lin.take(f"v2 {c}", pr.dve, f"v2 {c} out")
                            if emptied:
                                pe.wait_ge(*emptied)
                            for k in range(2):
                                mm = nc.tensor.matmul(bk, cx[:, k, :], w[:, k, c * T:(c + 1) * T], start=k == 0, stop=k == 1)
                            mm.then_inc(pe_done, pr.pe.step(f"v2 {c}"))
                        pe.wait_ge(dve_done, pr.dve.at("n2 out"))
                        st.pe_linear(pe, "q2", mat(w1b, W1B, "q", 2, INNER), st.ln, 2, range(8), pr.act)
                        pe.wait_ge(act_done, pr.act.at("q2 7 out"))
                        pe.wait_ge(dve_done, pr.dve.at("v2 1 out"))
                        st.pe_cross(pe, "x2", q1, kbd1, vbd1, True)
                        pe.wait_ge(dve_done, pr.dve.at("x2 o 7 out"))
                        st.pe_linear(pe, "o2", mat(w1b, W1B, "o", 8, D), q1, 8, range(2), pr.dve)
                        st.pe_norm(pe, "n3", x, (dve_done, pr.dve.at("o2 1 out")))
                        pe.wait_ge(dve_done, pr.dve.at("n3 out"))
                        w = mat(w1b, W1B, "p", 2, 2 * FF)
                        for j in range(8):
                            st.pe_linear(pe, "l1 gate", w, st.ln, 2, [8 + j], pr.act)
                            st.pe_linear(pe, "l1 up", w, st.ln, 2, [j], pr.dve)
                        pe.wait_ge(dve_done, pr.dve.at("l1 up 7 out"))
                        st.pe_linear(pe, "l1 down", mat(w1b, W1B, "f", 8, D), hid, 8, range(2), pr.dve)

                    @block.scalar
                    def _(act):
                        act.wait_ge(const_loaded, 32)
                        act.wait_ge(pe_done, pr.pe.at("pre1"))
                        nc.scalar.activation(p1[:, :, :], st.full("pre1")[:, 0:2 * KEYS].rearrange("p (k t) -> p k t", k=2),
                                             ACT.Silu).then_inc(act_done, pr.act.step("pre1 out"))
                        act.wait_ge(pe_done, pr.pe.at("k0"))
                        for j in range(2):
                            nc.scalar.activation(ksb[:, j, :], st.full("k0")[:, j * KEYS:(j + 1) * KEYS], ACT.Identity,
                                                 bias=vec("k")[:, j:j + 1])\
                                .then_inc(act_done, pr.act.step("k0 out" if j else None))
                        act.wait_ge(pe_done, pr.pe.at("pre2"))
                        nc.scalar.activation(p2[:, :, :], st.full("pre2")[:, 0:2 * KEYS].rearrange("p (k t) -> p k t", k=2),
                                             ACT.Copy).then_inc(act_done, pr.act.step("pre2 out"))
                        st.act_cross(act, "x0")
                        for j in range(2):
                            act.wait_ge(pe_done, pr.pe.at(f"o0 {j}"))
                            nc.scalar.activation(a0[:, j, :], st.full(f"o0 {j}"), ACT.Identity, bias=vec("o")[:, j:j + 1])\
                                .then_inc(act_done, pr.act.step(f"o0 {j} out"))
                        st.act_norm(act, "n0")
                        st.act_mlp(act, "l0", vec("b1", 8), hid)
                        st.act_norm(act, "n1")
                        for j in range(8):
                            act.wait_ge(pe_done, pr.pe.at(f"q1 {j}"))
                            nc.scalar.activation(q1[:, j, :], st.full(f"q1 {j}"), ACT.Copy, scale=0.125)\
                                .then_inc(act_done, pr.act.step(f"q1 {j} out"))
                        for j in range(8):
                            act.wait_ge(pe_done, pr.pe.at(f"k1 {j}"))
                            nc.scalar.activation(k1[:, j, :], st.full(f"k1 {j}"), ACT.Copy)\
                                .then_inc(act_done, pr.act.step(f"k1 {j} out"))
                        st.act_self(act, "s1", 64, q1)
                        act.wait_ge(pe_done, pr.pe.at("k2"))
                        nc.scalar.activation(ksb[:, :, :], st.full("k2").rearrange("p (f k) -> p f k", f=8), ACT.Copy)\
                            .then_inc(act_done, pr.act.step("k2 out"))
                        st.act_norm(act, "n2")
                        for j in range(8):
                            act.wait_ge(pe_done, pr.pe.at(f"q2 {j}"))
                            nc.scalar.activation(q1[:, j, :], st.full(f"q2 {j}"), ACT.Copy, scale=0.125)\
                                .then_inc(act_done, pr.act.step(f"q2 {j} out"))
                        st.act_cross(act, "x2")
                        st.act_norm(act, "n3")
                        for j in range(8):
                            act.wait_ge(pe_done, pr.pe.at(f"l1 gate {8 + j}"))
                            if j >= 3:
                                act.wait_ge(dve_done, pr.dve.at(f"l1 up {j - 3} out"))
                            nc.scalar.activation(st.pr[:, j % 3, :], st.full(f"l1 gate {8 + j}"), ACT.Gelu,
                                                 bias=vec("p", 16)[:, 8 + j:9 + j])\
                                .then_inc(act_done, pr.act.step(f"l1 gate {8 + j} out"))

                    @block.vector
                    def _(dve):
                        dve.wait_ge(const_loaded, 32)
                        dve.wait_ge(pe_done, pr.pe.at("v0"))
                        for g in range(2):
                            for hp in range(4):
                                nc.vector.tensor_tensor(
                                    vbd0[:, g, hp, :].rearrange("p (h d) -> p h d", h=8),
                                    st.full("v0")[:, g * P:(g + 1) * P].rearrange("p (h d) -> p h d", h=8),
                                    cst[:, C_MV + 8 * hp:C_MV + 8 * hp + 8].unsqueeze(2).to_broadcast([P, 8, 16]),
                                    ALU.mult).then_inc(dve_done, pr.dve.step("v0 out" if (g, hp) == (1, 3) else None))
                        for j in range(2):
                            dve.wait_ge(pe_done, pr.pe.at(f"q0 {j}"))
                            nc.vector.tensor_scalar(q0[:, j, :], st.full(f"q0 {j}"), vec("q")[:, j:j + 1], 0.25,
                                                    ALU.add, ALU.mult).then_inc(dve_done, pr.dve.step(f"q0 {j} out"))
                        dve.wait_ge(act_done, pr.act.at("k0 out"))
                        for g in range(2):
                            nc.vector.tensor_tensor(
                                kbd0[:, g, :].rearrange("p (h k) -> p h k", h=8),
                                ksb[:, g, :].unsqueeze(1).to_broadcast([P, 8, KEYS]),
                                cst[:, C_MK:C_MK + 8].unsqueeze(2).to_broadcast([P, 8, KEYS]),
                                ALU.mult).then_inc(dve_done, pr.dve.step("kbd0" if g else None))
                        st.dve_cross(dve, "x0")
                        for g in range(2):
                            dve.wait_ge(pe_done, pr.pe.at(f"x0 o {g}"))
                            nc.vector.tensor_scalar(o0[:, g, :], st.full(f"x0 o {g}"), vec("v")[:, g:g + 1], None, ALU.add)\
                                .then_inc(dve_done, pr.dve.step(f"x0 o {g} out"))
                        st.dve_norm(dve, "n0", a0, vec("g"), vec("b"))
                        for j in range(2):
                            dve.wait_ge(dve_done, pr.dve.n)
                            dve.wait_ge(act_done, pr.act.at(f"o0 {j} out"))
                            nc.vector.tensor_tensor(x[:, j, :], x[:, j, :], a0[:, j, :], ALU.add)\
                                .then_inc(dve_done, pr.dve.step())
                        st.dve_residual(dve, "l0 down", x, vec("b2"))
                        pr.dve.names["x0 sum"] = pr.dve.n
                        st.dve_norm(dve, "n1", x, vec("g1"), vec("n1"))
                        for t in range(NT):
                            for c in range(2):
                                dve.wait_ge(pe_done, pr.pe.at(f"v1 {t} {c}"))
                                nc.vector.tensor_copy(v1[:, t, c * T:(c + 1) * T], st.full(f"v1 {t} {c}"))\
                                    .then_inc(dve_done, pr.dve.step(f"v1 {t} {c} out"))
                        st.dve_self(dve, "s1", 64)
                        st.dve_residual(dve, "o1", x, vec("o1"))
                        dve.wait_ge(act_done, pr.act.at("k2 out"))
                        nc.vector.tensor_tensor(
                            kbd1.rearrange("p f (h k) -> p f h k", h=2),
                            ksb[:, :, :].unsqueeze(2).to_broadcast([P, 8, 2, KEYS]),
                            cst[:, C_M64:C_M64 + 2].unsqueeze(1).unsqueeze(3).to_broadcast([P, 8, 2, KEYS]),
                            ALU.mult).then_inc(dve_done, pr.dve.step())
                        st.dve_norm(dve, "n2", x, vec("g2"), vec("n2"))
                        for c in range(2):
                            dve.wait_ge(pe_done, pr.pe.at(f"v2 {c}"))
                            nc.vector.tensor_tensor(
                                vbd1[:, 4 * c:4 * c + 4, :].rearrange("p f (h d) -> p f h d", h=2),
                                st.full(f"v2 {c}").rearrange("p (f h d) -> p f h d", h=2, d=64),
                                cst[:, C_M64:C_M64 + 2].unsqueeze(1).unsqueeze(3).to_broadcast([P, 4, 2, 64]),
                                ALU.mult).then_inc(dve_done, pr.dve.step(f"v2 {c} out"))
                        st.dve_cross(dve, "x2")
                        for f in range(8):
                            dve.wait_ge(pe_done, pr.pe.at(f"x2 o {f}"))
                            nc.vector.tensor_copy(q1[:, f, :], st.full(f"x2 o {f}"))\
                                .then_inc(dve_done, pr.dve.step(f"x2 o {f} out"))
                        st.dve_residual(dve, "o2", x, vec("o2"))
                        st.dve_norm(dve, "n3", x, vec("g3"), vec("n3"))
                        for j in range(8):
                            dve.wait_ge(act_done, pr.act.at(f"l1 gate {8 + j} out"))
                            dve.wait_ge(pe_done, pr.pe.at(f"l1 up {j}"))
                            nc.vector.scalar_tensor_tensor(hid[:, j, :], st.full(f"l1 up {j}"), vec("p", 16)[:, j:j + 1],
                                                           st.pr[:, j % 3, :], ALU.add, ALU.mult)\
                                .then_inc(dve_done, pr.dve.step(f"l1 up {j} out"))
                        st.dve_residual(dve, "l1 down", x, vec("f"))

                    @block.gpsimd
                    def _(pool):
                        st.pool_cross(pool, "x0")
                        st.pool_cross(pool, "x2")
                found["a"] = pr.result()
                end_of_block()

        with ExitStack() as mem:
            def sb(name, shape):
                return mem.enter_context(nc.sbuf_tensor(f"m_{name}", shape, F32))

            w2, v2 = sb("w2", [P, W2N]), sb("v2", [P, V2N])
            h = sb("h", [P, ND, S2])
            sq = sb("sq", [P, ND, S2])
            rs = sb("rs", [P, S2])
            xn = sb("xn", [P, ND, S2])
            xc = sb("xc", [P, NE, 3 + S2])
            cv = sb("cv", [P, NE, S2])
            xi = sb("xi", [P, NE, S2])
            zs = sb("zs", [P, NE, S2])
            dt = sb("dt", [P, NE, S2])
            dtr = sb("dtr", [DR, S2])
            bc = sb("bc", [P, len(TT), NX])
            sp1, sp2, sp3, sp4 = sb("sp1", [P, NE, S2]), sb("sp2", [P, 2, S2]), sb("sp3", [P, 2, S2]), sb("sp4", [P, 2, S2])
            ut = sb("ut", [P, len(TT), DI])
            ub = sb("ub", [P, 2, len(TT), DI])
            da = sb("da", [P, 8, S2])
            hh = sb("hh", [P, 2, NE, S2])
            yt = sb("yt", [P, len(TT), DI])
            am = sb("am", [P, NE * DS])
            eps2 = sb("eps", [P, 1])

            def mat2(name, k, n):
                return w2[:, W2[name]:W2[name] + k * n].rearrange("p (k n) -> p k n", k=k)

            def vec2(name, i):
                return v2[:, V2[name] + i:V2[name] + i + 1]

            HALVES = ((0, BANK), (BANK, S2))

            with nc.Block() as block:
                @block.gpsimd
                def _(pool):
                    nc.gpsimd.memset(eps2[:, :], EPS).then_inc(pool_done, 1)
                    nc.gpsimd.memset(xc[:, :, 0:3], 0.0).then_inc(pool_done, 1)
                    pool.wait_ge(pool_done, 2)
            end_of_block()

            with nc.Fori(0, L) as layer:
                with nc.Block() as block:
                    @block.sync
                    def _(sp):
                        sp.dma_start(v2[:, :], v2_in[layer]).then_inc(layer_loaded, 16)
                        sp.dma_start(w2[:, :], w2_in[layer]).then_inc(x_loaded, 16)
                        sp.wait_ge(x_loaded, 16)

                    @block.scalar
                    def _(act):
                        act.wait_ge(layer_loaded, 16)
                        nc.scalar.activation(am[:, :], v2[:, V2["A"]:V2["A"] + NE * DS], ACT.Exp)\
                            .then_inc(act_done, 1)

                    @block.vector
                    def _(dve):
                        dve.wait_ge(act_done, 1)
                        nc.vector.tensor_scalar(am[:, :], am[:, :], -1.0, None, ALU.mult).then_inc(dve_done, 1)
                        dve.wait_ge(dve_done, 1)
                nc.sync.sem_clear(layer_loaded)
                end_of_block()

                with nc.Fori(0, B) as b:
                    pr = Program(engine_sems, known.get("m", {}))
                    wring, tring = Ring(pr, wide, [0, 2, 4]), Ring(pr, bank, [6, 7])
                    full = lambda job: wide(pr.bank_of(job))

                    with nc.Block() as block:
                        @block.sync
                        def _(sp):
                            h_dram = hs[b].rearrange("p (k t) -> p k t", k=ND)
                            sp.dma_start(h[:, :, :], h_dram).then_inc(x_loaded, 16)
                            sp.wait_ge(dve_done, pr.dve.at("h 1"))
                            sp.dma_start(h_dram, h[:, :, :]).then_inc(x_stored, 16)
                            sp.wait_ge(x_stored, 16)

                        @block.tensor
                        def _(pe):
                            def product(job, of, emptied, pairs, m=P):
                                s, freed = wring.take(job, of, emptied)
                                if freed:
                                    pe.wait_ge(*freed)
                                for lo, hi in HALVES:
                                    for k, (lhs, rhs) in enumerate(pairs):
                                        mm = nc.tensor.matmul(s[0:m, lo:hi], lhs, rhs[:, lo:hi],
                                                              start=k == 0, stop=k == len(pairs) - 1)
                                mm.then_inc(pe_done, pr.pe.step(job))

                            pe.wait_ge(act_done, pr.act.at("squares"))
                            product("var", pr.act, "log", [(mean_w, sq[:, k, :]) for k in range(ND)])
                            pe.wait_ge(dve_done, pr.dve.at("xn"))
                            w = mat2("in", ND, 2 * DI)
                            for j in range(2 * NE):
                                product(f"in {j}", pr.act, f"in {j} out",
                                        [(w[:, k, j * P:(j + 1) * P], xn[:, k, :]) for k in range(ND)])
                            w = mat2("x", NE, NX)
                            pe.wait_ge(act_done, pr.act.at(f"xi {NE - 1}"))
                            product("dtr", pr.dve, "dtr out", [(w[:, e, 0:DR], xi[:, e, :]) for e in range(NE)], m=DR)
                            s, emptied = wring.take("bc", pr.dve, "bc out")
                            if emptied:
                                pe.wait_ge(*emptied)
                            for i, (t0, n) in enumerate(TT):
                                for e in range(NE):
                                    mm = nc.tensor.matmul(s[0:n, i * NX:(i + 1) * NX], xi[:, e, t0:t0 + n], w[:, e, :],
                                                          start=e == 0, stop=e == NE - 1)
                            mm.then_inc(pe_done, pr.pe.step("bc"))
                            pe.wait_ge(dve_done, pr.dve.at("dtr out"))
                            for e in range(NE):
                                product(f"dt {e}", pr.act, f"dt {e} in",
                                        [(w2[0:DR, W2["dt"] + e * P:W2["dt"] + (e + 1) * P], dtr[:, :])])
                            pe.wait_ge(dve_done, pr.dve.at(f"u {NE - 1}"))
                            for i, (t0, n) in enumerate(TT):
                                s, emptied = tring.take(f"ut {i}", pr.act, f"ut {i} out")
                                if emptied:
                                    pe.wait_ge(*emptied)
                                for e in range(NE):
                                    mm = nc.tensor.transpose(s[0:n, e * P:(e + 1) * P], cv[:, e, t0:t0 + n], ident)
                                mm.then_inc(pe_done, pr.pe.step(f"ut {i}"))

                            def inputs(n):
                                pe.wait_ge(pool_done, pr.pool.at(f"ub {n}"))
                                for e in range(NE):
                                    s, emptied = wring.take(f"db {n} {e}", pr.dve, f"scan {n} {e}")
                                    if emptied:
                                        pe.wait_ge(*emptied)
                                    for i, (t0, m) in enumerate(TT):
                                        mm = nc.tensor.transpose(s[:, t0:t0 + m],
                                                                 ub[0:m, n % 2, i, e * P:(e + 1) * P],
                                                                 ident[0:m, 0:m])
                                    mm.then_inc(pe_done, pr.pe.step(f"db {n} {e}"))

                            def outputs(n):
                                pe.wait_ge(dve_done, pr.dve.at(f"scan {n} {NE - 1}"))
                                for i, (t0, m) in enumerate(TT):
                                    s, emptied = tring.take(f"ht {n} {i}", pr.dve, f"y {n} {i}")
                                    if emptied:
                                        pe.wait_ge(*emptied)
                                    for e in range(NE):
                                        mm = nc.tensor.transpose(s[0:m, e * P:(e + 1) * P],
                                                                 hh[:, n % 2, e, t0:t0 + m], ident)
                                    mm.then_inc(pe_done, pr.pe.step(f"ht {n} {i}"))

                            for n in range(DS + 1):
                                if n < DS:
                                    inputs(n)
                                if n:
                                    outputs(n - 1)
                            pe.wait_ge(dve_done, pr.dve.at(f"y {DS - 1} {len(TT) - 1}"))
                            for e in range(NE):
                                s, emptied = wring.take(f"yf {e}", pr.dve, f"yd {e}")
                                if emptied:
                                    pe.wait_ge(*emptied)
                                for i, (t0, m) in enumerate(TT):
                                    mm = nc.tensor.transpose(s[:, t0:t0 + m], yt[0:m, i, e * P:(e + 1) * P],
                                                             ident[0:m, 0:m])
                                mm.then_inc(pe_done, pr.pe.step(f"yf {e}"))
                            pe.wait_ge(dve_done, pr.dve.at(f"yg {NE - 1}"))
                            w = mat2("out", NE, D)
                            for j in range(ND):
                                product(f"out {j}", pr.dve, f"h {j}",
                                        [(w[:, e, j * P:(j + 1) * P], cv[:, e, :]) for e in range(NE)])

                        @block.scalar
                        def _(act):
                            act.wait_ge(x_loaded, 16)
                            for k in range(ND):
                                nc.scalar.activation(sq[:, k, :], h[:, k, :], ACT.Square)\
                                    .then_inc(act_done, pr.act.step("squares" if k else None))
                            act.wait_ge(pe_done, pr.pe.at("var"))
                            nc.scalar.activation(rs[:, :], full("var"), ACT.Ln, bias=eps2[:, 0:1])\
                                .then_inc(act_done, pr.act.step("log"))
                            act.wait_ge(act_done, pr.act.n)
                            nc.scalar.activation(rs[:, :], rs[:, :], ACT.Exp, scale=-0.5)\
                                .then_inc(act_done, pr.act.step("rstd"))
                            for e in range(NE):
                                act.wait_ge(pe_done, pr.pe.at(f"in {e}"))
                                nc.scalar.activation(xc[:, e, 3:3 + S2], full(f"in {e}"), ACT.Copy)\
                                    .then_inc(act_done, pr.act.step(f"in {e} out"))
                                act.wait_ge(act_done, pr.act.n)
                                nc.scalar.activation(cv[:, e, :], xc[:, e, 0:S2], ACT.Identity,
                                                     bias=vec2("cb", e), scale=vec2("cw", 4 * e))\
                                    .then_inc(act_done, pr.act.step(f"tap {e}"))
                            for e in range(NE):
                                act.wait_ge(pe_done, pr.pe.at(f"in {NE + e}"))
                                nc.scalar.activation(zs[:, e, :], full(f"in {NE + e}"), ACT.Silu)\
                                    .then_inc(act_done, pr.act.step(f"in {NE + e} out"))
                            for e in range(NE):
                                act.wait_ge(dve_done, pr.dve.at(f"conv {e}"))
                                nc.scalar.activation(xi[:, e, :], cv[:, e, :], ACT.Silu)\
                                    .then_inc(act_done, pr.act.step(f"xi {e}"))
                            for e in range(NE):
                                act.wait_ge(pe_done, pr.pe.at(f"dt {e}"))
                                nc.scalar.activation(sp1[:, e, :], full(f"dt {e}"), ACT.Identity, bias=vec2("dtb", e))\
                                    .then_inc(act_done, pr.act.step(f"dt {e} in"))
                            for e in range(NE):
                                k = e % 2
                                act.wait_ge(pool_done, pr.pool.at(f"clamp {e}"))
                                nc.scalar.activation(sp2[:, k, :], sp2[:, k, :], ACT.Exp)\
                                    .then_inc(act_done, pr.act.step())
                                act.wait_ge(act_done, pr.act.n)
                                nc.scalar.activation(dt[:, e, :], sp2[:, k, :], ACT.Ln, bias=1.0)\
                                    .then_inc(act_done, pr.act.step())
                                if e >= 2:
                                    act.wait_ge(dve_done, pr.dve.at(f"max {e - 2}"))
                                nc.scalar.activation(sp3[:, k, :], sp2[:, k, :], ACT.Square, scale=0.5 ** 0.5)\
                                    .then_inc(act_done, pr.act.step(f"log1p {e}"))
                            for i, (t0, n) in enumerate(TT):
                                act.wait_ge(pe_done, pr.pe.at(f"ut {i}"))
                                nc.scalar.activation(ut[0:n, i, :], bank(pr.bank_of(f"ut {i}"))[0:n, :],
                                                     ACT.Copy).then_inc(act_done, pr.act.step(f"ut {i} out"))
                            for n in range(DS):
                                for e in range(NE):
                                    u = NE * n + e
                                    if u >= 8:
                                        act.wait_ge(dve_done, pr.dve.at(f"scan {(u - 8) // NE} {e}"))
                                    nc.scalar.activation(da[:, u % 8, :], dt[:, e, :], ACT.Exp,
                                                         scale=am[:, e * DS + n:e * DS + n + 1])\
                                        .then_inc(act_done, pr.act.step(f"da {n} {e}"))

                        @block.vector
                        def _(dve):
                            dve.wait_ge(act_done, pr.act.at("rstd"))
                            for k in range(ND):
                                nc.vector.scalar_tensor_tensor(xn[:, k, :], h[:, k, :], vec2("norm", k), rs[:, :],
                                                               ALU.mult, ALU.mult)\
                                    .then_inc(dve_done, pr.dve.step("xn" if k else None))
                            for e in range(NE):
                                dve.wait_ge(act_done, pr.act.at(f"tap {e}"))
                                for t in range(1, 4):
                                    dve.wait_ge(dve_done, pr.dve.n)
                                    nc.vector.scalar_tensor_tensor(cv[:, e, :], xc[:, e, t:t + S2],
                                                                   vec2("cw", 4 * e + t), cv[:, e, :],
                                                                   ALU.mult, ALU.add)\
                                        .then_inc(dve_done, pr.dve.step(f"conv {e}" if t == 3 else None))
                            dve.wait_ge(pe_done, pr.pe.at("dtr"))
                            nc.vector.tensor_copy(dtr[:, :], full("dtr")[0:DR, :])\
                                .then_inc(dve_done, pr.dve.step("dtr out"))
                            dve.wait_ge(pe_done, pr.pe.at("bc"))
                            whole = T // P
                            nc.vector.tensor_copy(bc[:, 0:whole, :],
                                                  full("bc")[:, 0:whole * NX].rearrange("p (i c) -> p i c", i=whole))\
                                .then_inc(dve_done, pr.dve.step())
                            nc.vector.tensor_copy(bc[0:KEYS, whole, :],
                                                  full("bc")[0:KEYS, whole * NX:(whole + 1) * NX])\
                                .then_inc(dve_done, pr.dve.step("bc out"))
                            for e in range(NE):
                                dve.wait_ge(pool_done, pr.pool.at(f"lower {e}"))
                                nc.vector.scalar_tensor_tensor(sp4[:, e % 2, :], sp4[:, e % 2, :], 2.0 / 3.0,
                                                               sp3[:, e % 2, :], ALU.mult, ALU.add)\
                                    .then_inc(dve_done, pr.dve.step())
                                nc.vector.tensor_tensor(dt[:, e, :], dt[:, e, :], sp3[:, e % 2, :], ALU.max)\
                                    .then_inc(dve_done, pr.dve.step())
                                dve.wait_ge(dve_done, pr.dve.n)
                                nc.vector.tensor_tensor(dt[:, e, :], dt[:, e, :], sp4[:, e % 2, :], ALU.min)\
                                    .then_inc(dve_done, pr.dve.step(f"max {e}"))
                                dve.wait_ge(dve_done, pr.dve.n)
                                nc.vector.tensor_tensor(dt[:, e, :], dt[:, e, :], sp1[:, e, :], ALU.max)\
                                    .then_inc(dve_done, pr.dve.step(f"dt {e}"))
                                dve.wait_ge(dve_done, pr.dve.n)
                                nc.vector.tensor_tensor(cv[:, e, :], dt[:, e, :], xi[:, e, :], ALU.mult)\
                                    .then_inc(dve_done, pr.dve.step(f"u {e}"))

                            def scans(n):
                                for e in range(NE):
                                    dve.wait_ge(act_done, pr.act.at(f"da {n} {e}"))
                                    dve.wait_ge(pe_done, pr.pe.at(f"db {n} {e}"))
                                    if n >= 2:
                                        dve.wait_ge(pe_done, pr.pe.at(f"ht {n - 2} {len(TT) - 1}"))
                                    nc.vector.tensor_tensor_scan(hh[:, n % 2, e, :], da[:, (NE * n + e) % 8, :],
                                                                 full(f"db {n} {e}"), 0.0, ALU.mult, ALU.add)\
                                        .then_inc(dve_done, pr.dve.step(f"scan {n} {e}"))

                            def sums(n):
                                for i, (t0, m) in enumerate(TT):
                                    dve.wait_ge(pe_done, pr.pe.at(f"ht {n} {i}"))
                                    s = bank(pr.bank_of(f"ht {n} {i}"))[0:m, :]
                                    c = bc[0:m, i, DR + DS + n:DR + DS + n + 1]
                                    if n == 0:
                                        nc.vector.tensor_scalar(yt[0:m, i, :], s, c, None, ALU.mult)\
                                            .then_inc(dve_done, pr.dve.step(f"y {n} {i}"))
                                    else:
                                        dve.wait_ge(dve_done, pr.dve.at(f"y {n - 1} {i}"))
                                        nc.vector.scalar_tensor_tensor(yt[0:m, i, :], s, c, yt[0:m, i, :],
                                                                       ALU.mult, ALU.add)\
                                            .then_inc(dve_done, pr.dve.step(f"y {n} {i}"))

                            for n in range(DS + 1):
                                if n < DS:
                                    scans(n)
                                if n:
                                    sums(n - 1)
                            for e in range(NE):
                                dve.wait_ge(pe_done, pr.pe.at(f"yf {e}"))
                                nc.vector.scalar_tensor_tensor(cv[:, e, :], xi[:, e, :], vec2("D", e),
                                                               full(f"yf {e}"), ALU.mult, ALU.add)\
                                    .then_inc(dve_done, pr.dve.step(f"yd {e}"))
                                dve.wait_ge(dve_done, pr.dve.n)
                                nc.vector.tensor_tensor(cv[:, e, :], cv[:, e, :], zs[:, e, :], ALU.mult)\
                                    .then_inc(dve_done, pr.dve.step(f"yg {e}"))
                            for j in range(ND):
                                dve.wait_ge(pe_done, pr.pe.at(f"out {j}"))
                                nc.vector.tensor_tensor(h[:, j, :], h[:, j, :], full(f"out {j}"), ALU.add)\
                                    .then_inc(dve_done, pr.dve.step(f"h {j}"))

                        @block.gpsimd
                        def _(pool):
                            def clamp(e):
                                pool.wait_ge(act_done, pr.act.at(f"dt {e} in"))
                                if e >= 2:
                                    pool.wait_ge(act_done, pr.act.at(f"log1p {e - 2}"))
                                    pool.wait_ge(pool_done, pr.pool.n)
                                nc.gpsimd.tensor_scalar(sp2[:, e % 2, :], sp1[:, e, :], SOFTPLUS_LINEAR, None, ALU.min)\
                                    .then_inc(pool_done, pr.pool.step(f"clamp {e}"))

                            def lower(e):
                                pool.wait_ge(act_done, pr.act.at(f"log1p {e}"))
                                if e >= 2:
                                    pool.wait_ge(dve_done, pr.dve.at(f"max {e - 2}"))
                                nc.gpsimd.tensor_tensor(sp4[:, e % 2, :], sp2[:, e % 2, :], sp3[:, e % 2, :],
                                                        ALU.mult).then_inc(pool_done, pr.pool.step())
                                pool.wait_ge(pool_done, pr.pool.n)
                                nc.gpsimd.tensor_tensor(sp3[:, e % 2, :], sp2[:, e % 2, :], sp3[:, e % 2, :],
                                                        ALU.subtract).then_inc(pool_done, pr.pool.step(f"lower {e}"))

                            clamp(0)
                            clamp(1)
                            for e in range(NE):
                                lower(e)
                                if e + 2 < NE:
                                    clamp(e + 2)
                            for n in range(DS):
                                if n >= 2:
                                    pool.wait_ge(pe_done, pr.pe.at(f"db {n - 2} {NE - 1}"))
                                for i, (t0, m) in enumerate(TT):
                                    pool.wait_ge(act_done, pr.act.at(f"ut {i} out"))
                                    nc.gpsimd.tensor_scalar(ub[0:m, n % 2, i, :], ut[0:m, i, :],
                                                            bc[0:m, i, DR + n:DR + n + 1], 1.0, ALU.mult, ALU.mult)\
                                        .then_inc(pool_done,
                                                  pr.pool.step(f"ub {n}" if i == len(TT) - 1 else None))
                    found["m"] = pr.result()
                    end_of_block()

        with ExitStack() as mem:
            def sb(name, shape):
                return mem.enter_context(nc.sbuf_tensor(f"c_{name}", shape, F32))

            w3, v3 = sb("w3", [P, W3N]), sb("v3", [P, V3N])
            x = sb("x", [P, ND, T])
            cx = sb("ctx", [P, 2, P])
            ksb = sb("ksb", [P, 2, KEYS])
            hid = sb("hid", [P, 8, T])
            q3 = sb("q3", [P, ND, T])
            k3 = sb("k3", [P, 2, ND, T])
            v3s = sb("v3s", [P, NT, D])
            o3 = sb("o3", [P, ND, T])
            kbd3 = sb("kbd3", [P, 2, T])
            vbd3 = sb("vbd3", [P, 2, 4, P])
            st = Dense("c", sb)
            st.pt = sb("pt", [P, 2, 4, T])
            st.osb = sb("osb", [P, D])
            st.eps = sb("eps", [P, 1])
            pr = st.prog

            def mat3(name, k=2, n=D):
                return w3[:, W3[name]:W3[name] + k * n].rearrange("p (k n) -> p k n", k=k)

            def vec3(name, n=2):
                return v3[:, V3[name]:V3[name] + n]

            with nc.Block() as block:
                @block.sync
                def _(sp):
                    sp.dma_start(v3[:, :], v3_in).then_inc(w3_loaded, 16)
                    sp.dma_start(w3[:, :], w3_in).then_inc(w3_loaded, 16)

                @block.gpsimd
                def _(pool):
                    nc.gpsimd.memset(st.eps[:, :], EPS).then_inc(pool_done, 1)
                    pool.wait_ge(pool_done, 1)
            end_of_block()

            with nc.Fori(0, B) as b:
                with nc.Block() as block:
                    @block.sync
                    def _(sp):
                        sp.dma_start(x[:, :, :], hs[b].rearrange("p (k t) -> p k t", k=ND)[:, :, KEYS:S2])\
                            .then_inc(x_loaded, 16)
                        sp.dma_start(cx[:, :, :], ctx_in[b].rearrange("p (k t) -> p k t", k=2)).then_inc(x_loaded, 16)
                        sp.wait_ge(dve_done, pr.dve.at("l3 down 1 out"))
                        sp.dma_start(out[b].rearrange("p (k t) -> p k t", k=ND), x[:, :, :]).then_inc(x_stored, 16)
                        sp.wait_ge(x_stored, 16)

                    @block.tensor
                    def _(pe):
                        pe.wait_ge(w3_loaded, 32)
                        pe.wait_ge(x_loaded, 32)
                        st.pe_norm(pe, "nf", None, None, rms=True)
                        bk, emptied = st.lin.take("k4", pr.act, "k4 out")
                        if emptied:
                            pe.wait_ge(*emptied)
                        w = mat3("ck")
                        for j in range(2):
                            for k in range(2):
                                mm = nc.tensor.matmul(bk[:, j * KEYS:(j + 1) * KEYS], w[:, k, j * P:(j + 1) * P],
                                                      cx[:, k, 0:KEYS], start=k == 0, stop=k == 1)
                        mm.then_inc(pe_done, pr.pe.step("k4"))
                        st.pe_norm(pe, "n4", x, (dve_done, pr.dve.at("final norm")))
                        bk, emptied = st.lin.take("v4", pr.dve, "v4 out")
                        if emptied:
                            pe.wait_ge(*emptied)
                        w = mat3("cv")
                        for k in range(2):
                            mm = nc.tensor.matmul(bk[:, 0:D], cx[:, k, :], w[:, k, :], start=k == 0, stop=k == 1)
                        mm.then_inc(pe_done, pr.pe.step("v4"))
                        pe.wait_ge(dve_done, pr.dve.at("n4 out"))
                        st.pe_linear(pe, "q3", mat3("sq"), st.ln, 2, range(2), pr.dve)
                        st.pe_linear(pe, "k3", mat3("sk"), st.ln, 2, range(2), pr.dve)
                        w = mat3("sv")
                        for t in range(NT):
                            bk, emptied = st.lin.take(f"v3 {t}", pr.act, f"v3 {t} out")
                            if emptied:
                                pe.wait_ge(*emptied)
                            for k in range(ND):
                                mm = nc.tensor.matmul(bk[:, 0:D], st.ln[:, k, t * P:(t + 1) * P], w[:, k, :],
                                                      start=k == 0, stop=k == ND - 1)
                            mm.then_inc(pe_done, pr.pe.step(f"v3 {t}"))
                        pe.wait_ge(dve_done, pr.dve.at("k3 1 out"))
                        pe.wait_ge(act_done, pr.act.at(f"v3 {NT - 1} out"))

                        def keys_of(h):
                            rows = slice(32 * (h % 8 // 2), 32 * (h % 8 // 2) + 32)
                            return rows, h // 8, k3[rows, h % 2, h // 8, :]
                        st.pe_self(pe, "s3", q3, keys_of, v3s, 16)
                        pe.wait_ge(act_done, pr.act.at(f"s3 turned {NT - 1} 0"))
                        st.pe_linear(pe, "o3", mat3("so"), o3, 2, range(2), pr.dve)
                        st.pe_norm(pe, "n5", x, (dve_done, pr.dve.at("o3 1 out")))
                        pe.wait_ge(dve_done, pr.dve.at("n5 out"))
                        st.pe_linear(pe, "q4", mat3("cq"), st.ln, 2, range(2), pr.dve)
                        pe.wait_ge(dve_done, pr.dve.at("q4 1 out"))
                        st.pe_cross(pe, "x3", q3, kbd3, vbd3, False)
                        pe.wait_ge(dve_done, pr.dve.at("x3 o 1 out"))
                        st.pe_linear(pe, "o4", mat3("co"), o3, 2, range(2), pr.dve)
                        st.pe_norm(pe, "n6", x, (dve_done, pr.dve.at("o4 1 out")))
                        st.pe_mlp(pe, "l3", (dve_done, pr.dve.at("n6 out")), mat3("w1", 2, FF), mat3("w2", 8, D), hid)

                    @block.scalar
                    def _(act):
                        act.wait_ge(w3_loaded, 32)
                        act.wait_ge(x_loaded, 32)
                        st.act_norm(act, "nf", x)
                        act.wait_ge(pe_done, pr.pe.at("k4"))
                        for j in range(2):
                            nc.scalar.activation(ksb[:, j, :], st.full("k4")[:, j * KEYS:(j + 1) * KEYS], ACT.Identity,
                                                 bias=vec3("ck")[:, j:j + 1])\
                                .then_inc(act_done, pr.act.step("k4 out" if j else None))
                        st.act_norm(act, "n4")
                        for t in range(NT):
                            act.wait_ge(pe_done, pr.pe.at(f"v3 {t}"))
                            nc.scalar.activation(v3s[:, t, :], st.full(f"v3 {t}")[:, 0:D], ACT.Copy)\
                                .then_inc(act_done, pr.act.step(f"v3 {t} out"))
                        st.act_self(act, "s3", 16, o3, vec3("sv"))
                        st.act_norm(act, "n5")
                        st.act_cross(act, "x3")
                        st.act_norm(act, "n6")
                        st.act_mlp(act, "l3", vec3("b1", 8), hid)

                    @block.vector
                    def _(dve):
                        dve.wait_ge(act_done, pr.act.at("nf rstd"))
                        for k in range(ND):
                            nc.vector.scalar_tensor_tensor(x[:, k, :], x[:, k, :], vec3("fin")[:, k:k + 1],
                                                           st.rs[:, :], ALU.mult, ALU.mult)\
                                .then_inc(dve_done, pr.dve.step("final norm" if k else None))
                        st.dve_norm(dve, "n4", x, vec3("g1"), vec3("n1"))
                        dve.wait_ge(pe_done, pr.pe.at("v4"))
                        for g in range(2):
                            for hp in range(4):
                                nc.vector.tensor_tensor(
                                    vbd3[:, g, hp, :].rearrange("p (h d) -> p h d", h=8),
                                    st.full("v4")[:, g * P:(g + 1) * P].rearrange("p (h d) -> p h d", h=8),
                                    cst[:, C_MV + 8 * hp:C_MV + 8 * hp + 8].unsqueeze(2).to_broadcast([P, 8, 16]),
                                    ALU.mult).then_inc(dve_done, pr.dve.step("v4 out" if (g, hp) == (1, 3) else None))
                        for j in range(2):
                            dve.wait_ge(pe_done, pr.pe.at(f"q3 {j}"))
                            nc.vector.tensor_scalar(q3[:, j, :], st.full(f"q3 {j}"), vec3("sq")[:, j:j + 1], 0.25,
                                                    ALU.add, ALU.mult).then_inc(dve_done, pr.dve.step(f"q3 {j} out"))
                        for j in range(2):
                            dve.wait_ge(pe_done, pr.pe.at(f"k3 {j}"))
                            for odd in range(2):
                                nc.vector.tensor_scalar(k3[:, odd, j, :], st.full(f"k3 {j}"), vec3("sk")[:, j:j + 1],
                                                        cst[:, C_PAR + odd:C_PAR + odd + 1], ALU.add, ALU.mult)\
                                    .then_inc(dve_done, pr.dve.step(f"k3 {j} out" if odd else None))
                        dve.wait_ge(act_done, pr.act.at("k4 out"))
                        for g in range(2):
                            nc.vector.tensor_tensor(
                                kbd3[:, g, :].rearrange("p (h k) -> p h k", h=8),
                                ksb[:, g, :].unsqueeze(1).to_broadcast([P, 8, KEYS]),
                                cst[:, C_MK:C_MK + 8].unsqueeze(2).to_broadcast([P, 8, KEYS]),
                                ALU.mult).then_inc(dve_done, pr.dve.step())
                        st.dve_self(dve, "s3", 16)
                        st.dve_residual(dve, "o3", x, vec3("so"))
                        st.dve_norm(dve, "n5", x, vec3("g2"), vec3("n2"))
                        for j in range(2):
                            dve.wait_ge(pe_done, pr.pe.at(f"q4 {j}"))
                            nc.vector.tensor_scalar(q3[:, j, :], st.full(f"q4 {j}"), vec3("cq")[:, j:j + 1], 0.25,
                                                    ALU.add, ALU.mult).then_inc(dve_done, pr.dve.step(f"q4 {j} out"))
                        st.dve_cross(dve, "x3")
                        for g in range(2):
                            dve.wait_ge(pe_done, pr.pe.at(f"x3 o {g}"))
                            nc.vector.tensor_scalar(o3[:, g, :], st.full(f"x3 o {g}"), vec3("cv")[:, g:g + 1], None,
                                                    ALU.add).then_inc(dve_done, pr.dve.step(f"x3 o {g} out"))
                        st.dve_residual(dve, "o4", x, vec3("co"))
                        st.dve_norm(dve, "n6", x, vec3("g3"), vec3("n3"))
                        st.dve_residual(dve, "l3 down", x, vec3("b2"))

                    @block.gpsimd
                    def _(pool):
                        st.pool_cross(pool, "x3")
                found["c"] = pr.result()
                end_of_block()
        return found


def _rows(a, k):
    K, N = a.shape
    if K < k * P:
        a = np.concatenate([a, np.zeros((k * P - K, N), a.dtype)])
    return np.ascontiguousarray(a.reshape(k, P, N).transpose(1, 0, 2).reshape(P, k * N))


def _cols(v):
    return np.ascontiguousarray(v.reshape(-1, P).T)


def _arrays(i):
    g = {k: np.asarray(v) for k, v in i.items()}
    l0 = lambda n: g["L0_xattn_" + n]
    l1 = lambda n: g["L1_xattn_" + n]
    l2 = lambda n: g["L2_xattn_" + n]
    l3 = lambda n: g["L3_xattn_" + n]
    cat = lambda parts: np.ascontiguousarray(np.concatenate(parts, 1))
    p = np.arange(P)[:, None]
    cst = np.concatenate([
        np.eye(P), np.full((P, P), 1.0 / D), p // 16 == np.arange(8)[None],
        (np.arange(8)[None, None] == 2 * np.arange(4)[None, :, None] + (p // 64)[:, :, None]).reshape(P, 32),
        p // 64 == np.arange(2)[None], (p // 16) % 2 == np.arange(2)[None]], 1).astype(np.float32)
    ctx_t = g["ctx_768"].transpose(0, 2, 1)
    ctx = np.stack([_rows(np.concatenate([c, c], 1), 2) for c in ctx_t])
    per_layer = range(L)
    return {
        "x_in": np.stack([_rows(a.T, 2) for a in g["x"]]),
        "ctx_in": ctx,
        "cst_in": cst,
        "w0_in": cat([_rows(l0("Wq"), 2), _rows(l0("Wk"), 2), _rows(l0("Wv"), 2), _rows(l2("pre_w1"), 2),
                      _rows(l2("pre_w2"), 2), _rows(l0("Wo"), 2), _rows(l0("W1"), 2), _rows(l0("W2"), 8)]),
        "w1a_in": cat([_rows(l1("Wq1"), 2), _rows(l1("Wk1"), 2), _rows(l1("Wv1"), 2), _rows(l1("Wo1"), 8)]),
        "w1b_in": cat([_rows(l1("Wq2"), 2), _rows(l1("Wk2"), 2), _rows(l1("Wv2"), 2), _rows(l1("Wo2"), 8),
                       _rows(l1("Wp"), 2), _rows(l1("Wf"), 8)]),
        "v0_in": cat([_cols(l0(n)) for n in ("bq", "bk", "bv", "bo", "ln_g", "ln_b", "b1", "b2")]
                     + [_cols(l1(n)) for n in ("g1", "b1", "bo1", "g2", "b2", "bo2", "g3", "b3", "bp", "bf")]),
        "w2_in": np.stack([cat([_rows(l2("in_proj_w")[n].T, 2), _rows(l2("x_proj_w")[n].T, NE),
                                _rows(l2("out_proj_w")[n].T, NE), _rows(l2("dt_proj_w")[n].T, 1)])
                           for n in per_layer]),
        "v2_in": np.stack([cat([_cols(l2("norm_w")[n]), _rows(l2("conv_w")[n], NE), _cols(l2("conv_b")[n]),
                                _cols(l2("dt_proj_b")[n]), _cols(l2("D_param")[n]), _rows(l2("A_log")[n], NE)])
                           for n in per_layer]),
        "w3_in": cat([_rows(l3(n).T, 2) for n in ("sa_wq", "sa_wk", "sa_wv", "sa_wo", "ca_wq", "ca_wk", "ca_wv",
                                                  "ca_wo", "mlp_w1")] + [_rows(l3("mlp_w2").T, 8)]),
        "v3_in": cat([_cols(l2("final_norm_w"))] + [_cols(l3(n)) for n in (
            "ln1_g", "ln1_b", "ln2_g", "ln2_b", "ln3_g", "ln3_b", "sa_bq", "sa_bk", "sa_bv", "sa_bo",
            "ca_bq", "ca_bk", "ca_bv", "ca_bo", "mlp_b1", "mlp_b2")]),
    }


def kernel(**inputs):
    import concourse.bacc as _bacc
    from concourse.bass_utils import run_bass_kernel_spmd as _run

    arrays = _arrays(inputs)
    known = {}
    for _ in range(2):
        nc = _bacc.Bacc("TRN2", target_bir_lowering=False, num_devices=1)
        args = {n: nc.dram_tensor(n, a.shape, F32, kind="ExternalInput").ap() for n, a in arrays.items()}
        out = nc.dram_tensor("y_out", (B, P, ND * T), F32, kind="ExternalOutput").ap()
        known = build(nc, known, out=out, **args)
    r = _run(nc, [arrays], core_ids=[0])
    y = r.results[0]["y_out"].reshape(B, P, ND, T)
    return np.ascontiguousarray(y.transpose(0, 3, 2, 1).reshape(B, T, D))
```

```python
import numpy as np
from contextlib import ExitStack
import concourse.bass as bass
from concourse import mybir

F32 = mybir.dt.float32
ALU = mybir.AluOpType
ACT = mybir.ActivationFunctionType
AX = mybir.AxisListType

P = 128
B = 4
T = 512
D = 256
H = 16
KEYS = 64
CTX = 192
INNER = 1024
FF = 1024
NT = T // P
ND = D // P
EPS = 1e-5
L = 4
DI = 512
NE = DI // P
DS = 16
DR = 16
S2 = KEYS + T
NX = DR + 2 * DS
BANK = 512
TT = [(s, min(P, S2 - s)) for s in range(0, S2, P)]
SOFTPLUS_LINEAR = 20.0

C_IDENT, C_MEAN = 0, P
C_MK = 2 * P
C_MV = C_MK + 8
C_M64 = C_MV + 32
C_PAR = C_M64 + 2
C_END = C_PAR + 2


def columns(*parts):
    at, out = 0, {}
    for name, n in parts:
        out[name] = at
        at += n
    return out, at


W0, W0N = columns(("q", 2 * D), ("k", 2 * D), ("v", 2 * D), ("p1", 2 * D), ("p2", 2 * D),
                  ("o", 2 * D), ("w1", 2 * FF), ("w2", 8 * D))
W1A, W1AN = columns(("q", 2 * INNER), ("k", 2 * INNER), ("v", 2 * INNER), ("o", 8 * D))
W1B, W1BN = columns(("q", 2 * INNER), ("k", 2 * INNER), ("v", 2 * INNER), ("o", 8 * D),
                    ("p", 4 * FF), ("f", 8 * D))
W2, W2N = columns(("in", 2 * 2 * DI), ("x", NE * NX), ("dt", DI), ("out", NE * D))
W2A = W2["out"]
W3, W3N = columns(("sq", 2 * D), ("sk", 2 * D), ("sv", 2 * D), ("so", 2 * D),
                  ("cq", 2 * D), ("ck", 2 * D), ("cv", 2 * D), ("co", 2 * D),
                  ("w1", 2 * FF), ("w2", 8 * D))
V0, V0N = columns(("q", 2), ("k", 2), ("v", 2), ("o", 2), ("g", 2), ("b", 2), ("b1", 8), ("b2", 2),
                  ("g1", 2), ("n1", 2), ("o1", 2), ("g2", 2), ("n2", 2), ("o2", 2), ("g3", 2), ("n3", 2),
                  ("p", 16), ("f", 2))
V2, V2N = columns(("norm", 2), ("cw", NE * 4), ("cb", NE), ("dtb", NE), ("D", NE), ("A", NE * DS))
V2A = V2["D"]
V3, V3N = columns(("fin", 2), ("g1", 2), ("n1", 2), ("g2", 2), ("n2", 2), ("g3", 2), ("n3", 2),
                  ("sq", 2), ("sk", 2), ("sv", 2), ("so", 2), ("cq", 2), ("ck", 2), ("cv", 2), ("co", 2),
                  ("b1", 8), ("b2", 2))


class Steps:

    def __init__(self, sem, known):
        self.sem, self.known, self.n, self.names = sem, known, 0, {}

    def step(self, name=None):
        self.n += 1
        if name is not None:
            assert name not in self.names, name
            self.names[name] = self.n
        return 1

    def at(self, name):
        return self.known.get(name, 1)


class Program:

    def __init__(self, sems, known):
        self.pe, self.act, self.dve, self.pool = (
            Steps(s, known.get(n, {})) for s, n in zip(sems, ("pe", "act", "dve", "pool")))
        self.where = {}
        self.known_where = known.get("where", {})

    def bank_of(self, job):
        return self.known_where.get(job, 0)

    def result(self):
        return {"pe": self.pe.names, "act": self.act.names, "dve": self.dve.names,
                "pool": self.pool.names, "where": self.where}


class Ring:

    def __init__(self, prog, view, slots):
        self.prog, self.view, self.slots, self.i, self.last = prog, view, slots, 0, [None] * len(slots)

    def take(self, job, steps, emptied):
        k = self.i % len(self.slots)
        self.i += 1
        freed, self.last[k] = self.last[k], (steps.sem, steps.at(emptied))
        self.prog.where[job] = self.slots[k]
        return self.view(self.slots[k]), freed


def build(nc, known, x_in, ctx_in, cst_in, w0_in, w1a_in, w1b_in, v0_in, w2_in, v2_in, w3_in, v3_in, out):
    found = {}
    stack = ExitStack()
    with stack:
        sem = lambda name: stack.enter_context(nc.semaphore(name))
        pe_done, act_done, dve_done, pool_done = (sem(n) for n in ("pe_done", "act_done", "dve_done", "pool_done"))
        engine_sems = (pe_done, act_done, dve_done, pool_done)
        const_loaded, w0_loaded, w1a_loaded, w1b_loaded, w3_loaded = (
            sem(n) for n in ("const_loaded", "w0_loaded", "w1a_loaded", "w1b_loaded", "w3_loaded"))
        x_loaded, x_stored, layer_loaded = sem("x_loaded"), sem("x_stored"), sem("layer_loaded")
        per_block = (*engine_sems, x_loaded, x_stored, layer_loaded)

        hs = nc.dram_tensor("hs", (B, P, ND * S2), F32, kind="Internal").ap()
        psum = stack.enter_context(nc.psum_tensor("psum", [P, 8 * BANK], F32))
        cst = stack.enter_context(nc.sbuf_tensor("cst", [P, C_END], F32))
        ident = cst[:, C_IDENT:C_IDENT + P]
        mean_w = cst[:, C_MEAN:C_MEAN + P]

        def bank(i):
            return psum[:, i * BANK:(i + 1) * BANK]

        def wide(i):
            return psum[:, i * BANK:i * BANK + S2]

        def end_of_block():
            for s in per_block:
                nc.sync.sem_clear(s)
            nc.all_engine_barrier()

        class Dense:

            def __init__(self, name, sb):
                self.prog = prog = Program(engine_sems, known.get(name, {}))
                self.lin = Ring(prog, bank, [0, 1, 2])
                self.scr = Ring(prog, bank, [3, 4, 5])
                self.trn = Ring(prog, bank, [6, 7])
                norm = sb("norm", [P, 2 * ND, T])
                self.dx = norm[:, 0:ND, :]
                self.sq = norm[:, ND:2 * ND, :]
                self.rs = sb("rs", [P, T])
                self.eps = sb("eps", [P, 1])
                self.ln = sb("ln", [P, ND, T])
                self.pr = sb("pr", [P, 6, T])
                self.ptr = (sb("ptr", [P, NT, T]), norm)
                self.mx = sb("mx", [P, 4, H // 2])
                self.sm = sb("sm", [P, 4, H // 2])
                self.ri = sb("ri", [P, 4, H // 2])
                self.nm, self.smh, self.rih = self.mx[:, 0, :], self.sm[:, 0, :], self.ri[:, 0, :]

            def pe_linear(self, pe, name, w, x, nk, tiles, of, width=T):
                p = self.prog
                for j in tiles:
                    b, emptied = self.lin.take(f"{name} {j}", of, f"{name} {j} out")
                    if emptied:
                        pe.wait_ge(*emptied)
                    for k in range(nk):
                        mm = nc.tensor.matmul(b[:, 0:width], w[:, k, j * P:(j + 1) * P], x[:, k, 0:width],
                                              start=k == 0, stop=k == nk - 1)
                    mm.then_inc(pe_done, p.pe.step(f"{name} {j}"))

            def full(self, job):
                return bank(self.prog.bank_of(job))

            def pe_norm(self, pe, name, x, ready, rms=False):
                p = self.prog
                if not rms:
                    pe.wait_ge(*ready)
                    b, emptied = self.lin.take(f"{name} mean", p.dve, f"{name} centred")
                    if emptied:
                        pe.wait_ge(*emptied)
                    for k in range(ND):
                        mm = nc.tensor.matmul(b, mean_w, x[:, k, :], start=k == 0, stop=k == ND - 1)
                    mm.then_inc(pe_done, p.pe.step(f"{name} mean"))
                b, emptied = self.lin.take(f"{name} var", p.act, f"{name} log")
                if emptied:
                    pe.wait_ge(*emptied)
                pe.wait_ge(act_done, p.act.at(f"{name} squares"))
                for k in range(ND):
                    mm = nc.tensor.matmul(b, mean_w, self.sq[:, k, :], start=k == 0, stop=k == ND - 1)
                mm.then_inc(pe_done, p.pe.step(f"{name} var"))

            def act_norm(self, act, name, src=None):
                p = self.prog
                if src is None:
                    src = self.dx
                    act.wait_ge(dve_done, p.dve.at(f"{name} centred"))
                for k in range(ND):
                    a = nc.scalar.activation(self.sq[:, k, :], src[:, k, :], ACT.Square)
                    a.then_inc(act_done, p.act.step(f"{name} squares" if k == ND - 1 else None))
                act.wait_ge(pe_done, p.pe.at(f"{name} var"))
                nc.scalar.activation(self.rs[:, :], self.full(f"{name} var"), ACT.Ln, bias=self.eps[:, 0:1])\
                    .then_inc(act_done, p.act.step(f"{name} log"))
                act.wait_ge(act_done, p.act.n)
                nc.scalar.activation(self.rs[:, :], self.rs[:, :], ACT.Exp, scale=-0.5)\
                    .then_inc(act_done, p.act.step(f"{name} rstd"))

            def dve_norm(self, dve, name, x, g, b):
                p = self.prog
                dve.wait_ge(dve_done, p.dve.n)
                dve.wait_ge(pe_done, p.pe.at(f"{name} mean"))
                for k in range(ND):
                    nc.vector.tensor_tensor(self.dx[:, k, :], x[:, k, :], self.full(f"{name} mean"), ALU.subtract)\
                        .then_inc(dve_done, p.dve.step(f"{name} centred" if k == ND - 1 else None))
                dve.wait_ge(dve_done, p.dve.n)
                dve.wait_ge(act_done, p.act.at(f"{name} rstd"))
                for k in range(ND):
                    nc.vector.scalar_tensor_tensor(self.ln[:, k, :], self.dx[:, k, :], g[:, k:k + 1], self.rs[:, :],
                                                   ALU.mult, ALU.mult).then_inc(dve_done, p.dve.step())
                for k in range(ND):
                    dve.wait_ge(dve_done, p.dve.n - 1)
                    nc.vector.tensor_scalar(self.ln[:, k, :], self.ln[:, k, :], b[:, k:k + 1], None, ALU.add)\
                        .then_inc(dve_done, p.dve.step(f"{name} out" if k == ND - 1 else None))

            def dve_residual(self, dve, name, x, bias):
                p = self.prog
                for j in range(ND):
                    dve.wait_ge(dve_done, p.dve.n)
                    dve.wait_ge(pe_done, p.pe.at(f"{name} {j}"))
                    nc.vector.scalar_tensor_tensor(x[:, j, :], self.full(f"{name} {j}"), bias[:, j:j + 1], x[:, j, :],
                                                   ALU.add, ALU.add).then_inc(dve_done, p.dve.step(f"{name} {j} out"))

            def pe_mlp(self, pe, name, ready, w1, w2, hid):
                p = self.prog
                pe.wait_ge(*ready)
                self.pe_linear(pe, f"{name} up", w1, self.ln, ND, range(FF // P), p.act)
                pe.wait_ge(act_done, p.act.at(f"{name} up {FF // P - 1} out"))
                self.pe_linear(pe, f"{name} down", w2, hid, FF // P, range(ND), p.dve)

            def act_mlp(self, act, name, b1, hid):
                p = self.prog
                for j in range(FF // P):
                    act.wait_ge(pe_done, p.pe.at(f"{name} up {j}"))
                    nc.scalar.activation(hid[:, j, :], self.full(f"{name} up {j}"), ACT.Gelu, bias=b1[:, j:j + 1])\
                        .then_inc(act_done, p.act.step(f"{name} up {j} out"))

            def cross_units(self):
                return [(qt, g) for qt in range(NT) for g in range(2)]

            def pe_cross(self, pe, name, q, kbd, vbd, wide_heads):
                p = self.prog
                units = self.cross_units()

                def scores(u):
                    qt, g = units[u]
                    b, emptied = self.scr.take(f"{name} s {u}", p.dve, f"{name} shifted {u}")
                    if emptied:
                        pe.wait_ge(*emptied)
                    if wide_heads:
                        for f in range(4):
                            mm = nc.tensor.matmul(b[:, f * P:(f + 1) * P], q[:, 4 * g + f, qt * P:(qt + 1) * P],
                                                  kbd[:, 4 * g + f, :], start=True, stop=True)
                    else:
                        mm = nc.tensor.matmul(b, q[:, g, qt * P:(qt + 1) * P], kbd[:, g, :], start=True, stop=True)
                    mm.then_inc(pe_done, p.pe.step(f"{name} s {u}"))

                def flip(u):
                    b, emptied = self.trn.take(f"{name} t {u}", p.act, f"{name} flipped {u}")
                    if emptied:
                        pe.wait_ge(*emptied)
                    pe.wait_ge(pool_done, p.pool.at(f"{name} normed {u}"))
                    for hp in range(4):
                        mm = nc.tensor.transpose(b[:, hp * P:(hp + 1) * P], self.pr[:, u % 3, hp * P:(hp + 1) * P],
                                                 ident)
                    mm.then_inc(pe_done, p.pe.step(f"{name} t {u}"))

                for u in range(len(units) + 2):
                    if u < len(units):
                        scores(u)
                    if u >= 2:
                        flip(u - 2)
                pe.wait_ge(act_done, p.act.at(f"{name} flipped {len(units) - 1}"))
                if wide_heads:
                    for f in range(8):
                        b, emptied = self.lin.take(f"{name} o {f}", p.dve, f"{name} o {f} out")
                        if emptied:
                            pe.wait_ge(*emptied)
                        nc.tensor.matmul(b, vbd[:, f, :], self.pt[:, f // 4, f % 4, :], start=True, stop=True)\
                            .then_inc(pe_done, p.pe.step(f"{name} o {f}"))
                else:
                    for g in range(2):
                        b, emptied = self.lin.take(f"{name} o {g}", p.dve, f"{name} o {g} out")
                        if emptied:
                            pe.wait_ge(*emptied)
                        for hp in range(4):
                            mm = nc.tensor.matmul(b, vbd[:, g, hp, :], self.pt[:, g, hp, :],
                                                  start=hp == 0, stop=hp == 3)
                        mm.then_inc(pe_done, p.pe.step(f"{name} o {g}"))

            def dve_cross(self, dve, name):
                p = self.prog
                n = len(self.cross_units())

                def shift(u):
                    dve.wait_ge(pe_done, p.pe.at(f"{name} s {u}"))
                    s = self.full(f"{name} s {u}").rearrange("p (h k) -> p h k", k=KEYS)
                    dve.wait_ge(dve_done, p.dve.n)
                    nc.vector.tensor_reduce(self.mx[:, u % 4, :], s, AX.X, ALU.max)\
                        .then_inc(dve_done, p.dve.step())
                    dve.wait_ge(dve_done, p.dve.n)
                    if u >= 3:
                        dve.wait_ge(pe_done, p.pe.at(f"{name} t {u - 3}"))
                    nc.vector.tensor_tensor(self.pr[:, u % 3, :].rearrange("p (h k) -> p h k", k=KEYS), s,
                                            self.mx[:, u % 4, :].unsqueeze(2).to_broadcast([P, 8, KEYS]),
                                            ALU.subtract).then_inc(dve_done, p.dve.step(f"{name} shifted {u}"))

                def total(u):
                    dve.wait_ge(act_done, p.act.at(f"{name} exp {u}"))
                    dve.wait_ge(dve_done, p.dve.n)
                    nc.vector.tensor_reduce(self.sm[:, u % 4, :],
                                            self.pr[:, u % 3, :].rearrange("p (h k) -> p h k", k=KEYS),
                                            AX.X, ALU.add).then_inc(dve_done, p.dve.step())
                    dve.wait_ge(dve_done, p.dve.n)
                    nc.vector.reciprocal(self.ri[:, u % 4, :], self.sm[:, u % 4, :])\
                        .then_inc(dve_done, p.dve.step(f"{name} sums {u}"))

                for u in range(n + 1):
                    if u < n:
                        shift(u)
                    if u >= 1:
                        total(u - 1)

            def act_cross(self, act, name):
                p = self.prog
                n = len(self.cross_units())
                for u in range(n + 2):
                    if u < n:
                        act.wait_ge(dve_done, p.dve.at(f"{name} shifted {u}"))
                        nc.scalar.activation(self.pr[:, u % 3, :], self.pr[:, u % 3, :], ACT.Exp)\
                            .then_inc(act_done, p.act.step(f"{name} exp {u}"))
                    if u >= 2:
                        v = u - 2
                        qt, g = self.cross_units()[v]
                        act.wait_ge(pe_done, p.pe.at(f"{name} t {v}"))
                        nc.scalar.activation(self.pt[:, g, :, qt * P:(qt + 1) * P],
                                             self.full(f"{name} t {v}").rearrange("p (h t) -> p h t", h=4), ACT.Copy)\
                            .then_inc(act_done, p.act.step(f"{name} flipped {v}"))

            def pool_cross(self, pool, name):
                p = self.prog
                for u in range(len(self.cross_units())):
                    pool.wait_ge(dve_done, p.dve.at(f"{name} sums {u}"))
                    v = self.pr[:, u % 3, :].rearrange("p (h k) -> p h k", k=KEYS)
                    nc.gpsimd.tensor_tensor(v, v, self.ri[:, u % 4, :].unsqueeze(2).to_broadcast([P, 8, KEYS]),
                                            ALU.mult).then_inc(pool_done, p.pool.step(f"{name} normed {u}"))

            def pe_self(self, pe, name, q, k_of, v_of, per_bank):
                p = self.prog
                banks = {}

                def scores(h, qt):
                    u = NT * h + qt
                    rows, tile, keys = k_of(h)
                    b, emptied = self.scr.take(f"{name} s {u}", p.act, f"{name} exp {u}")
                    if emptied:
                        pe.wait_ge(*emptied)
                    nc.tensor.matmul(b, q[rows, tile, qt * P:(qt + 1) * P], keys, start=True, stop=True)\
                        .then_inc(pe_done, p.pe.step(f"{name} s {u}"))

                def flip(u):
                    b, emptied = self.trn.take(f"{name} t {u}", p.dve, f"{name} flipped {u}")
                    if emptied:
                        pe.wait_ge(*emptied)
                    pe.wait_ge(pool_done, p.pool.at(f"{name} normed {u}"))
                    for kt in range(NT):
                        mm = nc.tensor.transpose(b[:, kt * P:(kt + 1) * P], self.pr[:, u % 6, kt * P:(kt + 1) * P],
                                                 ident)
                    mm.then_inc(pe_done, p.pe.step(f"{name} t {u}"))

                def weigh(h, key_tiles):
                    g = h // per_bank
                    if h % per_bank == 0 and 0 in key_tiles:
                        banks[g], emptied = self.lin.take(f"{name} o {g}", p.dve, f"{name} o {g} out")
                        if emptied:
                            pe.wait_ge(*emptied)
                    if 0 in key_tiles:
                        pe.wait_ge(dve_done, p.dve.at(f"{name} flipped {NT * h + NT - 1}"))
                    for kt in key_tiles:
                        values, rows, first, last = v_of(h, kt)
                        mm = nc.tensor.matmul(banks[g][rows, :], values, self.ptr[h % 2][:, kt, :],
                                              start=first, stop=last)
                    if NT - 1 in key_tiles:
                        mm.then_inc(pe_done, p.pe.step(f"{name} w {h}"))

                for g in range(H + 2):
                    for qt in range(NT):
                        if g < H:
                            scores(g, qt)
                        if 1 <= g <= H:
                            flip(NT * (g - 1) + qt)
                        if g >= 2 and qt % 2:
                            weigh(g - 2, range(qt - 1, qt + 1))

            def dve_self(self, dve, name, per_bank, dst, bias=None):
                p = self.prog
                n = NT * H

                def maximum(u):
                    dve.wait_ge(pe_done, p.pe.at(f"{name} s {u}"))
                    if u >= 8:
                        dve.wait_ge(act_done, p.act.at(f"{name} exp {u - 8}"))
                    nc.vector.tensor_reduce(self.nm[:, u % 8:u % 8 + 1], self.full(f"{name} s {u}"), AX.X, ALU.max,
                                            negate=True).then_inc(dve_done, p.dve.step(f"{name} max {u}"))

                def inverse(u):
                    dve.wait_ge(act_done, p.act.at(f"{name} exp {u}"))
                    if u >= 8:
                        dve.wait_ge(pool_done, p.pool.at(f"{name} normed {u - 8}"))
                    nc.vector.reciprocal(self.rih[:, u % 8:u % 8 + 1], self.smh[:, u % 8:u % 8 + 1])\
                        .then_inc(dve_done, p.dve.step(f"{name} inverse {u}"))

                def flipped(u):
                    h, qt = divmod(u, NT)
                    dve.wait_ge(pe_done, p.pe.at(f"{name} t {u}"))
                    if h >= 2 and qt == 0:
                        dve.wait_ge(pe_done, p.pe.at(f"{name} w {h - 2}"))
                    nc.vector.tensor_copy(self.ptr[h % 2][:, :, qt * P:(qt + 1) * P],
                                          self.full(f"{name} t {u}").rearrange("p (k t) -> p k t", k=NT))\
                        .then_inc(dve_done, p.dve.step(f"{name} flipped {u}"))

                def output(g):
                    dve.wait_ge(pe_done, p.pe.at(f"{name} w {per_bank * g + per_bank - 1}"))
                    if bias is None:
                        nc.vector.tensor_copy(dst[:, g, :], self.full(f"{name} o {g}"))\
                            .then_inc(dve_done, p.dve.step(f"{name} o {g} out"))
                    else:
                        nc.vector.tensor_scalar(dst[:, g, :], self.full(f"{name} o {g}"), bias[:, g:g + 1], None,
                                                ALU.add).then_inc(dve_done, p.dve.step(f"{name} o {g} out"))

                for u in range(n + 2 * NT + 2):
                    if u < n:
                        maximum(u)
                    if 1 <= u <= n:
                        inverse(u - 1)
                    if NT <= u < n + NT:
                        flipped(u - NT)
                    h = (u - 1) // NT - 2 if u % NT == 1 and u > 2 * NT else None
                    if h is not None and h % per_bank == per_bank - 1:
                        output(h // per_bank)

            def act_self(self, act, name):
                p = self.prog
                for u in range(NT * H):
                    act.wait_ge(dve_done, p.dve.at(f"{name} max {u}"))
                    if u >= 6:
                        act.wait_ge(pe_done, p.pe.at(f"{name} t {u - 6}"))
                    if u >= 8:
                        act.wait_ge(dve_done, p.dve.at(f"{name} inverse {u - 8}"))
                    nc.scalar.activation(self.pr[:, u % 6, :], self.full(f"{name} s {u}"), ACT.Exp,
                                         bias=self.nm[:, u % 8:u % 8 + 1], accum_out=self.smh[:, u % 8:u % 8 + 1])\
                        .then_inc(act_done, p.act.step(f"{name} exp {u}"))

            def pool_self(self, pool, name):
                p = self.prog
                for u in range(NT * H):
                    pool.wait_ge(dve_done, p.dve.at(f"{name} inverse {u}"))
                    nc.gpsimd.tensor_scalar(self.pr[:, u % 6, :], self.pr[:, u % 6, :], self.rih[:, u % 8:u % 8 + 1],
                                            1.0, ALU.mult, ALU.mult)\
                        .then_inc(pool_done, p.pool.step(f"{name} normed {u}"))

        with ExitStack() as mem:
            def sb(name, shape):
                return mem.enter_context(nc.sbuf_tensor(f"a_{name}", shape, F32))

            w0, w1a, w1b, v0 = sb("w0", [P, W0N]), sb("w1a", [P, W1AN]), sb("w1b", [P, W1BN]), sb("v0", [P, V0N])
            big = sb("big", [P, 3, 8, T])
            x = sb("x", [P, ND, T])
            cx = sb("ctx", [P, 2, P])
            ksb = sb("ksb", [P, 8, KEYS])
            p1 = sb("p1", [P, 2, KEYS])
            p2 = sb("p2", [P, 2, KEYS])
            st = Dense("a", sb)
            st.pt = big[:, 1, :, :].rearrange("p (g h) t -> p g h t", g=2)
            pr = st.prog

            def mat(t, cols, name, k, n):
                return t[:, cols[name]:cols[name] + k * n].rearrange("p (k n) -> p k n", k=k)

            def vec(name, n=2):
                return v0[:, V0[name]:V0[name] + n]

            hid = big[:, 2, :, :]
            q1 = big[:, 0, :, :]
            k1 = big[:, 1, :, :]
            v1 = big[:, 2, :, :].rearrange("p (t a) c -> p t (a c)", t=NT)
            q0 = big[:, 0, 0:2, :]
            kbd0 = big[:, 0, 2:4, :]
            vbd0 = big[:, 0, 4:6, :].rearrange("p g (h m) -> p g h m", h=4)
            o0 = big[:, 0, 6:8, :]
            a0 = big[:, 1, 0:2, :]
            kbd1 = big[:, 2, 0:2, :].rearrange("p a (f m) -> p (a f) m", m=P)
            vbd1 = big[:, 2, 2:4, :].rearrange("p a (f m) -> p (a f) m", m=P)

            with nc.Block() as block:
                @block.sync
                def _(sp):
                    sp.dma_start(cst[:, :], cst_in).then_inc(const_loaded, 16)
                    sp.dma_start(v0[:, :], v0_in).then_inc(const_loaded, 16)
                    sp.dma_start(w0[:, :], w0_in).then_inc(w0_loaded, 16)
                    sp.dma_start(w1a[:, :], w1a_in).then_inc(w1a_loaded, 16)
                    sp.dma_start(w1b[:, :], w1b_in).then_inc(w1b_loaded, 16)

                @block.gpsimd
                def _(pool):
                    nc.gpsimd.memset(st.eps[:, :], EPS).then_inc(pool_done, 1)
                    pool.wait_ge(pool_done, 1)
            end_of_block()

            with nc.Fori(0, B) as b:
                with nc.Block() as block:
                    @block.sync
                    def _(sp):
                        sp.dma_start(x[:, :, :], x_in[b].rearrange("p (k t) -> p k t", k=ND)).then_inc(x_loaded, 16)
                        sp.dma_start(cx[:, :, :], ctx_in[b].rearrange("p (k t) -> p k t", k=2)).then_inc(x_loaded, 16)
                        h_out = hs[b].rearrange("p (k t) -> p k t", k=ND)
                        sp.wait_ge(act_done, pr.act.at("pre2 out"))
                        sp.dma_start(h_out[:, :, 0:KEYS], p2[:, :, :]).then_inc(x_stored, 16)
                        sp.wait_ge(dve_done, pr.dve.at("l1 down 1 out"))
                        sp.dma_start(h_out[:, :, KEYS:S2], x[:, :, :]).then_inc(x_stored, 16)
                        sp.wait_ge(x_stored, 32)

                    @block.tensor
                    def _(pe):
                        pe.wait_ge(const_loaded, 32)
                        pe.wait_ge(w0_loaded, 16)
                        pe.wait_ge(x_loaded, 32)
                        bk, emptied = st.lin.take("pre1", pr.act, "pre1 out")
                        if emptied:
                            pe.wait_ge(*emptied)
                        w = mat(w0, W0, "p1", 2, D)
                        for j in range(2):
                            for k in range(2):
                                mm = nc.tensor.matmul(bk[:, j * KEYS:(j + 1) * KEYS], w[:, k, j * P:(j + 1) * P],
                                                      cx[:, k, 0:KEYS], start=k == 0, stop=k == 1)
                        mm.then_inc(pe_done, pr.pe.step("pre1"))
                        bk, emptied = st.lin.take("k0", pr.act, "k0 out")
                        if emptied:
                            pe.wait_ge(*emptied)
                        w = mat(w0, W0, "k", 2, D)
                        for j in range(2):
                            for k in range(2):
                                mm = nc.tensor.matmul(bk[:, j * KEYS:(j + 1) * KEYS], w[:, k, j * P:(j + 1) * P],
                                                      cx[:, k, 0:KEYS], start=k == 0, stop=k == 1)
                        mm.then_inc(pe_done, pr.pe.step("k0"))
                        bk, emptied = st.lin.take("v0", pr.dve, "v0 out")
                        if emptied:
                            pe.wait_ge(*emptied)
                        w = mat(w0, W0, "v", 2, D)
                        for k in range(2):
                            mm = nc.tensor.matmul(bk[:, 0:D], cx[:, k, :], w[:, k, :], start=k == 0, stop=k == 1)
                        mm.then_inc(pe_done, pr.pe.step("v0"))
                        st.pe_linear(pe, "q0", mat(w0, W0, "q", 2, D), x, 2, range(2), pr.dve)
                        pe.wait_ge(act_done, pr.act.at("pre1 out"))
                        bk, emptied = st.lin.take("pre2", pr.act, "pre2 out")
                        if emptied:
                            pe.wait_ge(*emptied)
                        w = mat(w0, W0, "p2", 2, D)
                        for j in range(2):
                            for k in range(2):
                                mm = nc.tensor.matmul(bk[:, j * KEYS:(j + 1) * KEYS], w[:, k, j * P:(j + 1) * P],
                                                      p1[:, k, :], start=k == 0, stop=k == 1)
                        mm.then_inc(pe_done, pr.pe.step("pre2"))
                        pe.wait_ge(dve_done, pr.dve.at("q0 1 out"))
                        pe.wait_ge(dve_done, pr.dve.at("kbd0"))
                        st.pe_cross(pe, "x0", q0, kbd0, vbd0, False)
                        pe.wait_ge(dve_done, pr.dve.at("x0 o 1 out"))
                        st.pe_linear(pe, "o0", mat(w0, W0, "o", 2, D), o0, 2, range(2), pr.act)
                        st.pe_norm(pe, "n0", a0, (act_done, pr.act.at("o0 1 out")))
                        st.pe_mlp(pe, "l0", (dve_done, pr.dve.at("n0 out")), mat(w0, W0, "w1", 2, FF), mat(w0, W0, "w2", 8, D), hid)
                        st.pe_norm(pe, "n1", x, (dve_done, pr.dve.at("x0 sum")))
                        pe.wait_ge(w1a_loaded, 16)
                        pe.wait_ge(dve_done, pr.dve.at("n1 out"))
                        st.pe_linear(pe, "q1", mat(w1a, W1A, "q", 2, INNER), st.ln, 2, range(8), pr.act)
                        st.pe_linear(pe, "k1", mat(w1a, W1A, "k", 2, INNER), st.ln, 2, range(8), pr.act)
                        w = mat(w1a, W1A, "v", 2, INNER)
                        for t in range(NT):
                            for c in range(2):
                                bk, emptied = st.lin.take(f"v1 {t} {c}", pr.dve, f"v1 {t} {c} out")
                                if emptied:
                                    pe.wait_ge(*emptied)
                                for k in range(ND):
                                    mm = nc.tensor.matmul(bk, st.ln[:, k, t * P:(t + 1) * P], w[:, k, c * T:(c + 1) * T],
                                                          start=k == 0, stop=k == ND - 1)
                                mm.then_inc(pe_done, pr.pe.step(f"v1 {t} {c}"))
                        pe.wait_ge(act_done, pr.act.at("k1 7 out"))
                        pe.wait_ge(dve_done, pr.dve.at(f"v1 {NT - 1} 1 out"))

                        def keys_of(h):
                            rows = slice(64 * (h % 2), 64 * (h % 2) + 64)
                            return rows, h // 2, k1[rows, h // 2, :]

                        def values_of(h, kt):
                            return (v1[:, kt, 64 * h:64 * h + 64], slice(64 * (h % 2), 64 * (h % 2) + 64),
                                    kt == 0, kt == NT - 1)
                        st.pe_self(pe, "s1", q1, keys_of, values_of, 2)
                        pe.wait_ge(dve_done, pr.dve.at("s1 o 7 out"))
                        st.pe_linear(pe, "o1", mat(w1a, W1A, "o", 8, D), q1, 8, range(2), pr.dve)
                        pe.wait_ge(w1b_loaded, 16)
                        bk, emptied = st.lin.take("k2", pr.act, "k2 out")
                        if emptied:
                            pe.wait_ge(*emptied)
                        w = mat(w1b, W1B, "k", 2, INNER)
                        for j in range(8):
                            for k in range(2):
                                mm = nc.tensor.matmul(bk[:, j * KEYS:(j + 1) * KEYS], w[:, k, j * P:(j + 1) * P],
                                                      cx[:, k, 0:KEYS], start=k == 0, stop=k == 1)
                        mm.then_inc(pe_done, pr.pe.step("k2"))
                        st.pe_norm(pe, "n2", x, (dve_done, pr.dve.at("o1 1 out")))
                        w = mat(w1b, W1B, "v", 2, INNER)
                        for c in range(2):
                            bk, emptied = st.lin.take(f"v2 {c}", pr.dve, f"v2 {c} out")
                            if emptied:
                                pe.wait_ge(*emptied)
                            for k in range(2):
                                mm = nc.tensor.matmul(bk, cx[:, k, :], w[:, k, c * T:(c + 1) * T], start=k == 0, stop=k == 1)
                            mm.then_inc(pe_done, pr.pe.step(f"v2 {c}"))
                        pe.wait_ge(dve_done, pr.dve.at("n2 out"))
                        st.pe_linear(pe, "q2", mat(w1b, W1B, "q", 2, INNER), st.ln, 2, range(8), pr.act)
                        pe.wait_ge(act_done, pr.act.at("q2 7 out"))
                        pe.wait_ge(dve_done, pr.dve.at("v2 1 out"))
                        st.pe_cross(pe, "x2", q1, kbd1, vbd1, True)
                        pe.wait_ge(dve_done, pr.dve.at("x2 o 7 out"))
                        st.pe_linear(pe, "o2", mat(w1b, W1B, "o", 8, D), q1, 8, range(2), pr.dve)
                        st.pe_norm(pe, "n3", x, (dve_done, pr.dve.at("o2 1 out")))
                        pe.wait_ge(dve_done, pr.dve.at("n3 out"))
                        w = mat(w1b, W1B, "p", 2, 2 * FF)
                        for j in range(8):
                            st.pe_linear(pe, "l1 gate", w, st.ln, 2, [8 + j], pr.act)
                            st.pe_linear(pe, "l1 up", w, st.ln, 2, [j], pr.dve)
                        pe.wait_ge(dve_done, pr.dve.at("l1 up 7 out"))
                        st.pe_linear(pe, "l1 down", mat(w1b, W1B, "f", 8, D), hid, 8, range(2), pr.dve)

                    @block.scalar
                    def _(act):
                        act.wait_ge(const_loaded, 32)
                        act.wait_ge(pe_done, pr.pe.at("pre1"))
                        nc.scalar.activation(p1[:, :, :], st.full("pre1")[:, 0:2 * KEYS].rearrange("p (k t) -> p k t", k=2),
                                             ACT.Silu).then_inc(act_done, pr.act.step("pre1 out"))
                        act.wait_ge(pe_done, pr.pe.at("k0"))
                        for j in range(2):
                            nc.scalar.activation(ksb[:, j, :], st.full("k0")[:, j * KEYS:(j + 1) * KEYS], ACT.Identity,
                                                 bias=vec("k")[:, j:j + 1])\
                                .then_inc(act_done, pr.act.step("k0 out" if j else None))
                        act.wait_ge(pe_done, pr.pe.at("pre2"))
                        nc.scalar.activation(p2[:, :, :], st.full("pre2")[:, 0:2 * KEYS].rearrange("p (k t) -> p k t", k=2),
                                             ACT.Copy).then_inc(act_done, pr.act.step("pre2 out"))
                        st.act_cross(act, "x0")
                        for j in range(2):
                            act.wait_ge(pe_done, pr.pe.at(f"o0 {j}"))
                            nc.scalar.activation(a0[:, j, :], st.full(f"o0 {j}"), ACT.Identity, bias=vec("o")[:, j:j + 1])\
                                .then_inc(act_done, pr.act.step(f"o0 {j} out"))
                        st.act_norm(act, "n0")
                        st.act_mlp(act, "l0", vec("b1", 8), hid)
                        st.act_norm(act, "n1")
                        for j in range(8):
                            act.wait_ge(pe_done, pr.pe.at(f"q1 {j}"))
                            nc.scalar.activation(q1[:, j, :], st.full(f"q1 {j}"), ACT.Copy, scale=0.125)\
                                .then_inc(act_done, pr.act.step(f"q1 {j} out"))
                        for j in range(8):
                            act.wait_ge(pe_done, pr.pe.at(f"k1 {j}"))
                            nc.scalar.activation(k1[:, j, :], st.full(f"k1 {j}"), ACT.Copy)\
                                .then_inc(act_done, pr.act.step(f"k1 {j} out"))
                        st.act_self(act, "s1")
                        act.wait_ge(pe_done, pr.pe.at("k2"))
                        nc.scalar.activation(ksb[:, :, :], st.full("k2").rearrange("p (f k) -> p f k", f=8), ACT.Copy)\
                            .then_inc(act_done, pr.act.step("k2 out"))
                        st.act_norm(act, "n2")
                        for j in range(8):
                            act.wait_ge(pe_done, pr.pe.at(f"q2 {j}"))
                            nc.scalar.activation(q1[:, j, :], st.full(f"q2 {j}"), ACT.Copy, scale=0.125)\
                                .then_inc(act_done, pr.act.step(f"q2 {j} out"))
                        st.act_cross(act, "x2")
                        st.act_norm(act, "n3")
                        for j in range(8):
                            act.wait_ge(pe_done, pr.pe.at(f"l1 gate {8 + j}"))
                            if j >= 3:
                                act.wait_ge(dve_done, pr.dve.at(f"l1 up {j - 3} out"))
                            nc.scalar.activation(st.pr[:, j % 3, :], st.full(f"l1 gate {8 + j}"), ACT.Gelu,
                                                 bias=vec("p", 16)[:, 8 + j:9 + j])\
                                .then_inc(act_done, pr.act.step(f"l1 gate {8 + j} out"))

                    @block.vector
                    def _(dve):
                        dve.wait_ge(const_loaded, 32)
                        dve.wait_ge(pe_done, pr.pe.at("v0"))
                        for g in range(2):
                            for hp in range(4):
                                nc.vector.tensor_tensor(
                                    vbd0[:, g, hp, :].rearrange("p (h d) -> p h d", h=8),
                                    st.full("v0")[:, g * P:(g + 1) * P].rearrange("p (h d) -> p h d", h=8),
                                    cst[:, C_MV + 8 * hp:C_MV + 8 * hp + 8].unsqueeze(2).to_broadcast([P, 8, 16]),
                                    ALU.mult).then_inc(dve_done, pr.dve.step("v0 out" if (g, hp) == (1, 3) else None))
                        for j in range(2):
                            dve.wait_ge(pe_done, pr.pe.at(f"q0 {j}"))
                            nc.vector.tensor_scalar(q0[:, j, :], st.full(f"q0 {j}"), vec("q")[:, j:j + 1], 0.25,
                                                    ALU.add, ALU.mult).then_inc(dve_done, pr.dve.step(f"q0 {j} out"))
                        dve.wait_ge(act_done, pr.act.at("k0 out"))
                        for g in range(2):
                            nc.vector.tensor_tensor(
                                kbd0[:, g, :].rearrange("p (h k) -> p h k", h=8),
                                ksb[:, g, :].unsqueeze(1).to_broadcast([P, 8, KEYS]),
                                cst[:, C_MK:C_MK + 8].unsqueeze(2).to_broadcast([P, 8, KEYS]),
                                ALU.mult).then_inc(dve_done, pr.dve.step("kbd0" if g else None))
                        st.dve_cross(dve, "x0")
                        for g in range(2):
                            dve.wait_ge(pe_done, pr.pe.at(f"x0 o {g}"))
                            nc.vector.tensor_scalar(o0[:, g, :], st.full(f"x0 o {g}"), vec("v")[:, g:g + 1], None, ALU.add)\
                                .then_inc(dve_done, pr.dve.step(f"x0 o {g} out"))
                        st.dve_norm(dve, "n0", a0, vec("g"), vec("b"))
                        for j in range(2):
                            dve.wait_ge(dve_done, pr.dve.n)
                            dve.wait_ge(act_done, pr.act.at(f"o0 {j} out"))
                            nc.vector.tensor_tensor(x[:, j, :], x[:, j, :], a0[:, j, :], ALU.add)\
                                .then_inc(dve_done, pr.dve.step())
                        st.dve_residual(dve, "l0 down", x, vec("b2"))
                        pr.dve.names["x0 sum"] = pr.dve.n
                        st.dve_norm(dve, "n1", x, vec("g1"), vec("n1"))
                        for t in range(NT):
                            for c in range(2):
                                dve.wait_ge(pe_done, pr.pe.at(f"v1 {t} {c}"))
                                nc.vector.tensor_copy(v1[:, t, c * T:(c + 1) * T], st.full(f"v1 {t} {c}"))\
                                    .then_inc(dve_done, pr.dve.step(f"v1 {t} {c} out"))
                        st.dve_self(dve, "s1", 2, q1)
                        st.dve_residual(dve, "o1", x, vec("o1"))
                        dve.wait_ge(act_done, pr.act.at("k2 out"))
                        nc.vector.tensor_tensor(
                            kbd1.rearrange("p f (h k) -> p f h k", h=2),
                            ksb[:, :, :].unsqueeze(2).to_broadcast([P, 8, 2, KEYS]),
                            cst[:, C_M64:C_M64 + 2].unsqueeze(1).unsqueeze(3).to_broadcast([P, 8, 2, KEYS]),
                            ALU.mult).then_inc(dve_done, pr.dve.step())
                        st.dve_norm(dve, "n2", x, vec("g2"), vec("n2"))
                        for c in range(2):
                            dve.wait_ge(pe_done, pr.pe.at(f"v2 {c}"))
                            nc.vector.tensor_tensor(
                                vbd1[:, 4 * c:4 * c + 4, :].rearrange("p f (h d) -> p f h d", h=2),
                                st.full(f"v2 {c}").rearrange("p (f h d) -> p f h d", h=2, d=64),
                                cst[:, C_M64:C_M64 + 2].unsqueeze(1).unsqueeze(3).to_broadcast([P, 4, 2, 64]),
                                ALU.mult).then_inc(dve_done, pr.dve.step(f"v2 {c} out"))
                        st.dve_cross(dve, "x2")
                        for f in range(8):
                            dve.wait_ge(pe_done, pr.pe.at(f"x2 o {f}"))
                            nc.vector.tensor_copy(q1[:, f, :], st.full(f"x2 o {f}"))\
                                .then_inc(dve_done, pr.dve.step(f"x2 o {f} out"))
                        st.dve_residual(dve, "o2", x, vec("o2"))
                        st.dve_norm(dve, "n3", x, vec("g3"), vec("n3"))
                        for j in range(8):
                            dve.wait_ge(act_done, pr.act.at(f"l1 gate {8 + j} out"))
                            dve.wait_ge(pe_done, pr.pe.at(f"l1 up {j}"))
                            nc.vector.scalar_tensor_tensor(hid[:, j, :], st.full(f"l1 up {j}"), vec("p", 16)[:, j:j + 1],
                                                           st.pr[:, j % 3, :], ALU.add, ALU.mult)\
                                .then_inc(dve_done, pr.dve.step(f"l1 up {j} out"))
                        st.dve_residual(dve, "l1 down", x, vec("f"))

                    @block.gpsimd
                    def _(pool):
                        st.pool_cross(pool, "x0")
                        st.pool_self(pool, "s1")
                        st.pool_cross(pool, "x2")
                found["a"] = pr.result()
                end_of_block()

        with ExitStack() as mem:
            def sb(name, shape):
                return mem.enter_context(nc.sbuf_tensor(f"m_{name}", shape, F32))

            wa, va = sb("wa", [P, W2A]), sb("va", [P, V2A])
            wb, vb = sb("wb", [P, W2N - W2A]), sb("vb", [P, V2N - V2A])
            h = sb("h", [P, B, ND, S2])
            xc = sb("xc", [P, NE, 3 + S2])
            cv = sb("cv", [P, NE, S2])
            xi = sb("xi", [P, 2, NE, S2])
            zs = sb("zs", [P, 2, NE, S2])
            dt = sb("dt", [P, 2, NE, S2])
            bc = sb("bc", [P, 2, len(TT), NX])
            spe = sb("spe", [P, NE, S2])
            spl, spu = sb("spl", [P, 2, S2]), sb("spu", [P, 2, S2])
            sq, xn, rs, xd = spe[:, 0:ND, :], spe[:, ND:2 * ND, :], spl[:, 0, :], spu[0:NX, 0, :]
            ut = sb("ut", [P, len(TT), DI])
            ub = sb("ub", [P, 2, len(TT), DI])
            da = sb("da", [P, 8, S2])
            hh = sb("hh", [P, 2, NE, S2])
            yt = sb("yt", [P, len(TT), DI])
            ys = sb("ys", [P, 2, DI])
            am = sb("am", [P, NE * DS])
            eps2 = sb("eps", [P, 1])

            SHARED = 3
            ORDER = (0, 1, 2, 4, SHARED)
            LAST = DS - 1
            HALVES = ((0, BANK), (BANK, S2))

            def mat2(name, k, n):
                t, at = (wa, W2[name]) if W2[name] < W2A else (wb, W2[name] - W2A)
                return t[:, at:at + k * n].rearrange("p (k n) -> p k n", k=k)

            def vec2(name, i):
                t, at = (va, V2[name]) if V2[name] < V2A else (vb, V2[name] - V2A)
                return t[:, at + i:at + i + 1]

            def mamba(name, mains, last_item, first_loads, next_loads, store):
                pr = Program(engine_sems, known.get(name, {}))
                wring, sring, tring = Ring(pr, wide, [0, 2]), Ring(pr, wide, [4]), Ring(pr, bank, [6, 7])
                full = lambda job: wide(pr.bank_of(job))
                steps = [(i, n) for i in mains for n in range(DS)]

                def sides(i, n):
                    return (i - 1 if i - 1 in mains else None), (i + 1 if i + 1 <= last_item else None)

                alone = [(mains[-1] + 1 if mains else -1, k) for k in range(DS)]

                with nc.Block() as block:
                    @block.sync
                    def _(sp):
                        for dst, src in first_loads:
                            sp.dma_start(dst, src).then_inc(x_loaded, 16)
                        if next_loads:
                            sp.wait_ge(dve_done, pr.dve.at(f"{B - 1} dt {NE - 1}"))
                            for dst, src in next_loads:
                                sp.dma_start(dst, src).then_inc(layer_loaded, 16)
                        if store:
                            for i in mains:
                                sp.wait_ge(dve_done, pr.dve.at(f"{i} h 1"))
                                sp.dma_start(hs[i].rearrange("p (k t) -> p k t", k=ND), h[:, i, :, :])\
                                    .then_inc(x_stored, 16)
                            sp.wait_ge(x_stored, 16 * len(mains))
                        sp.wait_ge(x_loaded, 16 * len(first_loads))

                    @block.tensor
                    def _(pe):
                        def product(job, of, emptied, pairs, m=P, half=None):
                            if half != 1:
                                s, freed = sring.take(job, of, emptied)
                                if freed:
                                    pe.wait_ge(*freed)
                            s, n = full(job), len(pairs)
                            ks = range(n) if half is None else range(half * n // 2, (half + 1) * n // 2)
                            for lo, hi in HALVES:
                                for k in ks:
                                    lhs, rhs = pairs[k]
                                    mm = nc.tensor.matmul(s[0:m, lo:hi], lhs, rhs[:, lo:hi],
                                                          start=k == 0, stop=k == n - 1)
                            if half != 0:
                                mm.then_inc(pe_done, pr.pe.step(job))

                        def in_proj(i, j):
                            if j == 0:
                                pe.wait_ge(dve_done, pr.dve.at(f"{i} xn"))
                            w = mat2("in", ND, 2 * DI)
                            product(f"{i} in {j}", pr.act, f"{i} in {j} out",
                                    [(w[:, k, j * P:(j + 1) * P], xn[:, k, :]) for k in range(ND)])

                        def dt_proj(i, e):
                            if e == 0:
                                pe.wait_ge(dve_done, pr.dve.at(f"{i} xd"))
                            product(f"{i} dt {e}", pr.act, f"{i} dt {e} in",
                                    [(wa[0:DR, W2["dt"] + e * P:W2["dt"] + (e + 1) * P], xd[0:DR, :])])

                        def x_proj(i, half):
                            if half == 0:
                                pe.wait_ge(act_done, pr.act.at(f"{i} xi {NE - 1}"))
                            w = mat2("x", NE, NX)
                            product(f"{i} xd", pr.dve, f"{i} xd",
                                    [(w[:, e, :], xi[:, i % 2, e, :]) for e in range(NE)], m=NX, half=half)

                        def out_proj(i, j, half):
                            if j == 0 and half == 0:
                                pe.wait_ge(dve_done, pr.dve.at(f"{i} yg 1"))
                            if j == 0 and half == 1:
                                pe.wait_ge(pool_done, pr.pool.at(f"{i} yg {NE - 1}"))
                            w = mat2("out", NE, D)
                            product(f"{i} out {j}", pr.dve, f"{i} h {j}",
                                    [(w[:, e, j * P:(j + 1) * P], cv[:, e, :]) for e in range(NE)], half=half)

                        def y_back(i, e):
                            job = f"{i} yf {e}"
                            if e % 2:
                                freed = list(tring.last)
                                tring.last = [(pr.dve.sem, pr.dve.at(f"{i} yd {e}"))] * 2
                                pr.where[job] = 6
                                s = wide(6)
                                for f in freed:
                                    pe.wait_ge(*f)
                            else:
                                s, freed = sring.take(job, pr.dve, f"{i} yd {e}")
                                if freed:
                                    pe.wait_ge(*freed)
                            if e == 0:
                                pe.wait_ge(dve_done, pr.dve.at(f"{i} y {LAST} {ORDER[-2]}"))
                                pe.wait_ge(pool_done, pr.pool.at(f"{i} y {LAST} {SHARED}"))
                            for t, (t0, m) in enumerate(TT):
                                mm = nc.tensor.transpose(s[:, t0:t0 + m], yt[0:m, t, e * P:(e + 1) * P],
                                                         ident[0:m, 0:m])
                            mm.then_inc(pe_done, pr.pe.step(job))

                        def u_turn(i, pair):
                            tiles = list(enumerate(TT))[2 * pair:2 * pair + 2]
                            s, emptied = sring.take(f"{i} ut {pair}", pr.act, f"{i} ut {tiles[-1][0]} out")
                            pe.wait_ge(*emptied)
                            for t, (t0, m) in tiles:
                                for e in range(NE):
                                    mm = nc.tensor.transpose(
                                        psum[0:m, (4 + t % 2) * BANK + e * P:(4 + t % 2) * BANK + (e + 1) * P],
                                        cv[:, e, t0:t0 + m], ident)
                            mm.then_inc(pe_done, pr.pe.step(f"{i} ut {pair}"))

                        def early(k, post, pre):
                            if post is not None:
                                if k == 2:
                                    out_proj(post, 0, 1)
                                if k == 3:
                                    out_proj(post, 1, 1)
                            if pre is not None:
                                if k == 1:
                                    pe.wait_ge(act_done, pr.act.at(f"{pre} squares"))
                                    product(f"{pre} var", pr.act, f"{pre} log",
                                            [(mean_w, sq[:, j, :]) for j in range(ND)])
                                if 4 <= k <= 6:
                                    in_proj(pre, 2 * (k - 4) + 1)
                                if k == 8:
                                    x_proj(pre, 1)
                                if k == 9:
                                    dt_proj(pre, 0)
                                    dt_proj(pre, 1)
                                if k == 10:
                                    s, emptied = sring.take(f"{pre} bc", pr.dve, f"{pre} bc out")
                                    pe.wait_ge(*emptied)
                                    for t, (t0, m) in enumerate(TT):
                                        mm = nc.tensor.transpose(s[0:m, t * NX:(t + 1) * NX], xd[:, t0:t0 + m],
                                                                 ident[0:NX, 0:NX])
                                    mm.then_inc(pe_done, pr.pe.step(f"{pre} bc"))
                                if k == 15:
                                    u_turn(pre, 1)
                                    u_turn(pre, 2)

                        def late(k, post, pre):
                            if post is not None:
                                if k == 0:
                                    for e in range(NE):
                                        y_back(post, e)
                                if k == 1:
                                    out_proj(post, 0, 0)
                                if k == 2:
                                    out_proj(post, 1, 0)
                            if pre is not None:
                                if 3 <= k <= 5:
                                    in_proj(pre, 2 * (k - 3))
                                if k == 6:
                                    in_proj(pre, 6)
                                    in_proj(pre, 7)
                                if k == 7:
                                    x_proj(pre, 0)
                                if k == 9:
                                    dt_proj(pre, 2)
                                    dt_proj(pre, 3)
                                if k == 14:
                                    pe.wait_ge(dve_done, pr.dve.at(f"{pre} u {NE - 1}"))
                                    u_turn(pre, 0)

                        def state_input(i, n, e):
                            if e == 0:
                                pe.wait_ge(pool_done, pr.pool.at(f"{i} ub {n}"))
                            s, emptied = wring.take(f"{i} db {n} {e}", pr.dve, f"{i} scan {n} {e}")
                            if emptied:
                                pe.wait_ge(*emptied)
                            for t, (t0, m) in enumerate(TT):
                                mm = nc.tensor.transpose(s[:, t0:t0 + m], ub[0:m, n % 2, t, e * P:(e + 1) * P],
                                                         ident[0:m, 0:m])
                            mm.then_inc(pe_done, pr.pe.step(f"{i} db {n} {e}"))

                        def output(i, n, t):
                            t0, m = TT[t]
                            if t == ORDER[0]:
                                pe.wait_ge(dve_done, pr.dve.at(f"{i} scan {n} {NE - 1}"))
                            by = (pr.act, f"{i} ys {n}") if t == SHARED else (pr.dve, f"{i} y {n} {t}")
                            s, emptied = tring.take(f"{i} ht {n} {t}", *by)
                            if emptied:
                                pe.wait_ge(*emptied)
                            for e in range(NE):
                                mm = nc.tensor.transpose(s[0:m, e * P:(e + 1) * P], hh[:, n % 2, e, t0:t0 + m], ident)
                            mm.then_inc(pe_done, pr.pe.step(f"{i} ht {n} {t}"))

                        before = None
                        for i, n in steps:
                            for e in range(NE):
                                state_input(i, n, e)
                                if before:
                                    output(*before, ORDER[e])
                                if e == 1:
                                    early(n, *sides(i, n))
                            if before:
                                output(*before, SHARED)
                            late(n, *sides(i, n))
                            before = (i, n)
                        if before:
                            for t in ORDER:
                                output(*before, t)
                        else:
                            pe.wait_ge(x_loaded, 16 * len(first_loads))
                        for i, k in alone:
                            early(k, *sides(i, k))
                            late(k, *sides(i, k))

                    @block.scalar
                    def _(act):
                        def exponentials(i, n):
                            for e in range(NE):
                                u = NE * (DS * i + n) + e
                                if i and n == 0:
                                    act.wait_ge(dve_done, pr.dve.at(f"{i} dt {e}"))
                                if u >= 8:
                                    j, m = divmod(DS * i + n - 2, DS)
                                    act.wait_ge(dve_done, pr.dve.at(f"{j} scan {m} {e}"))
                                nc.scalar.activation(da[:, u % 8, :], dt[:, i % 2, e, :], ACT.Exp,
                                                     scale=am[:, e * DS + n:e * DS + n + 1])\
                                    .then_inc(act_done, pr.act.step(f"{i} da {n} {e}"))

                        def scaled(i, n):
                            if n == 0 and i:
                                act.wait_ge(pe_done, pr.pe.at(f"{i - 1} yf {NE - 1}"))
                            if n >= 3:
                                act.wait_ge(pool_done, pr.pool.at(f"{i} y {n - 2} {SHARED}"))
                            act.wait_ge(pe_done, pr.pe.at(f"{i} ht {n} {SHARED}"))
                            dst = yt[:, SHARED, :] if n == 0 else ys[:, n % 2, :]
                            nc.scalar.activation(dst, bank(pr.bank_of(f"{i} ht {n} {SHARED}")), ACT.Identity,
                                                 scale=bc[:, i % 2, SHARED, DR + DS + n:DR + DS + n + 1], bias=0.0)\
                                .then_inc(act_done, pr.act.step(f"{i} ys {n}"))

                        def side(k, post, pre):
                            if pre is None:
                                return
                            if k == 0:
                                if pre >= 2:
                                    act.wait_ge(dve_done, pr.dve.at(f"{pre - 1} dt {NE - 1}"))
                                if pre == B:
                                    act.wait_ge(dve_done, pr.dve.at("0 h 1"))
                                for j in range(ND):
                                    nc.scalar.activation(sq[:, j, :], h[:, pre % B, j, :], ACT.Square)\
                                        .then_inc(act_done, pr.act.step(f"{pre} squares" if j else None))
                            if k == 1:
                                act.wait_ge(pe_done, pr.pe.at(f"{pre} var"))
                                nc.scalar.activation(rs, full(f"{pre} var"), ACT.Ln, bias=eps2[:, 0:1])\
                                    .then_inc(act_done, pr.act.step(f"{pre} log"))
                                act.wait_ge(act_done, pr.act.n)
                                nc.scalar.activation(rs, rs, ACT.Exp, scale=-0.5)\
                                    .then_inc(act_done, pr.act.step(f"{pre} rstd"))
                            first, end = {3: (0, 1), 4: (1, 3), 5: (3, 5), 6: (5, 8)}.get(k, (0, 0))
                            for j in range(first, end):
                                act.wait_ge(pe_done, pr.pe.at(f"{pre} in {j}"))
                                if j < NE:
                                    if j == 0 and pre - 2 in mains:
                                        act.wait_ge(pe_done, pr.pe.at(f"{pre - 2} out 1"))
                                    nc.scalar.activation(xc[:, j, 3:3 + S2], full(f"{pre} in {j}"), ACT.Copy)\
                                        .then_inc(act_done, pr.act.step(f"{pre} in {j} out"))
                                    act.wait_ge(act_done, pr.act.n)
                                    nc.scalar.activation(cv[:, j, :], xc[:, j, 0:S2], ACT.Identity,
                                                         bias=vec2("cb", j), scale=vec2("cw", 4 * j))\
                                        .then_inc(act_done, pr.act.step(f"{pre} tap {j}"))
                                else:
                                    nc.scalar.activation(zs[:, pre % 2, j - NE, :], full(f"{pre} in {j}"), ACT.Copy)\
                                        .then_inc(act_done, pr.act.step(f"{pre} in {j} out"))
                            if k == 6:
                                for e in range(NE):
                                    act.wait_ge(dve_done, pr.dve.at(f"{pre} conv {e}"))
                                    nc.scalar.activation(xi[:, pre % 2, e, :], cv[:, e, :], ACT.Silu)\
                                        .then_inc(act_done, pr.act.step(f"{pre} xi {e}"))
                                act.wait_ge(act_done, pr.act.at(f"{pre} in {2 * NE - 1} out"))
                                nc.scalar.activation(zs[:, pre % 2, :, :], zs[:, pre % 2, :, :], ACT.Silu)\
                                    .then_inc(act_done, pr.act.step(f"{pre} zs"))
                            if k == 9:
                                for e in range(NE):
                                    act.wait_ge(pe_done, pr.pe.at(f"{pre} dt {e}"))
                                    nc.scalar.activation(xc[:, e, 3:3 + S2], full(f"{pre} dt {e}"), ACT.Identity,
                                                         bias=vec2("dtb", e))\
                                        .then_inc(act_done, pr.act.step(f"{pre} dt {e} in"))
                            if k == 10:
                                for e in range(NE):
                                    act.wait_ge(dve_done, pr.dve.at(f"{pre} clamp {e}"))
                                    nc.scalar.activation(spe[:, e, :], spe[:, e, :], ACT.Exp)\
                                        .then_inc(act_done, pr.act.step(f"{pre} exp {e}"))
                            if k in (10, 11):
                                for e in range(2 * (k - 10), 2 * (k - 10) + 2):
                                    act.wait_ge(act_done, pr.act.at(f"{pre} exp {e}"))
                                    if k == 11:
                                        act.wait_ge(dve_done, pr.dve.at(f"{pre} max {e - 2}"))
                                    nc.scalar.activation(spl[:, e % 2, :], spe[:, e, :], ACT.Square,
                                                         scale=0.5 ** 0.5)\
                                        .then_inc(act_done, pr.act.step(f"{pre} half {e}"))
                            if k == 10:
                                for e in range(NE):
                                    act.wait_ge(act_done, pr.act.at(f"{pre} exp {e}"))
                                    nc.scalar.activation(dt[:, pre % 2, e, :], spe[:, e, :], ACT.Ln, bias=1.0)\
                                        .then_inc(act_done, pr.act.step(f"{pre} log1p {e}"))
                            if k in (14, 15):
                                if k == 14 and pre - 1 in mains:
                                    act.wait_ge(pool_done, pr.pool.at(f"{pre - 1} ub {LAST}"))
                                for t, (t0, m) in list(enumerate(TT))[2 * (k - 14):2 if k == 14 else len(TT)]:
                                    act.wait_ge(pe_done, pr.pe.at(f"{pre} ut {t // 2}"))
                                    nc.scalar.activation(ut[0:m, t, :], bank(4 + t % 2)[0:m, :],
                                                         ACT.Copy).then_inc(act_done, pr.act.step(f"{pre} ut {t} out"))

                        if steps:
                            act.wait_ge(x_loaded, 16 * len(first_loads))
                            nc.scalar.activation(am[:, :], vb[:, V2["A"] - V2A:V2["A"] - V2A + NE * DS], ACT.Exp)\
                                .then_inc(act_done, pr.act.step())
                            act.wait_ge(act_done, pr.act.n)
                            nc.scalar.activation(am[:, :], am[:, :], ACT.Copy, scale=-1.0)\
                                .then_inc(act_done, pr.act.step("am"))
                            act.wait_ge(act_done, pr.act.n)
                            exponentials(*steps[0])
                        else:
                            act.wait_ge(x_loaded, 16 * len(first_loads))
                        for s, (i, n) in enumerate(steps):
                            if s + 1 < len(steps):
                                exponentials(*steps[s + 1])
                            if s and n not in (1, 9, LAST):
                                scaled(*steps[s - 1])
                            if n == 3 and i + 1 == B and next_loads:
                                act.wait_ge(layer_loaded, 16 * len(next_loads))
                            side(n, *sides(i, n))
                            if s and n in (1, 9, LAST):
                                scaled(*steps[s - 1])
                        if steps:
                            scaled(*steps[-1])
                        for i, k in alone:
                            side(k, *sides(i, k))

                    @block.vector
                    def _(dve):
                        def finish(i, j):
                            dve.wait_ge(pe_done, pr.pe.at(f"{i} out {j}"))
                            nc.vector.tensor_tensor(h[:, i, j, :], h[:, i, j, :], full(f"{i} out {j}"), ALU.add)\
                                .then_inc(dve_done, pr.dve.step(f"{i} h {j}"))

                        def clamp(i, e):
                            dve.wait_ge(pe_done, pr.pe.at(f"{i} dt {e}"))
                            dve.wait_ge(act_done, pr.act.at(f"{i} dt {e} in"))
                            nc.vector.tensor_scalar(spe[:, e, :], xc[:, e, 3:3 + S2], SOFTPLUS_LINEAR, None, ALU.min)\
                                .then_inc(dve_done, pr.dve.step(f"{i} clamp {e}"))

                        def early(k, post, pre):
                            if pre is not None:
                                if k == 2:
                                    dve.wait_ge(act_done, pr.act.at(f"{pre} rstd"))
                                    if pre == B:
                                        dve.wait_ge(layer_loaded, 16 * len(next_loads))
                                    for j in range(ND):
                                        nc.vector.scalar_tensor_tensor(xn[:, j, :], h[:, pre % B, j, :],
                                                                       vec2("norm", j), rs, ALU.mult, ALU.mult)\
                                            .then_inc(dve_done, pr.dve.step(f"{pre} xn" if j else None))
                                if k in (5, 6):
                                    conv(pre, 2 * (k - 5) + 1)
                                if k == 10:
                                    clamp(pre, 0)
                                    clamp(pre, 1)
                                if k in (12, 13):
                                    softplus(pre, 2 * (k - 12) + 1)

                        def late(k, post, pre):
                            if post is not None:
                                if k == 0:
                                    for e in range(NE):
                                        dve.wait_ge(pe_done, pr.pe.at(f"{post} yf {e}"))
                                        nc.vector.scalar_tensor_tensor(cv[:, e, :], xi[:, post % 2, e, :],
                                                                       vec2("D", e), full(f"{post} yf {e}"),
                                                                       ALU.mult, ALU.add)\
                                            .then_inc(dve_done, pr.dve.step(f"{post} yd {e}"))
                                    for e in range(2):
                                        dve.wait_ge(dve_done, pr.dve.at(f"{post} yd {e}"))
                                        nc.vector.tensor_tensor(cv[:, e, :], cv[:, e, :], zs[:, post % 2, e, :],
                                                                ALU.mult)\
                                            .then_inc(dve_done, pr.dve.step(f"{post} yg {e}"))
                                if k in (2, 3):
                                    finish(post, k - 2)
                            if pre is not None:
                                if k in (4, 5):
                                    conv(pre, 2 * (k - 4))
                                if k == 8:
                                    dve.wait_ge(pe_done, pr.pe.at(f"{pre} xd"))
                                    nc.vector.tensor_copy(xd, full(f"{pre} xd")[0:NX, :])\
                                        .then_inc(dve_done, pr.dve.step(f"{pre} xd"))
                                if k == 10:
                                    dve.wait_ge(pe_done, pr.pe.at(f"{pre} bc"))
                                    whole = T // P
                                    nc.vector.tensor_copy(
                                        bc[:, pre % 2, 0:whole, :],
                                        full(f"{pre} bc")[:, 0:whole * NX].rearrange("p (i c) -> p i c", i=whole))\
                                        .then_inc(dve_done, pr.dve.step())
                                    nc.vector.tensor_copy(bc[0:KEYS, pre % 2, whole, :],
                                                          full(f"{pre} bc")[0:KEYS, whole * NX:(whole + 1) * NX])\
                                        .then_inc(dve_done, pr.dve.step(f"{pre} bc out"))
                                    clamp(pre, 2)
                                    clamp(pre, 3)
                                if k in (11, 12):
                                    softplus(pre, 2 * (k - 11))

                        def conv(i, e):
                            dve.wait_ge(act_done, pr.act.at(f"{i} tap {e}"))
                            for t in range(1, 4):
                                dve.wait_ge(dve_done, pr.dve.n)
                                nc.vector.scalar_tensor_tensor(cv[:, e, :], xc[:, e, t:t + S2],
                                                               vec2("cw", 4 * e + t), cv[:, e, :], ALU.mult, ALU.add)\
                                    .then_inc(dve_done, pr.dve.step(f"{i} conv {e}" if t == 3 else None))

                        def softplus(i, e):
                            d = dt[:, i % 2, e, :]
                            dve.wait_ge(act_done, pr.act.at(f"{i} log1p {e}"))
                            dve.wait_ge(pool_done, pr.pool.at(f"{i} lower {e}"))
                            nc.vector.scalar_tensor_tensor(spu[:, e % 2, :], spu[:, e % 2, :], 2.0 / 3.0,
                                                           spl[:, e % 2, :], ALU.mult, ALU.add)\
                                .then_inc(dve_done, pr.dve.step())
                            nc.vector.tensor_tensor(d, d, spl[:, e % 2, :], ALU.max)\
                                .then_inc(dve_done, pr.dve.step())
                            dve.wait_ge(dve_done, pr.dve.n)
                            nc.vector.tensor_tensor(d, d, spu[:, e % 2, :], ALU.min)\
                                .then_inc(dve_done, pr.dve.step(f"{i} max {e}"))
                            dve.wait_ge(dve_done, pr.dve.n)
                            nc.vector.tensor_tensor(d, d, xc[:, e, 3:3 + S2], ALU.max)\
                                .then_inc(dve_done, pr.dve.step(f"{i} dt {e}"))
                            dve.wait_ge(dve_done, pr.dve.n)
                            nc.vector.tensor_tensor(cv[:, e, :], d, xi[:, i % 2, e, :], ALU.mult)\
                                .then_inc(dve_done, pr.dve.step(f"{i} u {e}"))

                        def scan(i, n, e):
                            u = NE * (DS * i + n) + e
                            dve.wait_ge(act_done, pr.act.at(f"{i} da {n} {e}"))
                            dve.wait_ge(pe_done, pr.pe.at(f"{i} db {n} {e}"))
                            if e == 0 and DS * i + n >= 2:
                                j, m = divmod(DS * i + n - 2, DS)
                                dve.wait_ge(pe_done, pr.pe.at(f"{j} ht {m} {SHARED}"))
                            nc.vector.tensor_tensor_scan(hh[:, n % 2, e, :], da[:, u % 8, :],
                                                         full(f"{i} db {n} {e}"), 0.0, ALU.mult, ALU.add)\
                                .then_inc(dve_done, pr.dve.step(f"{i} scan {n} {e}"))

                        def add(i, n, t):
                            t0, m = TT[t]
                            if n == 0 and i and t == ORDER[0]:
                                dve.wait_ge(pe_done, pr.pe.at(f"{i - 1} yf {NE - 1}"))
                            dve.wait_ge(pe_done, pr.pe.at(f"{i} ht {n} {t}"))
                            s = bank(pr.bank_of(f"{i} ht {n} {t}"))[0:m, :]
                            c = bc[0:m, i % 2, t, DR + DS + n:DR + DS + n + 1]
                            if n == 0:
                                nc.vector.tensor_scalar(yt[0:m, t, :], s, c, None, ALU.mult)\
                                    .then_inc(dve_done, pr.dve.step(f"{i} y {n} {t}"))
                            else:
                                dve.wait_ge(dve_done, pr.dve.at(f"{i} y {n - 1} {t}"))
                                nc.vector.scalar_tensor_tensor(yt[0:m, t, :], s, c, yt[0:m, t, :], ALU.mult, ALU.add)\
                                    .then_inc(dve_done, pr.dve.step(f"{i} y {n} {t}"))

                        before = None
                        for i, n in steps:
                            for e in range(NE):
                                scan(i, n, e)
                                if before:
                                    add(*before, ORDER[e])
                                if e == 1:
                                    early(n, *sides(i, n))
                            late(n, *sides(i, n))
                            before = (i, n)
                        if before:
                            for t in ORDER[:-1]:
                                add(*before, t)
                        else:
                            dve.wait_ge(x_loaded, 16 * len(first_loads))
                        for i, k in alone:
                            early(k, *sides(i, k))
                            late(k, *sides(i, k))

                    @block.gpsimd
                    def _(pool):
                        def state_inputs(i, n):
                            if DS * i + n >= 2:
                                j, m = divmod(DS * i + n - 2, DS)
                                pool.wait_ge(pe_done, pr.pe.at(f"{j} db {m} {NE - 1}"))
                            for t, (t0, m) in enumerate(TT):
                                if i and n == 0:
                                    pool.wait_ge(act_done, pr.act.at(f"{i} ut {t} out"))
                                nc.gpsimd.tensor_scalar(ub[0:m, n % 2, t, :], ut[0:m, t, :],
                                                        bc[0:m, i % 2, t, DR + n:DR + n + 1], 1.0, ALU.mult, ALU.mult)\
                                    .then_inc(pool_done,
                                              pr.pool.step(f"{i} ub {n}" if t == len(TT) - 1 else None))

                        def add(i, n):
                            if n == 0:
                                return
                            pool.wait_ge(act_done, pr.act.at(f"{i} ys {n}"))
                            if n >= 2:
                                pool.wait_ge(pool_done, pr.pool.at(f"{i} y {n - 1} {SHARED}"))
                            nc.gpsimd.tensor_tensor(yt[:, SHARED, :], yt[:, SHARED, :], ys[:, n % 2, :], ALU.add)\
                                .then_inc(pool_done, pr.pool.step(f"{i} y {n} {SHARED}"))

                        def side(k, post, pre):
                            if post is not None and k == 0:
                                for e in range(2, NE):
                                    pool.wait_ge(dve_done, pr.dve.at(f"{post} yd {e}"))
                                    nc.gpsimd.tensor_tensor(cv[:, e, :], cv[:, e, :], zs[:, post % 2, e, :], ALU.mult)\
                                        .then_inc(pool_done, pr.pool.step(f"{post} yg {e}"))
                            if pre is not None:
                                for e in {10: (0,), 11: (1,), 12: (2, 3)}.get(k, ()):
                                    lower(pre, e)

                        def lower(i, e):
                            pool.wait_ge(act_done, pr.act.at(f"{i} half {e}"))
                            if e == 0:
                                pool.wait_ge(pe_done, pr.pe.at(f"{i} bc"))
                            nc.gpsimd.tensor_tensor(spu[:, e % 2, :], spe[:, e, :], spl[:, e % 2, :],
                                                    ALU.mult).then_inc(pool_done, pr.pool.step())
                            pool.wait_ge(pool_done, pr.pool.n)
                            nc.gpsimd.tensor_tensor(spl[:, e % 2, :], spe[:, e, :], spl[:, e % 2, :],
                                                    ALU.subtract).then_inc(pool_done, pr.pool.step(f"{i} lower {e}"))

                        if steps:
                            state_inputs(*steps[0])
                        for s, (i, n) in enumerate(steps):
                            if s + 1 < len(steps):
                                state_inputs(*steps[s + 1])
                            if s:
                                add(*steps[s - 1])
                            side(n, *sides(i, n))
                        if steps:
                            add(*steps[-1])
                        for i, k in alone:
                            side(k, *sides(i, k))
                found[name] = pr.result()
                end_of_block()

            def first_weights(layer):
                return [(wa[:, :], w2_in[layer][:, 0:W2A]), (va[:, :], v2_in[layer][:, 0:V2A])]

            def loop_weights(layer):
                return [(wb[:, :], w2_in[layer][:, W2A:W2N]), (vb[:, :], v2_in[layer][:, V2A:V2N])]

            with nc.Block() as block:
                @block.gpsimd
                def _(pool):
                    nc.gpsimd.memset(eps2[:, :], EPS).then_inc(pool_done, 1)
                    nc.gpsimd.memset(xc[:, :, 0:3], 0.0).then_inc(pool_done, 1)
                    pool.wait_ge(pool_done, 2)
            end_of_block()

            mamba("m first", [], 0, first_weights(0)
                  + [(h[:, i, :, :], hs[i].rearrange("p (k t) -> p k t", k=ND)) for i in range(B)], [], False)
            w2_next, v2_next = w2_in[1:L], v2_in[1:L]
            with nc.Fori(0, L - 1) as layer:
                mamba("m", list(range(B)), B, loop_weights(layer),
                      [(wa[:, :], w2_next[layer][:, 0:W2A]), (va[:, :], v2_next[layer][:, 0:V2A])], False)
            mamba("m last", list(range(B)), B - 1, loop_weights(L - 1), [], True)

        with ExitStack() as mem:
            def sb(name, shape):
                return mem.enter_context(nc.sbuf_tensor(f"c_{name}", shape, F32))

            w3, v3 = sb("w3", [P, W3N]), sb("v3", [P, V3N])
            x = sb("x", [P, ND, T])
            cx = sb("ctx", [P, 2, P])
            ksb = sb("ksb", [P, 2, KEYS])
            hid = sb("hid", [P, 8, T])
            q3 = sb("q3", [P, ND, T])
            k3 = sb("k3", [P, 2, ND, T])
            v3s = sb("v3s", [P, NT, 2, 8 * 144])
            o3 = sb("o3", [P, ND, T])
            kbd3 = sb("kbd3", [P, 2, T])
            vbd3 = sb("vbd3", [P, 2, 4, P])
            st = Dense("c", sb)
            st.pt = sb("pt", [P, 2, 4, T])
            pr = st.prog

            def mat3(name, k=2, n=D):
                return w3[:, W3[name]:W3[name] + k * n].rearrange("p (k n) -> p k n", k=k)

            def vec3(name, n=2):
                return v3[:, V3[name]:V3[name] + n]

            with nc.Block() as block:
                @block.sync
                def _(sp):
                    sp.dma_start(v3[:, :], v3_in).then_inc(w3_loaded, 16)
                    sp.dma_start(w3[:, :], w3_in).then_inc(w3_loaded, 16)

                @block.gpsimd
                def _(pool):
                    nc.gpsimd.memset(st.eps[:, :], EPS).then_inc(pool_done, 1)
                    nc.gpsimd.memset(v3s[:, :, :, :], 0.0).then_inc(pool_done, 1)
                    pool.wait_ge(pool_done, 2)
            end_of_block()

            with nc.Fori(0, B) as b:
                with nc.Block() as block:
                    @block.sync
                    def _(sp):
                        sp.dma_start(x[:, :, :], hs[b].rearrange("p (k t) -> p k t", k=ND)[:, :, KEYS:S2])\
                            .then_inc(x_loaded, 16)
                        sp.dma_start(cx[:, :, :], ctx_in[b].rearrange("p (k t) -> p k t", k=2)).then_inc(x_loaded, 16)
                        sp.wait_ge(dve_done, pr.dve.at("l3 down 1 out"))
                        sp.dma_start(out[b].rearrange("p (k t) -> p k t", k=ND), x[:, :, :]).then_inc(x_stored, 16)
                        sp.wait_ge(x_stored, 16)

                    @block.tensor
                    def _(pe):
                        pe.wait_ge(w3_loaded, 32)
                        pe.wait_ge(x_loaded, 32)
                        st.pe_norm(pe, "nf", None, None, rms=True)
                        bk, emptied = st.lin.take("k4", pr.act, "k4 out")
                        if emptied:
                            pe.wait_ge(*emptied)
                        w = mat3("ck")
                        for j in range(2):
                            for k in range(2):
                                mm = nc.tensor.matmul(bk[:, j * KEYS:(j + 1) * KEYS], w[:, k, j * P:(j + 1) * P],
                                                      cx[:, k, 0:KEYS], start=k == 0, stop=k == 1)
                        mm.then_inc(pe_done, pr.pe.step("k4"))
                        st.pe_norm(pe, "n4", x, (dve_done, pr.dve.at("final norm")))
                        bk, emptied = st.lin.take("v4", pr.dve, "v4 out")
                        if emptied:
                            pe.wait_ge(*emptied)
                        w = mat3("cv")
                        for k in range(2):
                            mm = nc.tensor.matmul(bk[:, 0:D], cx[:, k, :], w[:, k, :], start=k == 0, stop=k == 1)
                        mm.then_inc(pe_done, pr.pe.step("v4"))
                        pe.wait_ge(dve_done, pr.dve.at("n4 out"))
                        st.pe_linear(pe, "q3", mat3("sq"), st.ln, 2, range(2), pr.dve)
                        st.pe_linear(pe, "k3", mat3("sk"), st.ln, 2, range(2), pr.dve)
                        w = mat3("sv")
                        for t in range(NT):
                            bk, emptied = st.lin.take(f"v3 {t}", pr.act, f"v3 {t} out")
                            if emptied:
                                pe.wait_ge(*emptied)
                            for k in range(ND):
                                mm = nc.tensor.matmul(bk[:, 0:D], st.ln[:, k, t * P:(t + 1) * P], w[:, k, :],
                                                      start=k == 0, stop=k == ND - 1)
                            mm.then_inc(pe_done, pr.pe.step(f"v3 {t}"))
                        pe.wait_ge(dve_done, pr.dve.at("k3 1 out"))
                        pe.wait_ge(act_done, pr.act.at(f"v3 {NT - 1} out"))

                        def keys_of(h):
                            rows = slice(32 * (h % 8 // 2), 32 * (h % 8 // 2) + 32)
                            return rows, h // 8, k3[rows, h % 2, h // 8, :]

                        def values_of(h, kt):
                            return (v3s[:, kt, h // 8, P * (h % 8):P * (h % 8) + P], slice(0, P),
                                    h % 8 == 0 and kt == 0, h % 8 == 7 and kt == NT - 1)
                        st.pe_self(pe, "s3", q3, keys_of, values_of, 8)
                        pe.wait_ge(dve_done, pr.dve.at("s3 o 1 out"))
                        st.pe_linear(pe, "o3", mat3("so"), o3, 2, range(2), pr.dve)
                        st.pe_norm(pe, "n5", x, (dve_done, pr.dve.at("o3 1 out")))
                        pe.wait_ge(dve_done, pr.dve.at("n5 out"))
                        st.pe_linear(pe, "q4", mat3("cq"), st.ln, 2, range(2), pr.dve)
                        pe.wait_ge(dve_done, pr.dve.at("q4 1 out"))
                        st.pe_cross(pe, "x3", q3, kbd3, vbd3, False)
                        pe.wait_ge(dve_done, pr.dve.at("x3 o 1 out"))
                        st.pe_linear(pe, "o4", mat3("co"), o3, 2, range(2), pr.dve)
                        st.pe_norm(pe, "n6", x, (dve_done, pr.dve.at("o4 1 out")))
                        st.pe_mlp(pe, "l3", (dve_done, pr.dve.at("n6 out")), mat3("w1", 2, FF), mat3("w2", 8, D), hid)

                    @block.scalar
                    def _(act):
                        act.wait_ge(w3_loaded, 32)
                        act.wait_ge(x_loaded, 32)
                        st.act_norm(act, "nf", x)
                        act.wait_ge(pe_done, pr.pe.at("k4"))
                        for j in range(2):
                            nc.scalar.activation(ksb[:, j, :], st.full("k4")[:, j * KEYS:(j + 1) * KEYS], ACT.Identity,
                                                 bias=vec3("ck")[:, j:j + 1])\
                                .then_inc(act_done, pr.act.step("k4 out" if j else None))
                        st.act_norm(act, "n4")
                        for t in range(NT):
                            act.wait_ge(pe_done, pr.pe.at(f"v3 {t}"))
                            for g in range(2):
                                nc.scalar.activation(
                                    v3s[:, t, g, :].rearrange("p (j c) -> p j c", c=144)[:, :, 0:16],
                                    st.full(f"v3 {t}")[:, g * P:(g + 1) * P].rearrange("p (j d) -> p j d", d=16),
                                    ACT.Copy).then_inc(act_done, pr.act.step(f"v3 {t} out" if g else None))
                        st.act_self(act, "s3")
                        st.act_norm(act, "n5")
                        st.act_cross(act, "x3")
                        st.act_norm(act, "n6")
                        st.act_mlp(act, "l3", vec3("b1", 8), hid)

                    @block.vector
                    def _(dve):
                        dve.wait_ge(act_done, pr.act.at("nf rstd"))
                        for k in range(ND):
                            nc.vector.scalar_tensor_tensor(x[:, k, :], x[:, k, :], vec3("fin")[:, k:k + 1],
                                                           st.rs[:, :], ALU.mult, ALU.mult)\
                                .then_inc(dve_done, pr.dve.step("final norm" if k else None))
                        st.dve_norm(dve, "n4", x, vec3("g1"), vec3("n1"))
                        dve.wait_ge(pe_done, pr.pe.at("v4"))
                        for g in range(2):
                            for hp in range(4):
                                nc.vector.tensor_tensor(
                                    vbd3[:, g, hp, :].rearrange("p (h d) -> p h d", h=8),
                                    st.full("v4")[:, g * P:(g + 1) * P].rearrange("p (h d) -> p h d", h=8),
                                    cst[:, C_MV + 8 * hp:C_MV + 8 * hp + 8].unsqueeze(2).to_broadcast([P, 8, 16]),
                                    ALU.mult).then_inc(dve_done, pr.dve.step("v4 out" if (g, hp) == (1, 3) else None))
                        for j in range(2):
                            dve.wait_ge(pe_done, pr.pe.at(f"q3 {j}"))
                            nc.vector.tensor_scalar(q3[:, j, :], st.full(f"q3 {j}"), vec3("sq")[:, j:j + 1], 0.25,
                                                    ALU.add, ALU.mult).then_inc(dve_done, pr.dve.step(f"q3 {j} out"))
                        for j in range(2):
                            dve.wait_ge(pe_done, pr.pe.at(f"k3 {j}"))
                            for odd in range(2):
                                nc.vector.tensor_scalar(k3[:, odd, j, :], st.full(f"k3 {j}"), vec3("sk")[:, j:j + 1],
                                                        cst[:, C_PAR + odd:C_PAR + odd + 1], ALU.add, ALU.mult)\
                                    .then_inc(dve_done, pr.dve.step(f"k3 {j} out" if odd else None))
                        dve.wait_ge(act_done, pr.act.at("k4 out"))
                        for g in range(2):
                            nc.vector.tensor_tensor(
                                kbd3[:, g, :].rearrange("p (h k) -> p h k", h=8),
                                ksb[:, g, :].unsqueeze(1).to_broadcast([P, 8, KEYS]),
                                cst[:, C_MK:C_MK + 8].unsqueeze(2).to_broadcast([P, 8, KEYS]),
                                ALU.mult).then_inc(dve_done, pr.dve.step())
                        st.dve_self(dve, "s3", 8, o3, vec3("sv"))
                        st.dve_residual(dve, "o3", x, vec3("so"))
                        st.dve_norm(dve, "n5", x, vec3("g2"), vec3("n2"))
                        for j in range(2):
                            dve.wait_ge(pe_done, pr.pe.at(f"q4 {j}"))
                            nc.vector.tensor_scalar(q3[:, j, :], st.full(f"q4 {j}"), vec3("cq")[:, j:j + 1], 0.25,
                                                    ALU.add, ALU.mult).then_inc(dve_done, pr.dve.step(f"q4 {j} out"))
                        st.dve_cross(dve, "x3")
                        for g in range(2):
                            dve.wait_ge(pe_done, pr.pe.at(f"x3 o {g}"))
                            nc.vector.tensor_scalar(o3[:, g, :], st.full(f"x3 o {g}"), vec3("cv")[:, g:g + 1], None,
                                                    ALU.add).then_inc(dve_done, pr.dve.step(f"x3 o {g} out"))
                        st.dve_residual(dve, "o4", x, vec3("co"))
                        st.dve_norm(dve, "n6", x, vec3("g3"), vec3("n3"))
                        st.dve_residual(dve, "l3 down", x, vec3("b2"))

                    @block.gpsimd
                    def _(pool):
                        st.pool_self(pool, "s3")
                        st.pool_cross(pool, "x3")
                found["c"] = pr.result()
                end_of_block()
        return found


def _rows(a, k):
    K, N = a.shape
    if K < k * P:
        a = np.concatenate([a, np.zeros((k * P - K, N), a.dtype)])
    return np.ascontiguousarray(a.reshape(k, P, N).transpose(1, 0, 2).reshape(P, k * N))


def _cols(v):
    return np.ascontiguousarray(v.reshape(-1, P).T)


def _arrays(i):
    g = {k: np.asarray(v) for k, v in i.items()}
    l0 = lambda n: g["L0_xattn_" + n]
    l1 = lambda n: g["L1_xattn_" + n]
    l2 = lambda n: g["L2_xattn_" + n]
    l3 = lambda n: g["L3_xattn_" + n]
    cat = lambda parts: np.ascontiguousarray(np.concatenate(parts, 1))
    p = np.arange(P)[:, None]
    cst = np.concatenate([
        np.eye(P), np.full((P, P), 1.0 / D), p // 16 == np.arange(8)[None],
        (np.arange(8)[None, None] == 2 * np.arange(4)[None, :, None] + (p // 64)[:, :, None]).reshape(P, 32),
        p // 64 == np.arange(2)[None], (p // 16) % 2 == np.arange(2)[None]], 1).astype(np.float32)
    ctx_t = g["ctx_768"].transpose(0, 2, 1)
    ctx = np.stack([_rows(np.concatenate([c, c], 1), 2) for c in ctx_t])
    per_layer = range(L)
    return {
        "x_in": np.stack([_rows(a.T, 2) for a in g["x"]]),
        "ctx_in": ctx,
        "cst_in": cst,
        "w0_in": cat([_rows(l0("Wq"), 2), _rows(l0("Wk"), 2), _rows(l0("Wv"), 2), _rows(l2("pre_w1"), 2),
                      _rows(l2("pre_w2"), 2), _rows(l0("Wo"), 2), _rows(l0("W1"), 2), _rows(l0("W2"), 8)]),
        "w1a_in": cat([_rows(l1("Wq1"), 2), _rows(l1("Wk1"), 2), _rows(l1("Wv1"), 2), _rows(l1("Wo1"), 8)]),
        "w1b_in": cat([_rows(l1("Wq2"), 2), _rows(l1("Wk2"), 2), _rows(l1("Wv2"), 2), _rows(l1("Wo2"), 8),
                       _rows(l1("Wp"), 2), _rows(l1("Wf"), 8)]),
        "v0_in": cat([_cols(l0(n)) for n in ("bq", "bk", "bv", "bo", "ln_g", "ln_b", "b1", "b2")]
                     + [_cols(l1(n)) for n in ("g1", "b1", "bo1", "g2", "b2", "bo2", "g3", "b3", "bp", "bf")]),
        "w2_in": np.stack([cat([_rows(l2("in_proj_w")[n].T, 2), _rows(l2("x_proj_w")[n].T, NE),
                                _rows(l2("dt_proj_w")[n].T, 1), _rows(l2("out_proj_w")[n].T, NE)])
                           for n in per_layer]),
        "v2_in": np.stack([cat([_cols(l2("norm_w")[n]), _rows(l2("conv_w")[n], NE), _cols(l2("conv_b")[n]),
                                _cols(l2("dt_proj_b")[n]), _cols(l2("D_param")[n]), _rows(l2("A_log")[n], NE)])
                           for n in per_layer]),
        "w3_in": cat([_rows(l3(n).T, 2) for n in ("sa_wq", "sa_wk", "sa_wv", "sa_wo", "ca_wq", "ca_wk", "ca_wv",
                                                  "ca_wo", "mlp_w1")] + [_rows(l3("mlp_w2").T, 8)]),
        "v3_in": cat([_cols(l2("final_norm_w"))] + [_cols(l3(n)) for n in (
            "ln1_g", "ln1_b", "ln2_g", "ln2_b", "ln3_g", "ln3_b", "sa_bq", "sa_bk", "sa_bv", "sa_bo",
            "ca_bq", "ca_bk", "ca_bv", "ca_bo", "mlp_b1", "mlp_b2")]),
    }


def kernel(**inputs):
    import concourse.bacc as _bacc
    from concourse.bass_utils import run_bass_kernel_spmd as _run

    arrays = _arrays(inputs)
    known = {}
    for _ in range(2):
        nc = _bacc.Bacc("TRN2", target_bir_lowering=False, num_devices=1)
        args = {n: nc.dram_tensor(n, a.shape, F32, kind="ExternalInput").ap() for n, a in arrays.items()}
        out = nc.dram_tensor("y_out", (B, P, ND * T), F32, kind="ExternalOutput").ap()
        known = build(nc, known, out=out, **args)
    r = _run(nc, [arrays], core_ids=[0])
    y = r.results[0]["y_out"].reshape(B, P, ND, T)
    return np.ascontiguousarray(y.transpose(0, 3, 2, 1).reshape(B, T, D))
```

```python
import numpy as np
from contextlib import ExitStack
import concourse.bass as bass
from concourse import mybir

F32 = mybir.dt.float32
ALU = mybir.AluOpType
ACT = mybir.ActivationFunctionType
AX = mybir.AxisListType

P = 128
B = 4
T = 512
D = 256
H = 16
KEYS = 64
CTX = 192
INNER = 1024
FF = 1024
NT = T // P
ND = D // P
EPS = 1e-5
L = 4
DI = 512
NE = DI // P
DS = 16
DR = 16
S2 = KEYS + T
NX = DR + 2 * DS
BANK = 512
TT = [(s, min(P, S2 - s)) for s in range(0, S2, P)]
EXP_AND_LN = "natural_log_exp_and_others"
SOFTPLUS_LINEAR = 20.0

C_IDENT, C_MEAN = 0, P
C_MK = 2 * P
C_MV = C_MK + 8
C_M64 = C_MV + 32
C_PAR = C_M64 + 2
C_END = C_PAR + 2


def columns(*parts):
    at, out = 0, {}
    for name, n in parts:
        out[name] = at
        at += n
    return out, at


W0, W0N = columns(("q", 2 * D), ("k", 2 * D), ("v", 2 * D), ("p1", 2 * D), ("p2", 2 * D),
                  ("o", 2 * D), ("w1", 2 * FF), ("w2", 8 * D))
W1A, W1AN = columns(("q", 2 * INNER), ("k", 2 * INNER), ("v", 2 * INNER), ("o", 8 * D))
W1B, W1BN = columns(("q", 2 * INNER), ("k", 2 * INNER), ("v", 2 * INNER), ("o", 8 * D),
                    ("p", 4 * FF), ("f", 8 * D))
W2, W2N = columns(("in", 2 * 2 * DI), ("x", NE * NX), ("dt", DI), ("out", NE * D))
W2A = W2["out"]
W3, W3N = columns(("sq", 2 * D), ("sk", 2 * D), ("sv", 2 * D), ("so", 2 * D),
                  ("cq", 2 * D), ("ck", 2 * D), ("cv", 2 * D), ("co", 2 * D),
                  ("w1", 2 * FF), ("w2", 8 * D))
V0, V0N = columns(("q", 2), ("k", 2), ("v", 2), ("o", 2), ("g", 2), ("b", 2), ("b1", 8), ("b2", 2),
                  ("g1", 2), ("n1", 2), ("o1", 2), ("g2", 2), ("n2", 2), ("o2", 2), ("g3", 2), ("n3", 2),
                  ("p", 16), ("f", 2))
V2, V2N = columns(("norm", 2), ("cw", NE * 4), ("cb", NE), ("dtb", NE), ("D", NE), ("A", NE * DS))
V2A = V2["D"]
V3, V3N = columns(("fin", 2), ("g1", 2), ("n1", 2), ("g2", 2), ("n2", 2), ("g3", 2), ("n3", 2),
                  ("sq", 2), ("sk", 2), ("sv", 2), ("so", 2), ("cq", 2), ("ck", 2), ("cv", 2), ("co", 2),
                  ("b1", 8), ("b2", 2))


class Steps:

    def __init__(self, sem, known):
        self.sem, self.known, self.n, self.names = sem, known, 0, {}

    def step(self, name=None):
        self.n += 1
        if name is not None:
            assert name not in self.names, name
            self.names[name] = self.n
        return 1

    def at(self, name):
        return self.known.get(name, 1)


class Program:

    def __init__(self, sems, known):
        self.pe, self.act, self.dve, self.pool = (
            Steps(s, known.get(n, {})) for s, n in zip(sems, ("pe", "act", "dve", "pool")))
        self.where = {}
        self.known_where = known.get("where", {})

    def bank_of(self, job):
        return self.known_where.get(job, 0)

    def result(self):
        return {"pe": self.pe.names, "act": self.act.names, "dve": self.dve.names,
                "pool": self.pool.names, "where": self.where}


class Ring:

    def __init__(self, prog, view, slots):
        self.prog, self.view, self.slots, self.i, self.last = prog, view, slots, 0, [None] * len(slots)

    def take(self, job, steps, emptied):
        k = self.i % len(self.slots)
        self.i += 1
        freed, self.last[k] = self.last[k], (steps.sem, steps.at(emptied))
        self.prog.where[job] = self.slots[k]
        return self.view(self.slots[k]), freed


def build(nc, known, x_in, ctx_in, cst_in, w0_in, w1a_in, w1b_in, v0_in, w2_in, v2_in, w3_in, v3_in, out):
    found = {}
    stack = ExitStack()
    with stack:
        sem = lambda name: stack.enter_context(nc.semaphore(name))
        pe_done, act_done, dve_done, pool_done = (sem(n) for n in ("pe_done", "act_done", "dve_done", "pool_done"))
        engine_sems = (pe_done, act_done, dve_done, pool_done)
        const_loaded, w0_loaded, w1a_loaded, w1b_loaded, w3_loaded = (
            sem(n) for n in ("const_loaded", "w0_loaded", "w1a_loaded", "w1b_loaded", "w3_loaded"))
        x_loaded, x_stored, layer_loaded = sem("x_loaded"), sem("x_stored"), sem("layer_loaded")
        per_block = (*engine_sems, x_loaded, x_stored, layer_loaded)

        hs = nc.dram_tensor("hs", (B, P, ND * S2), F32, kind="Internal").ap()
        psum = stack.enter_context(nc.psum_tensor("psum", [P, 8 * BANK], F32))
        cst = stack.enter_context(nc.sbuf_tensor("cst", [P, C_END], F32))
        ident = cst[:, C_IDENT:C_IDENT + P]
        mean_w = cst[:, C_MEAN:C_MEAN + P]

        def bank(i):
            return psum[:, i * BANK:(i + 1) * BANK]

        def wide(i):
            return psum[:, i * BANK:i * BANK + S2]

        def end_of_block():
            for s in per_block:
                nc.sync.sem_clear(s)
            nc.all_engine_barrier()

        class Dense:

            def __init__(self, name, sb):
                self.prog = prog = Program(engine_sems, known.get(name, {}))
                self.lin = Ring(prog, bank, [0, 1, 2])
                self.scr = Ring(prog, bank, [3, 4, 5])
                self.trn = Ring(prog, bank, [6, 7])
                norm = sb("norm", [P, 2 * ND, T])
                self.dx = norm[:, 0:ND, :]
                self.sq = norm[:, ND:2 * ND, :]
                self.rs = sb("rs", [P, T])
                self.eps = sb("eps", [P, 1])
                self.ln = sb("ln", [P, ND, T])
                self.pr = sb("pr", [P, 6, T])
                self.ptr = (sb("ptr", [P, NT, T]), norm)
                self.mx = sb("mx", [P, 4, H // 2])
                self.sm = sb("sm", [P, 4, H // 2])
                self.ri = sb("ri", [P, 4, H // 2])
                self.nm, self.smh, self.rih = self.mx[:, 0, :], self.sm[:, 0, :], self.ri[:, 0, :]

            def pe_linear(self, pe, name, w, x, nk, tiles, of, width=T):
                p = self.prog
                for j in tiles:
                    b, emptied = self.lin.take(f"{name} {j}", of, f"{name} {j} out")
                    if emptied:
                        pe.wait_ge(*emptied)
                    for k in range(nk):
                        mm = nc.tensor.matmul(b[:, 0:width], w[:, k, j * P:(j + 1) * P], x[:, k, 0:width],
                                              start=k == 0, stop=k == nk - 1)
                    mm.then_inc(pe_done, p.pe.step(f"{name} {j}"))

            def full(self, job):
                return bank(self.prog.bank_of(job))

            def pe_norm(self, pe, name, x, ready, rms=False):
                p = self.prog
                if not rms:
                    pe.wait_ge(*ready)
                    b, emptied = self.lin.take(f"{name} mean", p.dve, f"{name} centred {ND - 1}")
                    if emptied:
                        pe.wait_ge(*emptied)
                    for k in range(ND):
                        mm = nc.tensor.matmul(b, mean_w, x[:, k, :], start=k == 0, stop=k == ND - 1)
                    mm.then_inc(pe_done, p.pe.step(f"{name} mean"))
                b, emptied = self.lin.take(f"{name} var", p.act, f"{name} log")
                if emptied:
                    pe.wait_ge(*emptied)
                for k in range(ND):
                    pe.wait_ge(act_done, p.act.at(f"{name} squares {k}"))
                    mm = nc.tensor.matmul(b, mean_w, self.sq[:, k, :], start=k == 0, stop=k == ND - 1)
                mm.then_inc(pe_done, p.pe.step(f"{name} var"))

            def act_norm(self, act, name, src=None):
                p = self.prog
                nc.scalar.preload_act_table_set(EXP_AND_LN)
                for k in range(ND):
                    if src is None:
                        act.wait_ge(dve_done, p.dve.at(f"{name} centred {k}"))
                    nc.scalar.activation(self.sq[:, k, :], (self.dx if src is None else src)[:, k, :], ACT.Square)\
                        .then_inc(act_done, p.act.step(f"{name} squares {k}"))
                act.wait_ge(pe_done, p.pe.at(f"{name} var"))
                nc.scalar.activation(self.rs[:, :], self.full(f"{name} var"), ACT.Ln, bias=self.eps[:, 0:1])\
                    .then_inc(act_done, p.act.step(f"{name} log"))
                act.wait_ge(act_done, p.act.n)
                nc.scalar.activation(self.rs[:, :], self.rs[:, :], ACT.Exp, scale=-0.5)\
                    .then_inc(act_done, p.act.step(f"{name} rstd"))

            def dve_norm(self, dve, name, x, g, b):
                p = self.prog
                dve.wait_ge(dve_done, p.dve.n)
                dve.wait_ge(pe_done, p.pe.at(f"{name} mean"))
                for k in range(ND):
                    nc.vector.tensor_tensor(self.dx[:, k, :], x[:, k, :], self.full(f"{name} mean"), ALU.subtract)\
                        .then_inc(dve_done, p.dve.step(f"{name} centred {k}"))
                dve.wait_ge(dve_done, p.dve.n)
                dve.wait_ge(act_done, p.act.at(f"{name} rstd"))
                for k in range(ND):
                    nc.vector.scalar_tensor_tensor(self.ln[:, k, :], self.dx[:, k, :], g[:, k:k + 1], self.rs[:, :],
                                                   ALU.mult, ALU.mult).then_inc(dve_done, p.dve.step())
                for k in range(ND):
                    dve.wait_ge(dve_done, p.dve.n - 1)
                    nc.vector.tensor_scalar(self.ln[:, k, :], self.ln[:, k, :], b[:, k:k + 1], None, ALU.add)\
                        .then_inc(dve_done, p.dve.step(f"{name} out" if k == ND - 1 else None))

            def dve_residual(self, dve, name, x, bias):
                p = self.prog
                for j in range(ND):
                    dve.wait_ge(dve_done, p.dve.n)
                    dve.wait_ge(pe_done, p.pe.at(f"{name} {j}"))
                    nc.vector.scalar_tensor_tensor(x[:, j, :], self.full(f"{name} {j}"), bias[:, j:j + 1], x[:, j, :],
                                                   ALU.add, ALU.add).then_inc(dve_done, p.dve.step(f"{name} {j} out"))

            def pe_mlp(self, pe, name, ready, w1, w2, hid):
                p = self.prog
                pe.wait_ge(*ready)
                self.pe_linear(pe, f"{name} up", w1, self.ln, ND, range(FF // P), p.act)
                pe.wait_ge(act_done, p.act.at(f"{name} up {FF // P - 1} out"))
                self.pe_linear(pe, f"{name} down", w2, hid, FF // P, range(ND), p.dve)

            def act_mlp(self, act, name, b1, hid):
                p = self.prog
                for j in range(FF // P):
                    act.wait_ge(pe_done, p.pe.at(f"{name} up {j}"))
                    nc.scalar.activation(hid[:, j, :], self.full(f"{name} up {j}"), ACT.Gelu, bias=b1[:, j:j + 1])\
                        .then_inc(act_done, p.act.step(f"{name} up {j} out"))

            def cross_units(self):
                return [(qt, g) for qt in range(NT) for g in range(2)]

            def pe_cross(self, pe, name, q, kbd, vbd, wide_heads):
                p = self.prog
                units = self.cross_units()

                def scores(u):
                    qt, g = units[u]
                    b, emptied = self.scr.take(f"{name} s {u}", p.dve, f"{name} shifted {u}")
                    if emptied:
                        pe.wait_ge(*emptied)
                    if wide_heads:
                        for f in range(4):
                            mm = nc.tensor.matmul(b[:, f * P:(f + 1) * P], q[:, 4 * g + f, qt * P:(qt + 1) * P],
                                                  kbd[:, 4 * g + f, :], start=True, stop=True)
                    else:
                        mm = nc.tensor.matmul(b, q[:, g, qt * P:(qt + 1) * P], kbd[:, g, :], start=True, stop=True)
                    mm.then_inc(pe_done, p.pe.step(f"{name} s {u}"))

                def flip(u):
                    b, emptied = self.trn.take(f"{name} t {u}", p.act, f"{name} flipped {u}")
                    if emptied:
                        pe.wait_ge(*emptied)
                    pe.wait_ge(pool_done, p.pool.at(f"{name} normed {u}"))
                    for hp in range(4):
                        mm = nc.tensor.transpose(b[:, hp * P:(hp + 1) * P], self.pr[:, u % 6, hp * P:(hp + 1) * P],
                                                 ident)
                    mm.then_inc(pe_done, p.pe.step(f"{name} t {u}"))

                for u in range(len(units) + 3):
                    if u < len(units):
                        scores(u)
                    if u >= 3:
                        flip(u - 3)
                pe.wait_ge(act_done, p.act.at(f"{name} flipped {len(units) - 1}"))
                if wide_heads:
                    for f in range(8):
                        b, emptied = self.lin.take(f"{name} o {f}", p.dve, f"{name} o {f} out")
                        if emptied:
                            pe.wait_ge(*emptied)
                        nc.tensor.matmul(b, vbd[:, f, :], self.pt[:, f // 4, f % 4, :], start=True, stop=True)\
                            .then_inc(pe_done, p.pe.step(f"{name} o {f}"))
                else:
                    for g in range(2):
                        b, emptied = self.lin.take(f"{name} o {g}", p.dve, f"{name} o {g} out")
                        if emptied:
                            pe.wait_ge(*emptied)
                        for hp in range(4):
                            mm = nc.tensor.matmul(b, vbd[:, g, hp, :], self.pt[:, g, hp, :],
                                                  start=hp == 0, stop=hp == 3)
                        mm.then_inc(pe_done, p.pe.step(f"{name} o {g}"))

            def dve_cross(self, dve, name):
                p = self.prog
                n = len(self.cross_units())

                def shift(u):
                    dve.wait_ge(pe_done, p.pe.at(f"{name} s {u}"))
                    s = self.full(f"{name} s {u}").rearrange("p (h k) -> p h k", k=KEYS)
                    dve.wait_ge(dve_done, p.dve.n)
                    nc.vector.tensor_reduce(self.mx[:, u % 4, :], s, AX.X, ALU.max)\
                        .then_inc(dve_done, p.dve.step())
                    dve.wait_ge(dve_done, p.dve.n)
                    if u >= 6:
                        dve.wait_ge(pe_done, p.pe.at(f"{name} t {u - 6}"))
                    nc.vector.tensor_tensor(self.pr[:, u % 6, :].rearrange("p (h k) -> p h k", k=KEYS), s,
                                            self.mx[:, u % 4, :].unsqueeze(2).to_broadcast([P, 8, KEYS]),
                                            ALU.subtract).then_inc(dve_done, p.dve.step(f"{name} shifted {u}"))

                def total(u):
                    dve.wait_ge(act_done, p.act.at(f"{name} exp {u}"))
                    dve.wait_ge(dve_done, p.dve.n)
                    nc.vector.tensor_reduce(self.sm[:, u % 4, :],
                                            self.pr[:, u % 6, :].rearrange("p (h k) -> p h k", k=KEYS),
                                            AX.X, ALU.add).then_inc(dve_done, p.dve.step())
                    dve.wait_ge(dve_done, p.dve.n)
                    nc.vector.reciprocal(self.ri[:, u % 4, :], self.sm[:, u % 4, :])\
                        .then_inc(dve_done, p.dve.step(f"{name} sums {u}"))

                for u in range(n + 1):
                    if u < n:
                        shift(u)
                    if u >= 1:
                        total(u - 1)

            def act_cross(self, act, name):
                p = self.prog
                n = len(self.cross_units())
                for u in range(n + 3):
                    if u < n:
                        act.wait_ge(dve_done, p.dve.at(f"{name} shifted {u}"))
                        nc.scalar.activation(self.pr[:, u % 6, :], self.pr[:, u % 6, :], ACT.Exp)\
                            .then_inc(act_done, p.act.step(f"{name} exp {u}"))
                    if u >= 3:
                        v = u - 3
                        qt, g = self.cross_units()[v]
                        act.wait_ge(pe_done, p.pe.at(f"{name} t {v}"))
                        nc.scalar.activation(self.pt[:, g, :, qt * P:(qt + 1) * P],
                                             self.full(f"{name} t {v}").rearrange("p (h t) -> p h t", h=4), ACT.Copy)\
                            .then_inc(act_done, p.act.step(f"{name} flipped {v}"))

            def pool_cross(self, pool, name):
                p = self.prog
                for u in range(len(self.cross_units())):
                    pool.wait_ge(dve_done, p.dve.at(f"{name} sums {u}"))
                    v = self.pr[:, u % 6, :].rearrange("p (h k) -> p h k", k=KEYS)
                    nc.gpsimd.tensor_tensor(v, v, self.ri[:, u % 4, :].unsqueeze(2).to_broadcast([P, 8, KEYS]),
                                            ALU.mult).then_inc(pool_done, p.pool.step(f"{name} normed {u}"))

            def pe_self(self, pe, name, q, k_of, v_of, per_bank):
                p = self.prog
                banks = {}

                def scores(h, qt):
                    u = NT * h + qt
                    rows, tile, keys = k_of(h)
                    b, emptied = self.scr.take(f"{name} s {u}", p.act, f"{name} exp {u}")
                    if emptied:
                        pe.wait_ge(*emptied)
                    nc.tensor.matmul(b, q[rows, tile, qt * P:(qt + 1) * P], keys, start=True, stop=True)\
                        .then_inc(pe_done, p.pe.step(f"{name} s {u}"))

                def flip(u):
                    b, emptied = self.trn.take(f"{name} t {u}", p.dve, f"{name} flipped {u}")
                    if emptied:
                        pe.wait_ge(*emptied)
                    pe.wait_ge(pool_done, p.pool.at(f"{name} normed {u}"))
                    for kt in range(NT):
                        mm = nc.tensor.transpose(b[:, kt * P:(kt + 1) * P], self.pr[:, u % 6, kt * P:(kt + 1) * P],
                                                 ident)
                    mm.then_inc(pe_done, p.pe.step(f"{name} t {u}"))

                def weigh(h, key_tiles):
                    g = h // per_bank
                    if h % per_bank == 0 and 0 in key_tiles:
                        banks[g], emptied = self.lin.take(f"{name} o {g}", p.dve, f"{name} o {g} out")
                        if emptied:
                            pe.wait_ge(*emptied)
                    if 0 in key_tiles:
                        pe.wait_ge(dve_done, p.dve.at(f"{name} flipped {NT * h + NT - 1}"))
                    for kt in key_tiles:
                        values, rows, first, last = v_of(h, kt)
                        mm = nc.tensor.matmul(banks[g][rows, :], values, self.ptr[h % 2][:, kt, :],
                                              start=first, stop=last)
                    if NT - 1 in key_tiles:
                        mm.then_inc(pe_done, p.pe.step(f"{name} w {h}"))

                for g in range(H + 2):
                    for qt in range(NT):
                        if g < H:
                            scores(g, qt)
                        if 1 <= g <= H:
                            flip(NT * (g - 1) + qt)
                        if g >= 2 and qt % 2:
                            weigh(g - 2, range(qt - 1, qt + 1))

            def dve_self(self, dve, name, per_bank, dst, bias=None):
                p = self.prog
                n = NT * H

                def maximum(u):
                    dve.wait_ge(pe_done, p.pe.at(f"{name} s {u}"))
                    if u >= 8:
                        dve.wait_ge(act_done, p.act.at(f"{name} exp {u - 8}"))
                    nc.vector.tensor_reduce(self.nm[:, u % 8:u % 8 + 1], self.full(f"{name} s {u}"), AX.X, ALU.max,
                                            negate=True).then_inc(dve_done, p.dve.step(f"{name} max {u}"))

                def inverse(u):
                    dve.wait_ge(act_done, p.act.at(f"{name} exp {u}"))
                    if u >= 8:
                        dve.wait_ge(pool_done, p.pool.at(f"{name} normed {u - 8}"))
                    nc.vector.reciprocal(self.rih[:, u % 8:u % 8 + 1], self.smh[:, u % 8:u % 8 + 1])\
                        .then_inc(dve_done, p.dve.step(f"{name} inverse {u}"))

                def flipped(u):
                    h, qt = divmod(u, NT)
                    dve.wait_ge(pe_done, p.pe.at(f"{name} t {u}"))
                    if h >= 2 and qt == 0:
                        dve.wait_ge(pe_done, p.pe.at(f"{name} w {h - 2}"))
                    nc.vector.tensor_copy(self.ptr[h % 2][:, :, qt * P:(qt + 1) * P],
                                          self.full(f"{name} t {u}").rearrange("p (k t) -> p k t", k=NT))\
                        .then_inc(dve_done, p.dve.step(f"{name} flipped {u}"))

                def output(g):
                    dve.wait_ge(pe_done, p.pe.at(f"{name} w {per_bank * g + per_bank - 1}"))
                    if bias is None:
                        nc.vector.tensor_copy(dst[:, g, :], self.full(f"{name} o {g}"))\
                            .then_inc(dve_done, p.dve.step(f"{name} o {g} out"))
                    else:
                        nc.vector.tensor_scalar(dst[:, g, :], self.full(f"{name} o {g}"), bias[:, g:g + 1], None,
                                                ALU.add).then_inc(dve_done, p.dve.step(f"{name} o {g} out"))

                for u in range(n + 2 * NT + 2):
                    if u < n:
                        maximum(u)
                    if 1 <= u <= n:
                        inverse(u - 1)
                    if NT <= u < n + NT:
                        flipped(u - NT)
                    h = (u - 1) // NT - 2 if u % NT == 1 and u > 2 * NT else None
                    if h is not None and h % per_bank == per_bank - 1:
                        output(h // per_bank)

            def act_self(self, act, name):
                p = self.prog
                for u in range(NT * H):
                    act.wait_ge(dve_done, p.dve.at(f"{name} max {u}"))
                    if u >= 6:
                        act.wait_ge(pe_done, p.pe.at(f"{name} t {u - 6}"))
                    if u >= 8:
                        act.wait_ge(dve_done, p.dve.at(f"{name} inverse {u - 8}"))
                    nc.scalar.activation(self.pr[:, u % 6, :], self.full(f"{name} s {u}"), ACT.Exp,
                                         bias=self.nm[:, u % 8:u % 8 + 1], accum_out=self.smh[:, u % 8:u % 8 + 1])\
                        .then_inc(act_done, p.act.step(f"{name} exp {u}"))

            def pool_self(self, pool, name):
                p = self.prog
                for u in range(NT * H):
                    pool.wait_ge(dve_done, p.dve.at(f"{name} inverse {u}"))
                    nc.gpsimd.tensor_scalar(self.pr[:, u % 6, :], self.pr[:, u % 6, :], self.rih[:, u % 8:u % 8 + 1],
                                            1.0, ALU.mult, ALU.mult)\
                        .then_inc(pool_done, p.pool.step(f"{name} normed {u}"))

        with ExitStack() as mem:
            def sb(name, shape):
                return mem.enter_context(nc.sbuf_tensor(f"a_{name}", shape, F32))

            w0, w1a, w1b, v0 = sb("w0", [P, W0N]), sb("w1a", [P, W1AN]), sb("w1b", [P, W1BN]), sb("v0", [P, V0N])
            big = sb("big", [P, 3, 8, T])
            x = sb("x", [P, ND, T])
            cx = sb("ctx", [P, 2, P])
            ksb = sb("ksb", [P, 8, KEYS])
            p1 = sb("p1", [P, 2, KEYS])
            p2 = sb("p2", [P, 2, KEYS])
            st = Dense("a", sb)
            st.pt = big[:, 1, :, :].rearrange("p (g h) t -> p g h t", g=2)
            pr = st.prog

            def mat(t, cols, name, k, n):
                return t[:, cols[name]:cols[name] + k * n].rearrange("p (k n) -> p k n", k=k)

            def vec(name, n=2):
                return v0[:, V0[name]:V0[name] + n]

            hid = big[:, 2, :, :]
            q1 = big[:, 0, :, :]
            k1 = big[:, 1, :, :]
            v1 = big[:, 2, :, :].rearrange("p (t a) c -> p t (a c)", t=NT)
            q0 = big[:, 0, 0:2, :]
            kbd0 = big[:, 0, 2:4, :]
            vbd0 = big[:, 0, 4:6, :].rearrange("p g (h m) -> p g h m", h=4)
            o0 = big[:, 0, 6:8, :]
            a0 = big[:, 1, 0:2, :]
            kbd1 = big[:, 2, 0:2, :].rearrange("p a (f m) -> p (a f) m", m=P)
            vbd1 = big[:, 2, 2:4, :].rearrange("p a (f m) -> p (a f) m", m=P)

            with nc.Block() as block:
                @block.sync
                def _(sp):
                    sp.dma_start(cst[:, :], cst_in).then_inc(const_loaded, 16)
                    sp.dma_start(v0[:, :], v0_in).then_inc(const_loaded, 16)
                    sp.dma_start(w0[:, :], w0_in).then_inc(w0_loaded, 16)

                @block.gpsimd
                def _(pool):
                    nc.gpsimd.memset(st.eps[:, :], EPS).then_inc(pool_done, 1)
                    pool.wait_ge(pool_done, 1)
            end_of_block()

            nc.gpsimd.wait_ge(w0_loaded, 16)
            nc.gpsimd.dma_start(w1a[:, :], w1a_in).then_inc(w1a_loaded, 16)
            nc.gpsimd.dma_start(w1b[:, :], w1b_in).then_inc(w1b_loaded, 16)

            with nc.Fori(0, B) as b:
                with nc.Block() as block:
                    @block.sync
                    def _(sp):
                        sp.dma_start(x[:, :, :], x_in[b].rearrange("p (k t) -> p k t", k=ND)).then_inc(x_loaded, 16)
                        sp.dma_start(cx[:, :, :], ctx_in[b].rearrange("p (k t) -> p k t", k=2)).then_inc(x_loaded, 16)
                        h_out = hs[b].rearrange("p (k t) -> p k t", k=ND)
                        sp.wait_ge(act_done, pr.act.at("pre2 out"))
                        sp.dma_start(h_out[:, :, 0:KEYS], p2[:, :, :]).then_inc(x_stored, 16)
                        sp.wait_ge(dve_done, pr.dve.at("l1 down 1 out"))
                        sp.dma_start(h_out[:, :, KEYS:S2], x[:, :, :]).then_inc(x_stored, 16)
                        sp.wait_ge(x_stored, 32)

                    @block.tensor
                    def _(pe):
                        pe.wait_ge(const_loaded, 32)
                        pe.wait_ge(w0_loaded, 16)
                        pe.wait_ge(x_loaded, 32)
                        bk, emptied = st.lin.take("pre1", pr.act, "pre1 out")
                        if emptied:
                            pe.wait_ge(*emptied)
                        w = mat(w0, W0, "p1", 2, D)
                        for j in range(2):
                            for k in range(2):
                                mm = nc.tensor.matmul(bk[:, j * KEYS:(j + 1) * KEYS], w[:, k, j * P:(j + 1) * P],
                                                      cx[:, k, 0:KEYS], start=k == 0, stop=k == 1)
                        mm.then_inc(pe_done, pr.pe.step("pre1"))
                        bk, emptied = st.lin.take("k0", pr.act, "k0 out")
                        if emptied:
                            pe.wait_ge(*emptied)
                        w = mat(w0, W0, "k", 2, D)
                        for j in range(2):
                            for k in range(2):
                                mm = nc.tensor.matmul(bk[:, j * KEYS:(j + 1) * KEYS], w[:, k, j * P:(j + 1) * P],
                                                      cx[:, k, 0:KEYS], start=k == 0, stop=k == 1)
                        mm.then_inc(pe_done, pr.pe.step("k0"))
                        bk, emptied = st.lin.take("v0", pr.dve, "v0 out")
                        if emptied:
                            pe.wait_ge(*emptied)
                        w = mat(w0, W0, "v", 2, D)
                        for k in range(2):
                            mm = nc.tensor.matmul(bk[:, 0:D], cx[:, k, :], w[:, k, :], start=k == 0, stop=k == 1)
                        mm.then_inc(pe_done, pr.pe.step("v0"))
                        st.pe_linear(pe, "q0", mat(w0, W0, "q", 2, D), x, 2, range(2), pr.dve)
                        pe.wait_ge(act_done, pr.act.at("pre1 out"))
                        bk, emptied = st.lin.take("pre2", pr.act, "pre2 out")
                        if emptied:
                            pe.wait_ge(*emptied)
                        w = mat(w0, W0, "p2", 2, D)
                        for j in range(2):
                            for k in range(2):
                                mm = nc.tensor.matmul(bk[:, j * KEYS:(j + 1) * KEYS], w[:, k, j * P:(j + 1) * P],
                                                      p1[:, k, :], start=k == 0, stop=k == 1)
                        mm.then_inc(pe_done, pr.pe.step("pre2"))
                        pe.wait_ge(dve_done, pr.dve.at("q0 1 out"))
                        pe.wait_ge(dve_done, pr.dve.at("kbd0"))
                        st.pe_cross(pe, "x0", q0, kbd0, vbd0, False)
                        pe.wait_ge(dve_done, pr.dve.at("x0 o 1 out"))
                        st.pe_linear(pe, "o0", mat(w0, W0, "o", 2, D), o0, 2, range(2), pr.act)
                        st.pe_norm(pe, "n0", a0, (act_done, pr.act.at("o0 1 out")))
                        st.pe_mlp(pe, "l0", (dve_done, pr.dve.at("n0 out")), mat(w0, W0, "w1", 2, FF), mat(w0, W0, "w2", 8, D), hid)
                        st.pe_norm(pe, "n1", x, (dve_done, pr.dve.at("x0 sum")))
                        pe.wait_ge(w1a_loaded, 16)
                        pe.wait_ge(dve_done, pr.dve.at("n1 out"))
                        st.pe_linear(pe, "q1", mat(w1a, W1A, "q", 2, INNER), st.ln, 2, range(8), pr.act)
                        st.pe_linear(pe, "k1", mat(w1a, W1A, "k", 2, INNER), st.ln, 2, range(8), pr.act)
                        w = mat(w1a, W1A, "v", 2, INNER)
                        for t in range(NT):
                            for c in range(2):
                                bk, emptied = st.lin.take(f"v1 {t} {c}", pr.dve, f"v1 {t} {c} out")
                                if emptied:
                                    pe.wait_ge(*emptied)
                                for k in range(ND):
                                    mm = nc.tensor.matmul(bk, st.ln[:, k, t * P:(t + 1) * P], w[:, k, c * T:(c + 1) * T],
                                                          start=k == 0, stop=k == ND - 1)
                                mm.then_inc(pe_done, pr.pe.step(f"v1 {t} {c}"))
                        pe.wait_ge(act_done, pr.act.at("k1 7 out"))
                        pe.wait_ge(dve_done, pr.dve.at(f"v1 {NT - 1} 1 out"))

                        def keys_of(h):
                            rows = slice(64 * (h % 2), 64 * (h % 2) + 64)
                            return rows, h // 2, k1[rows, h // 2, :]

                        def values_of(h, kt):
                            return (v1[:, kt, 64 * h:64 * h + 64], slice(64 * (h % 2), 64 * (h % 2) + 64),
                                    kt == 0, kt == NT - 1)
                        st.pe_self(pe, "s1", q1, keys_of, values_of, 2)
                        pe.wait_ge(dve_done, pr.dve.at("s1 o 7 out"))
                        st.pe_linear(pe, "o1", mat(w1a, W1A, "o", 8, D), q1, 8, range(2), pr.dve)
                        pe.wait_ge(w1b_loaded, 16)
                        bk, emptied = st.lin.take("k2", pr.act, "k2 out")
                        if emptied:
                            pe.wait_ge(*emptied)
                        w = mat(w1b, W1B, "k", 2, INNER)
                        for j in range(8):
                            for k in range(2):
                                mm = nc.tensor.matmul(bk[:, j * KEYS:(j + 1) * KEYS], w[:, k, j * P:(j + 1) * P],
                                                      cx[:, k, 0:KEYS], start=k == 0, stop=k == 1)
                        mm.then_inc(pe_done, pr.pe.step("k2"))
                        st.pe_norm(pe, "n2", x, (dve_done, pr.dve.at("o1 1 out")))
                        w = mat(w1b, W1B, "v", 2, INNER)
                        for c in range(2):
                            bk, emptied = st.lin.take(f"v2 {c}", pr.dve, f"v2 {c} out")
                            if emptied:
                                pe.wait_ge(*emptied)
                            for k in range(2):
                                mm = nc.tensor.matmul(bk, cx[:, k, :], w[:, k, c * T:(c + 1) * T], start=k == 0, stop=k == 1)
                            mm.then_inc(pe_done, pr.pe.step(f"v2 {c}"))
                        pe.wait_ge(dve_done, pr.dve.at("n2 out"))
                        st.pe_linear(pe, "q2", mat(w1b, W1B, "q", 2, INNER), st.ln, 2, range(8), pr.act)
                        pe.wait_ge(act_done, pr.act.at("q2 7 out"))
                        pe.wait_ge(dve_done, pr.dve.at("v2 1 out"))
                        st.pe_cross(pe, "x2", q1, kbd1, vbd1, True)
                        pe.wait_ge(dve_done, pr.dve.at("x2 o 7 out"))
                        st.pe_linear(pe, "o2", mat(w1b, W1B, "o", 8, D), q1, 8, range(2), pr.dve)
                        st.pe_norm(pe, "n3", x, (dve_done, pr.dve.at("o2 1 out")))
                        pe.wait_ge(dve_done, pr.dve.at("n3 out"))
                        w = mat(w1b, W1B, "p", 2, 2 * FF)
                        for j in range(8):
                            st.pe_linear(pe, "l1 gate", w, st.ln, 2, [8 + j], pr.act)
                            st.pe_linear(pe, "l1 up", w, st.ln, 2, [j], pr.dve)
                        pe.wait_ge(dve_done, pr.dve.at("l1 up 7 out"))
                        st.pe_linear(pe, "l1 down", mat(w1b, W1B, "f", 8, D), hid, 8, range(2), pr.dve)

                    @block.scalar
                    def _(act):
                        act.wait_ge(const_loaded, 32)
                        act.wait_ge(pe_done, pr.pe.at("pre1"))
                        nc.scalar.activation(p1[:, :, :], st.full("pre1")[:, 0:2 * KEYS].rearrange("p (k t) -> p k t", k=2),
                                             ACT.Silu).then_inc(act_done, pr.act.step("pre1 out"))
                        act.wait_ge(pe_done, pr.pe.at("k0"))
                        for j in range(2):
                            nc.scalar.activation(ksb[:, j, :], st.full("k0")[:, j * KEYS:(j + 1) * KEYS], ACT.Identity,
                                                 bias=vec("k")[:, j:j + 1])\
                                .then_inc(act_done, pr.act.step("k0 out" if j else None))
                        act.wait_ge(pe_done, pr.pe.at("pre2"))
                        nc.scalar.activation(p2[:, :, :], st.full("pre2")[:, 0:2 * KEYS].rearrange("p (k t) -> p k t", k=2),
                                             ACT.Copy).then_inc(act_done, pr.act.step("pre2 out"))
                        st.act_cross(act, "x0")
                        for j in range(2):
                            act.wait_ge(pe_done, pr.pe.at(f"o0 {j}"))
                            nc.scalar.activation(a0[:, j, :], st.full(f"o0 {j}"), ACT.Identity, bias=vec("o")[:, j:j + 1])\
                                .then_inc(act_done, pr.act.step(f"o0 {j} out"))
                        st.act_norm(act, "n0")
                        st.act_mlp(act, "l0", vec("b1", 8), hid)
                        st.act_norm(act, "n1")
                        for j in range(8):
                            act.wait_ge(pe_done, pr.pe.at(f"q1 {j}"))
                            nc.scalar.activation(q1[:, j, :], st.full(f"q1 {j}"), ACT.Copy, scale=0.125)\
                                .then_inc(act_done, pr.act.step(f"q1 {j} out"))
                        for j in range(8):
                            act.wait_ge(pe_done, pr.pe.at(f"k1 {j}"))
                            nc.scalar.activation(k1[:, j, :], st.full(f"k1 {j}"), ACT.Copy)\
                                .then_inc(act_done, pr.act.step(f"k1 {j} out"))
                        st.act_self(act, "s1")
                        act.wait_ge(pe_done, pr.pe.at("k2"))
                        nc.scalar.activation(ksb[:, :, :], st.full("k2").rearrange("p (f k) -> p f k", f=8), ACT.Copy)\
                            .then_inc(act_done, pr.act.step("k2 out"))
                        st.act_norm(act, "n2")
                        for j in range(8):
                            act.wait_ge(pe_done, pr.pe.at(f"q2 {j}"))
                            nc.scalar.activation(q1[:, j, :], st.full(f"q2 {j}"), ACT.Copy, scale=0.125)\
                                .then_inc(act_done, pr.act.step(f"q2 {j} out"))
                        st.act_cross(act, "x2")
                        st.act_norm(act, "n3")
                        for j in range(8):
                            act.wait_ge(pe_done, pr.pe.at(f"l1 gate {8 + j}"))
                            if j >= 3:
                                act.wait_ge(dve_done, pr.dve.at(f"l1 up {j - 3} out"))
                            nc.scalar.activation(st.pr[:, j % 3, :], st.full(f"l1 gate {8 + j}"), ACT.Gelu,
                                                 bias=vec("p", 16)[:, 8 + j:9 + j])\
                                .then_inc(act_done, pr.act.step(f"l1 gate {8 + j} out"))

                    @block.vector
                    def _(dve):
                        dve.wait_ge(const_loaded, 32)
                        dve.wait_ge(pe_done, pr.pe.at("v0"))
                        for g in range(2):
                            for hp in range(4):
                                nc.vector.tensor_tensor(
                                    vbd0[:, g, hp, :].rearrange("p (h d) -> p h d", h=8),
                                    st.full("v0")[:, g * P:(g + 1) * P].rearrange("p (h d) -> p h d", h=8),
                                    cst[:, C_MV + 8 * hp:C_MV + 8 * hp + 8].unsqueeze(2).to_broadcast([P, 8, 16]),
                                    ALU.mult).then_inc(dve_done, pr.dve.step("v0 out" if (g, hp) == (1, 3) else None))
                        for j in range(2):
                            dve.wait_ge(pe_done, pr.pe.at(f"q0 {j}"))
                            nc.vector.tensor_scalar(q0[:, j, :], st.full(f"q0 {j}"), vec("q")[:, j:j + 1], 0.25,
                                                    ALU.add, ALU.mult).then_inc(dve_done, pr.dve.step(f"q0 {j} out"))
                        dve.wait_ge(act_done, pr.act.at("k0 out"))
                        for g in range(2):
                            nc.vector.tensor_tensor(
                                kbd0[:, g, :].rearrange("p (h k) -> p h k", h=8),
                                ksb[:, g, :].unsqueeze(1).to_broadcast([P, 8, KEYS]),
                                cst[:, C_MK:C_MK + 8].unsqueeze(2).to_broadcast([P, 8, KEYS]),
                                ALU.mult).then_inc(dve_done, pr.dve.step("kbd0" if g else None))
                        st.dve_cross(dve, "x0")
                        for g in range(2):
                            dve.wait_ge(pe_done, pr.pe.at(f"x0 o {g}"))
                            nc.vector.tensor_scalar(o0[:, g, :], st.full(f"x0 o {g}"), vec("v")[:, g:g + 1], None, ALU.add)\
                                .then_inc(dve_done, pr.dve.step(f"x0 o {g} out"))
                        st.dve_norm(dve, "n0", a0, vec("g"), vec("b"))
                        for j in range(2):
                            dve.wait_ge(dve_done, pr.dve.n)
                            dve.wait_ge(act_done, pr.act.at(f"o0 {j} out"))
                            nc.vector.tensor_tensor(x[:, j, :], x[:, j, :], a0[:, j, :], ALU.add)\
                                .then_inc(dve_done, pr.dve.step())
                        st.dve_residual(dve, "l0 down", x, vec("b2"))
                        pr.dve.names["x0 sum"] = pr.dve.n
                        st.dve_norm(dve, "n1", x, vec("g1"), vec("n1"))
                        for t in range(NT):
                            for c in range(2):
                                dve.wait_ge(pe_done, pr.pe.at(f"v1 {t} {c}"))
                                nc.vector.tensor_copy(v1[:, t, c * T:(c + 1) * T], st.full(f"v1 {t} {c}"))\
                                    .then_inc(dve_done, pr.dve.step(f"v1 {t} {c} out"))
                        st.dve_self(dve, "s1", 2, q1)
                        st.dve_residual(dve, "o1", x, vec("o1"))
                        dve.wait_ge(act_done, pr.act.at("k2 out"))
                        nc.vector.tensor_tensor(
                            kbd1.rearrange("p f (h k) -> p f h k", h=2),
                            ksb[:, :, :].unsqueeze(2).to_broadcast([P, 8, 2, KEYS]),
                            cst[:, C_M64:C_M64 + 2].unsqueeze(1).unsqueeze(3).to_broadcast([P, 8, 2, KEYS]),
                            ALU.mult).then_inc(dve_done, pr.dve.step())
                        st.dve_norm(dve, "n2", x, vec("g2"), vec("n2"))
                        for c in range(2):
                            dve.wait_ge(pe_done, pr.pe.at(f"v2 {c}"))
                            nc.vector.tensor_tensor(
                                vbd1[:, 4 * c:4 * c + 4, :].rearrange("p f (h d) -> p f h d", h=2),
                                st.full(f"v2 {c}").rearrange("p (f h d) -> p f h d", h=2, d=64),
                                cst[:, C_M64:C_M64 + 2].unsqueeze(1).unsqueeze(3).to_broadcast([P, 4, 2, 64]),
                                ALU.mult).then_inc(dve_done, pr.dve.step(f"v2 {c} out"))
                        st.dve_cross(dve, "x2")
                        for f in range(8):
                            dve.wait_ge(pe_done, pr.pe.at(f"x2 o {f}"))
                            nc.vector.tensor_copy(q1[:, f, :], st.full(f"x2 o {f}"))\
                                .then_inc(dve_done, pr.dve.step(f"x2 o {f} out"))
                        st.dve_residual(dve, "o2", x, vec("o2"))
                        st.dve_norm(dve, "n3", x, vec("g3"), vec("n3"))
                        for j in range(8):
                            dve.wait_ge(act_done, pr.act.at(f"l1 gate {8 + j} out"))
                            dve.wait_ge(pe_done, pr.pe.at(f"l1 up {j}"))
                            nc.vector.scalar_tensor_tensor(hid[:, j, :], st.full(f"l1 up {j}"), vec("p", 16)[:, j:j + 1],
                                                           st.pr[:, j % 3, :], ALU.add, ALU.mult)\
                                .then_inc(dve_done, pr.dve.step(f"l1 up {j} out"))
                        st.dve_residual(dve, "l1 down", x, vec("f"))

                    @block.gpsimd
                    def _(pool):
                        st.pool_cross(pool, "x0")
                        st.pool_self(pool, "s1")
                        st.pool_cross(pool, "x2")
                found["a"] = pr.result()
                end_of_block()

        with ExitStack() as mem:
            def sb(name, shape):
                return mem.enter_context(nc.sbuf_tensor(f"m_{name}", shape, F32))

            AHEAD = 6
            IN, XD, DTP, SP, Z, UT = 14, 26, 31, 40, 37, 57
            wa, va = sb("wa", [P, W2A]), sb("va", [P, V2A])
            wb, vb = sb("wb", [P, W2N - W2A]), sb("vb", [P, V2N - V2A])
            h = sb("h", [P, B, ND, S2])
            xc = sb("xc", [P, NE, 3 + S2])
            cv = sb("cv", [P, NE, S2])
            xi = sb("xi", [P, 2, NE, S2])
            zs = sb("zs", [P, 2, NE, S2])
            dt = sb("dt", [P, 2, NE, S2])
            bc = sb("bc", [P, 2, len(TT), NX])
            spe = sb("spe", [P, NE, S2])
            spl, spu = sb("spl", [P, 2, S2]), sb("spu", [P, 2, S2])
            sq, rs, xd = spe[:, 0:ND, :], spl[:, 0, :], spu[0:NX, 0, :]
            ut = sb("ut", [P, len(TT), DI])
            xn = sb("xn", [P, ND, S2])
            ub = sb("ub", [P, 2, len(TT), DI])
            da = sb("da", [P, AHEAD, S2])
            hh = sb("hh", [P, 2, NE, S2])
            yt = sb("yt", [P, len(TT), DI])
            ys = sb("ys", [P, 2, DI])
            am = sb("am", [P, NE * DS])
            eps2 = sb("eps", [P, 1])

            SHARED = 3
            ORDER = (0, 1, 2, 4, SHARED)
            LAST = DS - 1
            HALVES = ((0, BANK), (BANK, S2))

            def mat2(name, k, n):
                t, at = (wa, W2[name]) if W2[name] < W2A else (wb, W2[name] - W2A)
                return t[:, at:at + k * n].rearrange("p (k n) -> p k n", k=k)

            def vec2(name, i):
                t, at = (va, V2[name]) if V2[name] < V2A else (vb, V2[name] - V2A)
                return t[:, at + i:at + i + 1]

            def mamba(name, mains, last_item, first_loads, next_loads, store):
                pr = Program(engine_sems, known.get(name, {}))
                wring, sring, tring = Ring(pr, wide, [0, 2]), Ring(pr, wide, [4]), Ring(pr, bank, [6, 7])
                full = lambda job: wide(pr.bank_of(job))
                steps = [(i, n) for i in mains for n in range(DS)]

                def sides(i, n):
                    return (i - 1 if i - 1 in mains else None), (i + 1 if i + 1 <= last_item else None)

                alone = [(mains[-1] + 1 if mains else -1, q) for q in range(NE * DS)]

                with nc.Block() as block:
                    @block.sync
                    def _(sp):
                        for dst, src in first_loads:
                            sp.dma_start(dst, src).then_inc(x_loaded, 16)
                        if next_loads:
                            sp.wait_ge(dve_done, pr.dve.at(f"{B - 1} dt {NE - 1}"))
                            sp.wait_ge(pe_done, pr.pe.at(f"{B - 1} in {2 * NE - 1}"))
                            for dst, src in next_loads:
                                sp.dma_start(dst, src).then_inc(layer_loaded, 16)
                        if store:
                            for i in mains:
                                sp.wait_ge(dve_done, pr.dve.at(f"{i} h 1"))
                                sp.dma_start(hs[i].rearrange("p (k t) -> p k t", k=ND), h[:, i, :, :])\
                                    .then_inc(x_stored, 16)
                            sp.wait_ge(x_stored, 16 * len(mains))
                        sp.wait_ge(x_loaded, 16 * len(first_loads))

                    @block.tensor
                    def _(pe):
                        def product(job, of, emptied, pairs, first, end, m=P):
                            if first == 0:
                                s, freed = sring.take(job, of, emptied)
                                if freed:
                                    pe.wait_ge(*freed)
                            s, n = full(job), len(pairs)
                            for lo, hi in HALVES:
                                for k in range(first, end):
                                    lhs, rhs = pairs[k]
                                    mm = nc.tensor.matmul(s[0:m, lo:hi], lhs, rhs[:, lo:hi],
                                                          start=k == 0, stop=k == n - 1)
                            if end == n:
                                mm.then_inc(pe_done, pr.pe.step(job))

                        def in_proj(i, j, k):
                            if j == 0 and k == 0:
                                pe.wait_ge(dve_done, pr.dve.at(f"{i} xn"))
                            w = mat2("in", ND, 2 * DI)
                            product(f"{i} in {j}", pr.act, f"{i} in {j} out",
                                    [(w[:, k, j * P:(j + 1) * P], xn[:, k, :]) for k in range(ND)], k, k + 1)

                        def x_proj(i, e):
                            if e == 0:
                                pe.wait_ge(act_done, pr.act.at(f"{i} xi {NE - 1}"))
                            w = mat2("x", NE, NX)
                            product(f"{i} xd", pr.dve, f"{i} xd",
                                    [(w[:, e, :], xi[:, i % 2, e, :]) for e in range(NE)], e, e + 1, m=NX)

                        def dt_proj(i, e):
                            if e == 0:
                                pe.wait_ge(dve_done, pr.dve.at(f"{i} xd"))
                            product(f"{i} dt {e}", pr.act, f"{i} dt {e} in",
                                    [(wa[0:DR, W2["dt"] + e * P:W2["dt"] + (e + 1) * P], xd[0:DR, :])], 0, 1)

                        def out_proj(i, j, e):
                            if j == 0 and e == 0:
                                pe.wait_ge(dve_done, pr.dve.at(f"{i} yg 1"))
                            if j == 0 and e == 2:
                                pe.wait_ge(pool_done, pr.pool.at(f"{i} yg {NE - 1}"))
                            w = mat2("out", NE, D)
                            product(f"{i} out {j}", pr.dve, f"{i} h {j}",
                                    [(w[:, e, j * P:(j + 1) * P], cv[:, e, :]) for e in range(NE)], e, e + 2)

                        def y_back(i, e):
                            job = f"{i} yf {e}"
                            if e % 2:
                                freed = list(tring.last)
                                tring.last = [(pr.dve.sem, pr.dve.at(f"{i} yd {e}"))] * 2
                                pr.where[job] = 6
                                s = wide(6)
                                for f in freed:
                                    pe.wait_ge(*f)
                            else:
                                s, freed = sring.take(job, pr.dve, f"{i} yd {e}")
                                if freed:
                                    pe.wait_ge(*freed)
                            if e == 0:
                                pe.wait_ge(dve_done, pr.dve.at(f"{i} y {LAST} {SHARED}"))
                            for t, (t0, m) in enumerate(TT):
                                mm = nc.tensor.transpose(s[:, t0:t0 + m], yt[0:m, t, e * P:(e + 1) * P],
                                                         ident[0:m, 0:m])
                            mm.then_inc(pe_done, pr.pe.step(job))

                        def u_turn(i, pair):
                            tiles = list(enumerate(TT))[2 * pair:2 * pair + 2]
                            s, emptied = sring.take(f"{i} ut {pair}", pr.act, f"{i} ut {tiles[-1][0]} out")
                            pe.wait_ge(*emptied)
                            for t, (t0, m) in tiles:
                                for e in range(NE):
                                    mm = nc.tensor.transpose(
                                        psum[0:m, (4 + t % 2) * BANK + e * P:(4 + t % 2) * BANK + (e + 1) * P],
                                        cv[:, e, t0:t0 + m], ident)
                            mm.then_inc(pe_done, pr.pe.step(f"{i} ut {pair}"))

                        def side(q, post, pre):
                            if post is not None:
                                if q == 3:
                                    for e in range(NE):
                                        y_back(post, e)
                                for j, at in ((0, 5), (1, 9)):
                                    if q == at:
                                        out_proj(post, j, 0)
                                    if q == at + 2:
                                        out_proj(post, j, 2)
                            if pre is not None:
                                if q == 4:
                                    pe.wait_ge(act_done, pr.act.at(f"{pre} squares"))
                                    product(f"{pre} var", pr.act, f"{pre} log",
                                            [(mean_w, sq[:, j, :]) for j in range(ND)], 0, ND)
                                if IN <= q < IN + 2 * NE:
                                    in_proj(pre, (q - IN) // 2, (q - IN) % 2)
                                if XD <= q < XD + NE:
                                    x_proj(pre, q - XD)
                                if DTP <= q < DTP + NE:
                                    dt_proj(pre, q - DTP)
                                if q == DTP + NE:
                                    s, emptied = sring.take(f"{pre} bc", pr.dve, f"{pre} bc out")
                                    pe.wait_ge(*emptied)
                                    for t, (t0, m) in enumerate(TT):
                                        mm = nc.tensor.transpose(s[0:m, t * NX:(t + 1) * NX], xd[:, t0:t0 + m],
                                                                 ident[0:NX, 0:NX])
                                    mm.then_inc(pe_done, pr.pe.step(f"{pre} bc"))
                                if Z <= q < Z + 4 * NE and (q - Z) % 4 < 2:
                                    in_proj(pre, NE + (q - Z) // 4, (q - Z) % 4)
                                if q == UT:
                                    pe.wait_ge(pool_done, pr.pool.at(f"{pre} u {NE - 2}"))
                                    pe.wait_ge(dve_done, pr.dve.at(f"{pre} u {NE - 1}"))
                                for pair, at in enumerate((UT, UT + 2, UT + 3)):
                                    if q == at:
                                        u_turn(pre, pair)

                        def state_input(i, n, e):
                            if e == 0:
                                pe.wait_ge(pool_done, pr.pool.at(f"{i} ub {n}"))
                            s, emptied = wring.take(f"{i} db {n} {e}", pr.dve, f"{i} scan {n} {e}")
                            if emptied:
                                pe.wait_ge(*emptied)
                            for t, (t0, m) in enumerate(TT):
                                mm = nc.tensor.transpose(s[:, t0:t0 + m], ub[0:m, n % 2, t, e * P:(e + 1) * P],
                                                         ident[0:m, 0:m])
                            mm.then_inc(pe_done, pr.pe.step(f"{i} db {n} {e}"))

                        def output(i, n, t):
                            t0, m = TT[t]
                            if t == ORDER[0]:
                                pe.wait_ge(dve_done, pr.dve.at(f"{i} scan {n} {NE - 1}"))
                            by = (pr.act, f"{i} ys {n}") if t == SHARED and n < LAST else (pr.dve, f"{i} y {n} {t}")
                            s, emptied = tring.take(f"{i} ht {n} {t}", *by)
                            if emptied:
                                pe.wait_ge(*emptied)
                            for e in range(NE):
                                mm = nc.tensor.transpose(s[0:m, e * P:(e + 1) * P], hh[:, n % 2, e, t0:t0 + m], ident)
                            mm.then_inc(pe_done, pr.pe.step(f"{i} ht {n} {t}"))

                        before = None
                        for i, n in steps:
                            for e in range(NE):
                                state_input(i, n, e)
                                if before:
                                    output(*before, ORDER[e])
                                if before and e == NE - 1:
                                    output(*before, SHARED)
                                side(NE * n + e, *sides(i, n))
                            before = (i, n)
                        if before:
                            for t in ORDER:
                                output(*before, t)
                        else:
                            pe.wait_ge(x_loaded, 16 * len(first_loads))
                        for i, q in alone:
                            side(q, *sides(i, q))

                    @block.scalar
                    def _(act):
                        def decay(i, n, e):
                            u = NE * (DS * i + n) + e
                            if i and n == 0:
                                act.wait_ge(dve_done, pr.dve.at(f"{i} dt {e}"))
                            if u >= AHEAD:
                                s, before = divmod(u - AHEAD, NE)
                                act.wait_ge(dve_done, pr.dve.at(f"{s // DS} scan {s % DS} {before}"))
                            nc.scalar.activation(da[:, u % AHEAD, :], dt[:, i % 2, e, :], ACT.Exp,
                                                 scale=am[:, e * DS + n:e * DS + n + 1])\
                                .then_inc(act_done, pr.act.step(f"{i} da {n} {e}"))

                        def scaled(i, n):
                            if n == LAST:
                                return
                            if n == 0 and i:
                                act.wait_ge(pe_done, pr.pe.at(f"{i - 1} yf {NE - 1}"))
                            if n >= 3:
                                act.wait_ge(pool_done, pr.pool.at(f"{i} y {n - 2} {SHARED}"))
                            act.wait_ge(pe_done, pr.pe.at(f"{i} ht {n} {SHARED}"))
                            dst = yt[:, SHARED, :] if n == 0 else ys[:, n % 2, :]
                            nc.scalar.activation(dst, bank(pr.bank_of(f"{i} ht {n} {SHARED}")), ACT.Identity,
                                                 scale=bc[:, i % 2, SHARED, DR + DS + n:DR + DS + n + 1], bias=0.0)\
                                .then_inc(act_done, pr.act.step(f"{i} ys {n}"))

                        def in_out(i, j):
                            act.wait_ge(pe_done, pr.pe.at(f"{i} in {j}"))
                            if j < NE:
                                if j == 0 and i - 2 in mains:
                                    act.wait_ge(pe_done, pr.pe.at(f"{i - 2} out 1"))
                                nc.scalar.activation(xc[:, j, 3:3 + S2], full(f"{i} in {j}"), ACT.Copy)\
                                    .then_inc(act_done, pr.act.step(f"{i} in {j} out"))
                                act.wait_ge(act_done, pr.act.n)
                                nc.scalar.activation(cv[:, j, :], xc[:, j, 0:S2], ACT.Identity,
                                                     bias=vec2("cb", j), scale=vec2("cw", 4 * j))\
                                    .then_inc(act_done, pr.act.step(f"{i} tap {j}"))
                            else:
                                nc.scalar.activation(zs[:, i % 2, j - NE, :], full(f"{i} in {j}"), ACT.Copy)\
                                    .then_inc(act_done, pr.act.step(f"{i} in {j} out"))

                        def dt_in(i, e):
                            act.wait_ge(pe_done, pr.pe.at(f"{i} dt {e}"))
                            nc.scalar.activation(xc[:, e, 3:3 + S2], full(f"{i} dt {e}"), ACT.Identity,
                                                 bias=vec2("dtb", e)).then_inc(act_done, pr.act.step(f"{i} dt {e} in"))

                        def ut_out(i, tiles):
                            for t in tiles:
                                m = TT[t][1]
                                act.wait_ge(pe_done, pr.pe.at(f"{i} ut {t // 2}"))
                                nc.scalar.activation(ut[0:m, t, :], bank(4 + t % 2)[0:m, :],
                                                     ACT.Copy).then_inc(act_done, pr.act.step(f"{i} ut {t} out"))

                        def side(q, post, pre):
                            if pre is None:
                                return
                            if q == 0:
                                if pre >= 2:
                                    act.wait_ge(dve_done, pr.dve.at(f"{pre - 1} dt {NE - 1}"))
                                if pre == B:
                                    act.wait_ge(dve_done, pr.dve.at("0 h 1"))
                                for j in range(ND):
                                    nc.scalar.activation(sq[:, j, :], h[:, pre % B, j, :], ACT.Square)\
                                        .then_inc(act_done, pr.act.step(f"{pre} squares" if j else None))
                            if q == 4:
                                act.wait_ge(pe_done, pr.pe.at(f"{pre} var"))
                                nc.scalar.activation(rs, full(f"{pre} var"), ACT.Ln, bias=eps2[:, 0:1])\
                                    .then_inc(act_done, pr.act.step(f"{pre} log"))
                                act.wait_ge(act_done, pr.act.n)
                                nc.scalar.activation(rs, rs, ACT.Exp, scale=-0.5)\
                                    .then_inc(act_done, pr.act.step(f"{pre} rstd"))
                            if IN <= q < IN + 2 * NE and (q - IN) % 2:
                                if q == IN + 1 and pre == B:
                                    act.wait_ge(layer_loaded, 16 * len(next_loads))
                                in_out(pre, (q - IN) // 2)
                            if q == XD - 1:
                                for e in range(NE):
                                    act.wait_ge(dve_done, pr.dve.at(f"{pre} conv {e}"))
                                    nc.scalar.activation(xi[:, pre % 2, e, :], cv[:, e, :], ACT.Silu)\
                                        .then_inc(act_done, pr.act.step(f"{pre} xi {e}"))
                            if DTP <= q < DTP + NE:
                                dt_in(pre, q - DTP)
                            if DTP + NE <= q < DTP + 2 * NE:
                                e = q - DTP - NE
                                act.wait_ge(dve_done, pr.dve.at(f"{pre} clamp {e}"))
                                nc.scalar.activation(spe[:, e, :], spe[:, e, :], ACT.Exp)\
                                    .then_inc(act_done, pr.act.step(f"{pre} exp {e}"))
                            for e, at in enumerate((SP - 4, SP - 4, SP + 4, SP + 8)):
                                if q == at:
                                    act.wait_ge(act_done, pr.act.at(f"{pre} exp {e}"))
                                    if e >= 2:
                                        act.wait_ge(dve_done, pr.dve.at(f"{pre} max {e - 2}"))
                                    nc.scalar.activation(spl[:, e % 2, :], spe[:, e, :], ACT.Square,
                                                         scale=0.5 ** 0.5)\
                                        .then_inc(act_done, pr.act.step(f"{pre} half {e}"))
                            if q == SP - 1:
                                for e in range(NE):
                                    act.wait_ge(act_done, pr.act.at(f"{pre} exp {e}"))
                                    nc.scalar.activation(dt[:, pre % 2, e, :], spe[:, e, :], ACT.Ln, bias=1.0)\
                                        .then_inc(act_done, pr.act.step(f"{pre} log1p {e}"))
                            if Z <= q < Z + 4 * NE and (q - Z) % 4 == 1:
                                in_out(pre, NE + (q - Z) // 4)
                            if q == UT - 2:
                                act.wait_ge(act_done, pr.act.at(f"{pre} in {2 * NE - 1} out"))
                                nc.scalar.activation(zs[:, pre % 2, :, :], zs[:, pre % 2, :, :], ACT.Silu)\
                                    .then_inc(act_done, pr.act.step(f"{pre} zs"))
                            if q == UT and pre - 1 in mains:
                                act.wait_ge(pool_done, pr.pool.at(f"{pre - 1} ub {LAST}"))
                            for tiles, at in (((0, 1), UT), ((2, 3), UT + 2), ((4,), UT + 3)):
                                if q == at:
                                    ut_out(pre, tiles)

                        if steps:
                            act.wait_ge(x_loaded, 16 * len(first_loads))
                            nc.scalar.activation(am[:, :], vb[:, V2["A"] - V2A:V2["A"] - V2A + NE * DS], ACT.Exp)\
                                .then_inc(act_done, pr.act.step())
                            act.wait_ge(act_done, pr.act.n)
                            nc.scalar.activation(am[:, :], am[:, :], ACT.Copy, scale=-1.0)\
                                .then_inc(act_done, pr.act.step("am"))
                            act.wait_ge(act_done, pr.act.n)
                            for e in range(NE):
                                decay(*steps[0], e)
                        else:
                            act.wait_ge(x_loaded, 16 * len(first_loads))
                        for s, (i, n) in enumerate(steps):
                            for e in range(NE):
                                if s + 1 < len(steps):
                                    decay(*steps[s + 1], e)
                                if s and e == NE - 1:
                                    scaled(*steps[s - 1])
                                side(NE * n + e, *sides(i, n))
                        if steps:
                            scaled(*steps[-1])
                        for i, q in alone:
                            side(q, *sides(i, q))

                    @block.vector
                    def _(dve):
                        def finish(i, j):
                            dve.wait_ge(pe_done, pr.pe.at(f"{i} out {j}"))
                            nc.vector.tensor_tensor(h[:, i, j, :], h[:, i, j, :], full(f"{i} out {j}"), ALU.add)\
                                .then_inc(dve_done, pr.dve.step(f"{i} h {j}"))

                        def clamp(i, e):
                            dve.wait_ge(pe_done, pr.pe.at(f"{i} dt {e}"))
                            dve.wait_ge(act_done, pr.act.at(f"{i} dt {e} in"))
                            nc.vector.tensor_scalar(spe[:, e, :], xc[:, e, 3:3 + S2], SOFTPLUS_LINEAR, None, ALU.min)\
                                .then_inc(dve_done, pr.dve.step(f"{i} clamp {e}"))

                        def side(q, post, pre):
                            if post is not None:
                                if q == 3:
                                    for e in range(NE):
                                        dve.wait_ge(pe_done, pr.pe.at(f"{post} yf {e}"))
                                        nc.vector.scalar_tensor_tensor(cv[:, e, :], xi[:, post % 2, e, :],
                                                                       vec2("D", e), full(f"{post} yf {e}"),
                                                                       ALU.mult, ALU.add)\
                                            .then_inc(dve_done, pr.dve.step(f"{post} yd {e}"))
                                if q == 4:
                                    for e in range(2):
                                        dve.wait_ge(dve_done, pr.dve.at(f"{post} yd {e}"))
                                        nc.vector.tensor_tensor(cv[:, e, :], cv[:, e, :], zs[:, post % 2, e, :],
                                                                ALU.mult)\
                                            .then_inc(dve_done, pr.dve.step(f"{post} yg {e}"))
                                if q in (8, 12):
                                    finish(post, (q - 8) // 4)
                            if pre is not None:
                                if q in (9, 10):
                                    j = q - 9
                                    dve.wait_ge(act_done, pr.act.at(f"{pre} rstd"))
                                    if pre == B:
                                        dve.wait_ge(layer_loaded, 16 * len(next_loads))
                                    nc.vector.scalar_tensor_tensor(xn[:, j, :], h[:, pre % B, j, :],
                                                                   vec2("norm", j), rs, ALU.mult, ALU.mult)\
                                        .then_inc(dve_done, pr.dve.step(f"{pre} xn" if j else None))
                                if IN + 2 <= q < IN + 2 + 2 * NE:
                                    e = (q - IN - 2) // 2
                                    taps(pre, e, (3,) if q % 2 != IN % 2 else (1, 2))
                                if q == XD + NE:
                                    dve.wait_ge(pe_done, pr.pe.at(f"{pre} xd"))
                                    nc.vector.tensor_copy(xd, full(f"{pre} xd")[0:NX, :])\
                                        .then_inc(dve_done, pr.dve.step(f"{pre} xd"))
                                if DTP + 1 <= q < DTP + 1 + NE:
                                    clamp(pre, q - DTP - 1)
                                if q == DTP + NE + 1:
                                    dve.wait_ge(pe_done, pr.pe.at(f"{pre} bc"))
                                    whole = T // P
                                    nc.vector.tensor_copy(
                                        bc[:, pre % 2, 0:whole, :],
                                        full(f"{pre} bc")[:, 0:whole * NX].rearrange("p (i c) -> p i c", i=whole))\
                                        .then_inc(dve_done, pr.dve.step())
                                    nc.vector.tensor_copy(bc[0:KEYS, pre % 2, whole, :],
                                                          full(f"{pre} bc")[0:KEYS, whole * NX:(whole + 1) * NX])\
                                        .then_inc(dve_done, pr.dve.step(f"{pre} bc out"))
                                if SP <= q < SP + 4 * NE:
                                    softplus(pre, (q - SP) // 4, (q - SP) % 4)
                                if q == SP + 4 * NE:
                                    e = NE - 1
                                    dve.wait_ge(dve_done, pr.dve.at(f"{pre} dt {e}"))
                                    nc.vector.tensor_tensor(cv[:, e, :], dt[:, pre % 2, e, :], xi[:, pre % 2, e, :],
                                                            ALU.mult).then_inc(dve_done, pr.dve.step(f"{pre} u {e}"))

                        def taps(i, e, which):
                            dve.wait_ge(act_done, pr.act.at(f"{i} tap {e}"))
                            for t in which:
                                dve.wait_ge(dve_done, pr.dve.n)
                                nc.vector.scalar_tensor_tensor(cv[:, e, :], xc[:, e, t:t + S2],
                                                               vec2("cw", 4 * e + t), cv[:, e, :], ALU.mult, ALU.add)\
                                    .then_inc(dve_done, pr.dve.step(f"{i} conv {e}" if t == 3 else None))

                        def softplus(i, e, part):
                            d = dt[:, i % 2, e, :]
                            if part == 0:
                                dve.wait_ge(pool_done, pr.pool.at(f"{i} lower {e}"))
                                nc.vector.scalar_tensor_tensor(spu[:, e % 2, :], spu[:, e % 2, :], 2.0 / 3.0,
                                                               spl[:, e % 2, :], ALU.mult, ALU.add)\
                                    .then_inc(dve_done, pr.dve.step(f"{i} upper {e}"))
                            if part == 1:
                                dve.wait_ge(act_done, pr.act.at(f"{i} log1p {e}"))
                                nc.vector.tensor_tensor(d, d, spl[:, e % 2, :], ALU.max)\
                                    .then_inc(dve_done, pr.dve.step(f"{i} bounded {e}"))
                            if part == 2:
                                dve.wait_ge(dve_done, pr.dve.at(f"{i} bounded {e}"))
                                nc.vector.tensor_tensor(d, d, spu[:, e % 2, :], ALU.min)\
                                    .then_inc(dve_done, pr.dve.step(f"{i} max {e}"))
                            if part == 3:
                                dve.wait_ge(dve_done, pr.dve.at(f"{i} max {e}"))
                                nc.vector.tensor_tensor(d, d, xc[:, e, 3:3 + S2], ALU.max)\
                                    .then_inc(dve_done, pr.dve.step(f"{i} dt {e}"))

                        def scan(i, n, e):
                            u = NE * (DS * i + n) + e
                            dve.wait_ge(act_done, pr.act.at(f"{i} da {n} {e}"))
                            dve.wait_ge(pe_done, pr.pe.at(f"{i} db {n} {e}"))
                            if e == 0 and DS * i + n >= 2:
                                j, m = divmod(DS * i + n - 2, DS)
                                dve.wait_ge(pe_done, pr.pe.at(f"{j} ht {m} {SHARED}"))
                            nc.vector.tensor_tensor_scan(hh[:, n % 2, e, :], da[:, u % AHEAD, :],
                                                         full(f"{i} db {n} {e}"), 0.0, ALU.mult, ALU.add)\
                                .then_inc(dve_done, pr.dve.step(f"{i} scan {n} {e}"))

                        def add(i, n, t):
                            t0, m = TT[t]
                            if n == 0 and i and t == ORDER[0]:
                                dve.wait_ge(pe_done, pr.pe.at(f"{i - 1} yf {NE - 1}"))
                            dve.wait_ge(pe_done, pr.pe.at(f"{i} ht {n} {t}"))
                            s = bank(pr.bank_of(f"{i} ht {n} {t}"))[0:m, :]
                            c = bc[0:m, i % 2, t, DR + DS + n:DR + DS + n + 1]
                            if n == 0:
                                nc.vector.tensor_scalar(yt[0:m, t, :], s, c, None, ALU.mult)\
                                    .then_inc(dve_done, pr.dve.step(f"{i} y {n} {t}"))
                            else:
                                if t == SHARED:
                                    dve.wait_ge(pool_done, pr.pool.at(f"{i} y {n - 1} {t}"))
                                else:
                                    dve.wait_ge(dve_done, pr.dve.at(f"{i} y {n - 1} {t}"))
                                nc.vector.scalar_tensor_tensor(yt[0:m, t, :], s, c, yt[0:m, t, :], ALU.mult, ALU.add)\
                                    .then_inc(dve_done, pr.dve.step(f"{i} y {n} {t}"))

                        before = None
                        for i, n in steps:
                            for e in range(NE):
                                scan(i, n, e)
                                if before:
                                    add(*before, ORDER[e])
                                if before and before[1] == LAST and e == NE - 1:
                                    add(*before, SHARED)
                                side(NE * n + e, *sides(i, n))
                            before = (i, n)
                        if before:
                            for t in ORDER:
                                add(*before, t)
                        else:
                            dve.wait_ge(x_loaded, 16 * len(first_loads))
                        for i, q in alone:
                            side(q, *sides(i, q))

                    @block.gpsimd
                    def _(pool):
                        def state_inputs(i, n):
                            if DS * i + n >= 2:
                                j, m = divmod(DS * i + n - 2, DS)
                                pool.wait_ge(pe_done, pr.pe.at(f"{j} db {m} {NE - 1}"))
                            for t, (t0, m) in enumerate(TT):
                                if i and n == 0:
                                    pool.wait_ge(act_done, pr.act.at(f"{i} ut {t} out"))
                                nc.gpsimd.tensor_scalar(ub[0:m, n % 2, t, :], ut[0:m, t, :],
                                                        bc[0:m, i % 2, t, DR + n:DR + n + 1], 1.0, ALU.mult, ALU.mult)\
                                    .then_inc(pool_done,
                                              pr.pool.step(f"{i} ub {n}" if t == len(TT) - 1 else None))

                        def add(i, n):
                            if n in (0, LAST):
                                return
                            pool.wait_ge(act_done, pr.act.at(f"{i} ys {n}"))
                            if n >= 2:
                                pool.wait_ge(pool_done, pr.pool.at(f"{i} y {n - 1} {SHARED}"))
                            nc.gpsimd.tensor_tensor(yt[:, SHARED, :], yt[:, SHARED, :], ys[:, n % 2, :], ALU.add)\
                                .then_inc(pool_done, pr.pool.step(f"{i} y {n} {SHARED}"))

                        def side(k, post, pre):
                            if post is not None and k == 0:
                                for e in range(2, NE):
                                    pool.wait_ge(dve_done, pr.dve.at(f"{post} yd {e}"))
                                    nc.gpsimd.tensor_tensor(cv[:, e, :], cv[:, e, :], zs[:, post % 2, e, :], ALU.mult)\
                                        .then_inc(pool_done, pr.pool.step(f"{post} yg {e}"))
                            if pre is not None:
                                if SP // 4 - 1 <= k < SP // 4 - 1 + NE:
                                    lower(pre, k - SP // 4 + 1)
                                if SP // 4 + 1 <= k < SP // 4 + NE:
                                    e = k - SP // 4 - 1
                                    pool.wait_ge(dve_done, pr.dve.at(f"{pre} dt {e}"))
                                    nc.gpsimd.tensor_tensor(cv[:, e, :], dt[:, pre % 2, e, :], xi[:, pre % 2, e, :],
                                                            ALU.mult).then_inc(pool_done, pr.pool.step(f"{pre} u {e}"))

                        def lower(i, e):
                            pool.wait_ge(act_done, pr.act.at(f"{i} half {e}"))
                            if e == 0:
                                pool.wait_ge(pe_done, pr.pe.at(f"{i} bc"))
                            nc.gpsimd.tensor_tensor(spu[:, e % 2, :], spe[:, e, :], spl[:, e % 2, :],
                                                    ALU.mult).then_inc(pool_done, pr.pool.step())
                            pool.wait_ge(pool_done, pr.pool.n)
                            nc.gpsimd.tensor_tensor(spl[:, e % 2, :], spe[:, e, :], spl[:, e % 2, :],
                                                    ALU.subtract).then_inc(pool_done, pr.pool.step(f"{i} lower {e}"))

                        if steps:
                            state_inputs(*steps[0])
                        for s, (i, n) in enumerate(steps):
                            if s + 1 < len(steps):
                                state_inputs(*steps[s + 1])
                            side(n, *sides(i, n))
                            if s:
                                add(*steps[s - 1])
                        if steps:
                            add(*steps[-1])
                        for i, q in alone:
                            if q % NE == NE - 1:
                                side(q // NE, *sides(i, q))
                found[name] = pr.result()
                end_of_block()

            def first_weights(layer):
                return [(wa[:, :], w2_in[layer][:, 0:W2A]), (va[:, :], v2_in[layer][:, 0:V2A])]

            def loop_weights(layer):
                return [(wb[:, :], w2_in[layer][:, W2A:W2N]), (vb[:, :], v2_in[layer][:, V2A:V2N])]

            with nc.Block() as block:
                @block.gpsimd
                def _(pool):
                    nc.gpsimd.memset(eps2[:, :], EPS).then_inc(pool_done, 1)
                    nc.gpsimd.memset(xc[:, :, 0:3], 0.0).then_inc(pool_done, 1)
                    pool.wait_ge(pool_done, 2)
            end_of_block()

            mamba("m first", [], 0, first_weights(0)
                  + [(h[:, i, :, :], hs[i].rearrange("p (k t) -> p k t", k=ND)) for i in range(B)], [], False)
            w2_next, v2_next = w2_in[1:L], v2_in[1:L]
            with nc.Fori(0, L - 1) as layer:
                mamba("m", list(range(B)), B, loop_weights(layer),
                      [(wa[:, :], w2_next[layer][:, 0:W2A]), (va[:, :], v2_next[layer][:, 0:V2A])], False)
            mamba("m last", list(range(B)), B - 1, loop_weights(L - 1), [], True)

        with ExitStack() as mem:
            def sb(name, shape):
                return mem.enter_context(nc.sbuf_tensor(f"c_{name}", shape, F32))

            w3, v3 = sb("w3", [P, W3N]), sb("v3", [P, V3N])
            x = sb("x", [P, ND, T])
            cx = sb("ctx", [P, 2, P])
            ksb = sb("ksb", [P, 2, KEYS])
            hid = sb("hid", [P, 8, T])
            q3 = sb("q3", [P, ND, T])
            k3 = sb("k3", [P, 2, ND, T])
            v3s = sb("v3s", [P, NT, 2, 8 * 144])
            o3 = sb("o3", [P, ND, T])
            kbd3 = sb("kbd3", [P, 2, T])
            vbd3 = sb("vbd3", [P, 2, 4, P])
            st = Dense("c", sb)
            st.pt = sb("pt", [P, 2, 4, T])
            pr = st.prog

            def mat3(name, k=2, n=D):
                return w3[:, W3[name]:W3[name] + k * n].rearrange("p (k n) -> p k n", k=k)

            def vec3(name, n=2):
                return v3[:, V3[name]:V3[name] + n]

            with nc.Block() as block:
                @block.sync
                def _(sp):
                    sp.dma_start(v3[:, :], v3_in).then_inc(w3_loaded, 16)
                    sp.dma_start(w3[:, :], w3_in).then_inc(w3_loaded, 16)

                @block.gpsimd
                def _(pool):
                    nc.gpsimd.memset(st.eps[:, :], EPS).then_inc(pool_done, 1)
                    nc.gpsimd.memset(v3s[:, :, :, :], 0.0).then_inc(pool_done, 1)
                    pool.wait_ge(pool_done, 2)
            end_of_block()

            with nc.Fori(0, B) as b:
                with nc.Block() as block:
                    @block.sync
                    def _(sp):
                        sp.dma_start(x[:, :, :], hs[b].rearrange("p (k t) -> p k t", k=ND)[:, :, KEYS:S2])\
                            .then_inc(x_loaded, 16)
                        sp.dma_start(cx[:, :, :], ctx_in[b].rearrange("p (k t) -> p k t", k=2)).then_inc(x_loaded, 16)
                        sp.wait_ge(dve_done, pr.dve.at("l3 down 1 out"))
                        sp.dma_start(out[b].rearrange("p (k t) -> p k t", k=ND), x[:, :, :]).then_inc(x_stored, 16)
                        sp.wait_ge(x_stored, 16)

                    @block.tensor
                    def _(pe):
                        pe.wait_ge(w3_loaded, 32)
                        pe.wait_ge(x_loaded, 32)
                        st.pe_norm(pe, "nf", None, None, rms=True)
                        bk, emptied = st.lin.take("k4", pr.act, "k4 out")
                        if emptied:
                            pe.wait_ge(*emptied)
                        w = mat3("ck")
                        for j in range(2):
                            for k in range(2):
                                mm = nc.tensor.matmul(bk[:, j * KEYS:(j + 1) * KEYS], w[:, k, j * P:(j + 1) * P],
                                                      cx[:, k, 0:KEYS], start=k == 0, stop=k == 1)
                        mm.then_inc(pe_done, pr.pe.step("k4"))
                        st.pe_norm(pe, "n4", x, (dve_done, pr.dve.at("final norm")))
                        bk, emptied = st.lin.take("v4", pr.dve, "v4 out")
                        if emptied:
                            pe.wait_ge(*emptied)
                        w = mat3("cv")
                        for k in range(2):
                            mm = nc.tensor.matmul(bk[:, 0:D], cx[:, k, :], w[:, k, :], start=k == 0, stop=k == 1)
                        mm.then_inc(pe_done, pr.pe.step("v4"))
                        pe.wait_ge(dve_done, pr.dve.at("n4 out"))
                        st.pe_linear(pe, "q3", mat3("sq"), st.ln, 2, range(2), pr.dve)
                        st.pe_linear(pe, "k3", mat3("sk"), st.ln, 2, range(2), pr.dve)
                        w = mat3("sv")
                        for t in range(NT):
                            bk, emptied = st.lin.take(f"v3 {t}", pr.act, f"v3 {t} out")
                            if emptied:
                                pe.wait_ge(*emptied)
                            for k in range(ND):
                                mm = nc.tensor.matmul(bk[:, 0:D], st.ln[:, k, t * P:(t + 1) * P], w[:, k, :],
                                                      start=k == 0, stop=k == ND - 1)
                            mm.then_inc(pe_done, pr.pe.step(f"v3 {t}"))
                        pe.wait_ge(dve_done, pr.dve.at("k3 1 out"))
                        pe.wait_ge(act_done, pr.act.at(f"v3 {NT - 1} out"))

                        def keys_of(h):
                            rows = slice(32 * (h % 8 // 2), 32 * (h % 8 // 2) + 32)
                            return rows, h // 8, k3[rows, h % 2, h // 8, :]

                        def values_of(h, kt):
                            return (v3s[:, kt, h // 8, P * (h % 8):P * (h % 8) + P], slice(0, P),
                                    h % 8 == 0 and kt == 0, h % 8 == 7 and kt == NT - 1)
                        st.pe_self(pe, "s3", q3, keys_of, values_of, 8)
                        pe.wait_ge(dve_done, pr.dve.at("s3 o 1 out"))
                        st.pe_linear(pe, "o3", mat3("so"), o3, 2, range(2), pr.dve)
                        st.pe_norm(pe, "n5", x, (dve_done, pr.dve.at("o3 1 out")))
                        pe.wait_ge(dve_done, pr.dve.at("n5 out"))
                        st.pe_linear(pe, "q4", mat3("cq"), st.ln, 2, range(2), pr.dve)
                        pe.wait_ge(dve_done, pr.dve.at("q4 1 out"))
                        st.pe_cross(pe, "x3", q3, kbd3, vbd3, False)
                        pe.wait_ge(dve_done, pr.dve.at("x3 o 1 out"))
                        st.pe_linear(pe, "o4", mat3("co"), o3, 2, range(2), pr.dve)
                        st.pe_norm(pe, "n6", x, (dve_done, pr.dve.at("o4 1 out")))
                        st.pe_mlp(pe, "l3", (dve_done, pr.dve.at("n6 out")), mat3("w1", 2, FF), mat3("w2", 8, D), hid)

                    @block.scalar
                    def _(act):
                        act.wait_ge(w3_loaded, 32)
                        act.wait_ge(x_loaded, 32)
                        st.act_norm(act, "nf", x)
                        act.wait_ge(pe_done, pr.pe.at("k4"))
                        for j in range(2):
                            nc.scalar.activation(ksb[:, j, :], st.full("k4")[:, j * KEYS:(j + 1) * KEYS], ACT.Identity,
                                                 bias=vec3("ck")[:, j:j + 1])\
                                .then_inc(act_done, pr.act.step("k4 out" if j else None))
                        st.act_norm(act, "n4")
                        for t in range(NT):
                            act.wait_ge(pe_done, pr.pe.at(f"v3 {t}"))
                            for g in range(2):
                                nc.scalar.activation(
                                    v3s[:, t, g, :].rearrange("p (j c) -> p j c", c=144)[:, :, 0:16],
                                    st.full(f"v3 {t}")[:, g * P:(g + 1) * P].rearrange("p (j d) -> p j d", d=16),
                                    ACT.Copy).then_inc(act_done, pr.act.step(f"v3 {t} out" if g else None))
                        st.act_self(act, "s3")
                        st.act_norm(act, "n5")
                        st.act_cross(act, "x3")
                        st.act_norm(act, "n6")
                        st.act_mlp(act, "l3", vec3("b1", 8), hid)

                    @block.vector
                    def _(dve):
                        dve.wait_ge(act_done, pr.act.at("nf rstd"))
                        for k in range(ND):
                            nc.vector.scalar_tensor_tensor(x[:, k, :], x[:, k, :], vec3("fin")[:, k:k + 1],
                                                           st.rs[:, :], ALU.mult, ALU.mult)\
                                .then_inc(dve_done, pr.dve.step("final norm" if k else None))
                        st.dve_norm(dve, "n4", x, vec3("g1"), vec3("n1"))
                        dve.wait_ge(pe_done, pr.pe.at("v4"))
                        for g in range(2):
                            for hp in range(4):
                                nc.vector.tensor_tensor(
                                    vbd3[:, g, hp, :].rearrange("p (h d) -> p h d", h=8),
                                    st.full("v4")[:, g * P:(g + 1) * P].rearrange("p (h d) -> p h d", h=8),
                                    cst[:, C_MV + 8 * hp:C_MV + 8 * hp + 8].unsqueeze(2).to_broadcast([P, 8, 16]),
                                    ALU.mult).then_inc(dve_done, pr.dve.step("v4 out" if (g, hp) == (1, 3) else None))
                        for j in range(2):
                            dve.wait_ge(pe_done, pr.pe.at(f"q3 {j}"))
                            nc.vector.tensor_scalar(q3[:, j, :], st.full(f"q3 {j}"), vec3("sq")[:, j:j + 1], 0.25,
                                                    ALU.add, ALU.mult).then_inc(dve_done, pr.dve.step(f"q3 {j} out"))
                        for j in range(2):
                            dve.wait_ge(pe_done, pr.pe.at(f"k3 {j}"))
                            for odd in range(2):
                                nc.vector.tensor_scalar(k3[:, odd, j, :], st.full(f"k3 {j}"), vec3("sk")[:, j:j + 1],
                                                        cst[:, C_PAR + odd:C_PAR + odd + 1], ALU.add, ALU.mult)\
                                    .then_inc(dve_done, pr.dve.step(f"k3 {j} out" if odd else None))
                        dve.wait_ge(act_done, pr.act.at("k4 out"))
                        for g in range(2):
                            nc.vector.tensor_tensor(
                                kbd3[:, g, :].rearrange("p (h k) -> p h k", h=8),
                                ksb[:, g, :].unsqueeze(1).to_broadcast([P, 8, KEYS]),
                                cst[:, C_MK:C_MK + 8].unsqueeze(2).to_broadcast([P, 8, KEYS]),
                                ALU.mult).then_inc(dve_done, pr.dve.step())
                        st.dve_self(dve, "s3", 8, o3, vec3("sv"))
                        st.dve_residual(dve, "o3", x, vec3("so"))
                        st.dve_norm(dve, "n5", x, vec3("g2"), vec3("n2"))
                        for j in range(2):
                            dve.wait_ge(pe_done, pr.pe.at(f"q4 {j}"))
                            nc.vector.tensor_scalar(q3[:, j, :], st.full(f"q4 {j}"), vec3("cq")[:, j:j + 1], 0.25,
                                                    ALU.add, ALU.mult).then_inc(dve_done, pr.dve.step(f"q4 {j} out"))
                        st.dve_cross(dve, "x3")
                        for g in range(2):
                            dve.wait_ge(pe_done, pr.pe.at(f"x3 o {g}"))
                            nc.vector.tensor_scalar(o3[:, g, :], st.full(f"x3 o {g}"), vec3("cv")[:, g:g + 1], None,
                                                    ALU.add).then_inc(dve_done, pr.dve.step(f"x3 o {g} out"))
                        st.dve_residual(dve, "o4", x, vec3("co"))
                        st.dve_norm(dve, "n6", x, vec3("g3"), vec3("n3"))
                        st.dve_residual(dve, "l3 down", x, vec3("b2"))

                    @block.gpsimd
                    def _(pool):
                        st.pool_self(pool, "s3")
                        st.pool_cross(pool, "x3")
                found["c"] = pr.result()
                end_of_block()
        return found


def _rows(a, k):
    K, N = a.shape
    if K < k * P:
        a = np.concatenate([a, np.zeros((k * P - K, N), a.dtype)])
    return np.ascontiguousarray(a.reshape(k, P, N).transpose(1, 0, 2).reshape(P, k * N))


def _cols(v):
    return np.ascontiguousarray(v.reshape(-1, P).T)


def _arrays(i):
    g = {k: np.asarray(v) for k, v in i.items()}
    l0 = lambda n: g["L0_xattn_" + n]
    l1 = lambda n: g["L1_xattn_" + n]
    l2 = lambda n: g["L2_xattn_" + n]
    l3 = lambda n: g["L3_xattn_" + n]
    cat = lambda parts: np.ascontiguousarray(np.concatenate(parts, 1))
    p = np.arange(P)[:, None]
    cst = np.concatenate([
        np.eye(P), np.full((P, P), 1.0 / D), p // 16 == np.arange(8)[None],
        (np.arange(8)[None, None] == 2 * np.arange(4)[None, :, None] + (p // 64)[:, :, None]).reshape(P, 32),
        p // 64 == np.arange(2)[None], (p // 16) % 2 == np.arange(2)[None]], 1).astype(np.float32)
    ctx_t = g["ctx_768"].transpose(0, 2, 1)
    ctx = np.stack([_rows(np.concatenate([c, c], 1), 2) for c in ctx_t])
    per_layer = range(L)
    return {
        "x_in": np.stack([_rows(a.T, 2) for a in g["x"]]),
        "ctx_in": ctx,
        "cst_in": cst,
        "w0_in": cat([_rows(l0("Wq"), 2), _rows(l0("Wk"), 2), _rows(l0("Wv"), 2), _rows(l2("pre_w1"), 2),
                      _rows(l2("pre_w2"), 2), _rows(l0("Wo"), 2), _rows(l0("W1"), 2), _rows(l0("W2"), 8)]),
        "w1a_in": cat([_rows(l1("Wq1"), 2), _rows(l1("Wk1"), 2), _rows(l1("Wv1"), 2), _rows(l1("Wo1"), 8)]),
        "w1b_in": cat([_rows(l1("Wq2"), 2), _rows(l1("Wk2"), 2), _rows(l1("Wv2"), 2), _rows(l1("Wo2"), 8),
                       _rows(l1("Wp"), 2), _rows(l1("Wf"), 8)]),
        "v0_in": cat([_cols(l0(n)) for n in ("bq", "bk", "bv", "bo", "ln_g", "ln_b", "b1", "b2")]
                     + [_cols(l1(n)) for n in ("g1", "b1", "bo1", "g2", "b2", "bo2", "g3", "b3", "bp", "bf")]),
        "w2_in": np.stack([cat([_rows(l2("in_proj_w")[n].T, 2), _rows(l2("x_proj_w")[n].T, NE),
                                _rows(l2("dt_proj_w")[n].T, 1), _rows(l2("out_proj_w")[n].T, NE)])
                           for n in per_layer]),
        "v2_in": np.stack([cat([_cols(l2("norm_w")[n]), _rows(l2("conv_w")[n], NE), _cols(l2("conv_b")[n]),
                                _cols(l2("dt_proj_b")[n]), _cols(l2("D_param")[n]), _rows(l2("A_log")[n], NE)])
                           for n in per_layer]),
        "w3_in": cat([_rows(l3(n).T, 2) for n in ("sa_wq", "sa_wk", "sa_wv", "sa_wo", "ca_wq", "ca_wk", "ca_wv",
                                                  "ca_wo", "mlp_w1")] + [_rows(l3("mlp_w2").T, 8)]),
        "v3_in": cat([_cols(l2("final_norm_w"))] + [_cols(l3(n)) for n in (
            "ln1_g", "ln1_b", "ln2_g", "ln2_b", "ln3_g", "ln3_b", "sa_bq", "sa_bk", "sa_bv", "sa_bo",
            "ca_bq", "ca_bk", "ca_bv", "ca_bo", "mlp_b1", "mlp_b2")]),
    }


def kernel(**inputs):
    import concourse.bacc as _bacc
    from concourse.bass_utils import run_bass_kernel_spmd as _run

    arrays = _arrays(inputs)
    known = {}
    for _ in range(2):
        nc = _bacc.Bacc("TRN2", target_bir_lowering=False, num_devices=1)
        args = {n: nc.dram_tensor(n, a.shape, F32, kind="ExternalInput").ap() for n, a in arrays.items()}
        out = nc.dram_tensor("y_out", (B, P, ND * T), F32, kind="ExternalOutput").ap()
        known = build(nc, known, out=out, **args)
    r = _run(nc, [arrays], core_ids=[0])
    y = r.results[0]["y_out"].reshape(B, P, ND, T)
    return np.ascontiguousarray(y.transpose(0, 3, 2, 1).reshape(B, T, D))
```
